# Optimizing a Trainium2 kernel written in Bass

```python
import numpy as np
import jax
import jax.numpy as jnp

def _softmax(x, axis=-1):
    return jax.nn.softmax(x, axis=axis)

def _gelu(x):
    return jax.nn.gelu(x, approximate=True)

def _silu(x):
    return jax.nn.silu(x)

def _sigmoid(x):
    return jax.nn.sigmoid(x)

def _layernorm(x, axis=-1, eps=1e-05):
    m = jnp.mean(x, axis=axis, keepdims=True)
    v = jnp.var(x, axis=axis, keepdims=True)
    return (x - m) / jnp.sqrt(v + eps)

def _scatter_add(tgt, idx, src, axis=0):
    return tgt.at[idx].add(src)

def _segment_sum(src, seg, n):
    return jax.ops.segment_sum(src, seg, n)
kernel_name = 'mk_seq_postln_d1_jaxref_r8_6d6a56'

def setup_inputs(seed: int=0):
    np.random.seed(seed)
    _w = jnp.asarray

    def _L0_attn_setup():
        import jax, jax.numpy as jnp
        import numpy as np
        H, DK, DV, M = (8, 64, 64, 8)

        def _l2norm(x, eps=1e-06):
            return x * jax.lax.rsqrt(jnp.sum(x * x, axis=-1, keepdims=True) + eps)

        def _rotary(x, cos, sin):
            d = x.shape[-1] // 2
            x1, x2 = (x[..., :d], x[..., d:])
            c = cos[:, None]
            s = sin[:, None]
            return jnp.concatenate([x1 * c + x2 * s, -x1 * s + x2 * c], axis=-1)
        key = jax.random.key(seed)
        ks = jax.random.split(key, 11)
        B, T, D = (2, 256, 128)
        w = lambda k, shape, s=0.02: jax.random.normal(k, shape, jnp.float32) * s
        return {'hidden_states': jax.random.normal(ks[0], (B, T, D), jnp.float32), 'Wq': w(ks[1], (D, H * DK)), 'Wk': w(ks[2], (D, H * DK)), 'Wv': w(ks[3], (D, H * DV)), 'Wbeta': w(ks[4], (D, H * M)), 'Wtg': w(ks[5], (D, H * M)), 'mode_logits': w(ks[6], (H, M), 0.1), 'log_decay': w(ks[7], (H, M), 0.1), 'omega_log_scale': w(ks[8], (H, M), 0.1), 'Wg': w(ks[9], (D, H * DV)), 'Wo': w(ks[10], (H * DV, D))}
    _L0_attn_in = _L0_attn_setup()

    def _L0_ffn_setup():
        import jax, jax.numpy as jnp
        import numpy as np
        import math
        D_MODEL = 128
        D_FF = 512
        NUM_EXPERTS = 8
        NUM_SHARED = 1
        E_ROUTED = NUM_EXPERTS - NUM_SHARED
        TOP_K = 2
        CAP_FACTOR = 1.25
        B, S = (4, 256)
        T = B * S
        CAPACITY = math.ceil(CAP_FACTOR * T * TOP_K / E_ROUTED)
        SHARED_SCALE = 1.0

        def _layernorm(x, g, b, eps=1e-05):
            mu = jnp.mean(x, axis=-1, keepdims=True)
            var = jnp.mean((x - mu) ** 2, axis=-1, keepdims=True)
            return (x - mu) * jax.lax.rsqrt(var + eps) * g + b
        key = jax.random.key(seed)
        ks = jax.random.split(key, 10)
        s = 0.02
        return {'x': jax.random.normal(ks[0], (B, S, D_MODEL), dtype=jnp.float32), 'ln_g': jnp.ones((D_MODEL,), jnp.float32), 'ln_b': jnp.zeros((D_MODEL,), jnp.float32), 'Wr': jax.random.normal(ks[1], (D_MODEL, E_ROUTED), jnp.float32) * s, 'W1': jax.random.normal(ks[2], (E_ROUTED, D_MODEL, D_FF), jnp.float32) * s, 'W3': jax.random.normal(ks[3], (E_ROUTED, D_MODEL, D_FF), jnp.float32) * s, 'W2': jax.random.normal(ks[4], (E_ROUTED, D_FF, D_MODEL), jnp.float32) * s, 'W1s': jax.random.normal(ks[5], (D_MODEL, D_FF), jnp.float32) * s, 'W3s': jax.random.normal(ks[6], (D_MODEL, D_FF), jnp.float32) * s, 'W2s': jax.random.normal(ks[7], (D_FF, D_MODEL), jnp.float32) * s}
    _L0_ffn_in = _L0_ffn_setup()
    _d = {'L0_attn_hidden_states': _L0_attn_in['hidden_states'], 'L0_attn_Wq': _L0_attn_in['Wq'], 'L0_attn_Wk': _L0_attn_in['Wk'], 'L0_attn_Wv': _L0_attn_in['Wv'], 'L0_attn_Wbeta': _L0_attn_in['Wbeta'], 'L0_attn_Wtg': _L0_attn_in['Wtg'], 'L0_attn_mode_logits': _L0_attn_in['mode_logits'], 'L0_attn_log_decay': _L0_attn_in['log_decay'], 'L0_attn_omega_log_scale': _L0_attn_in['omega_log_scale'], 'L0_attn_Wg': _L0_attn_in['Wg'], 'L0_attn_Wo': _L0_attn_in['Wo'], 'L0_ffn_ln_g': _L0_ffn_in['ln_g'], 'L0_ffn_ln_b': _L0_ffn_in['ln_b'], 'L0_ffn_Wr': _L0_ffn_in['Wr'], 'L0_ffn_W1': _L0_ffn_in['W1'], 'L0_ffn_W3': _L0_ffn_in['W3'], 'L0_ffn_W2': _L0_ffn_in['W2'], 'L0_ffn_W1s': _L0_ffn_in['W1s'], 'L0_ffn_W3s': _L0_ffn_in['W3s'], 'L0_ffn_W2s': _L0_ffn_in['W2s']}
    _x0 = _d['L0_attn_hidden_states']
    _d['L0_attn_hidden_states'] = jax.random.normal(jax.random.fold_in(jax.random.key(seed), 1), (16, 512, 128), dtype=_x0.dtype)
    del _x0
    return _d

def reference(L0_attn_hidden_states, L0_attn_Wq, L0_attn_Wk, L0_attn_Wv, L0_attn_Wbeta, L0_attn_Wtg, L0_attn_mode_logits, L0_attn_log_decay, L0_attn_omega_log_scale, L0_attn_Wg, L0_attn_Wo, L0_ffn_ln_g, L0_ffn_ln_b, L0_ffn_Wr, L0_ffn_W1, L0_ffn_W3, L0_ffn_W2, L0_ffn_W1s, L0_ffn_W3s, L0_ffn_W2s):

    def _L0_attn_ref(hidden_states, Wq, Wk, Wv, Wbeta, Wtg, mode_logits, log_decay, omega_log_scale, Wg, Wo):
        import jax, jax.numpy as jnp
        import numpy as np
        H, DK, DV, M = (8, 64, 64, 8)

        def _l2norm(x, eps=1e-06):
            return x * jax.lax.rsqrt(jnp.sum(x * x, axis=-1, keepdims=True) + eps)

        def _rotary(x, cos, sin):
            d = x.shape[-1] // 2
            x1, x2 = (x[..., :d], x[..., d:])
            c = cos[:, None]
            s = sin[:, None]
            return jnp.concatenate([x1 * c + x2 * s, -x1 * s + x2 * c], axis=-1)
        x = hidden_states
        B, T, D = x.shape
        q = (x @ Wq).reshape(B, T, H, DK)
        k = (x @ Wk).reshape(B, T, H, DK)
        v = (x @ Wv).reshape(B, T, H, DV)
        beta = jax.nn.sigmoid((x @ Wbeta).reshape(B, T, H, M))
        tg = jax.nn.sigmoid((x @ Wtg).reshape(B, T, H, M))
        pair = jnp.arange(0, DK, 2, dtype=jnp.float32)
        inv_freq = 1.0 / 10000.0 ** (pair / DK)
        omega_scale = jnp.exp(omega_log_scale)
        pos = jnp.arange(T, dtype=jnp.float32)
        angles = pos[:, None, None, None] * omega_scale[None, :, :, None] * inv_freq
        cos = jnp.transpose(jnp.cos(angles), (2, 0, 1, 3))
        sin = jnp.transpose(jnp.sin(angles), (2, 0, 1, 3))
        scale = DK ** (-0.5)
        qr = _l2norm(_rotary(q, cos, sin)) * scale
        kr = _l2norm(_rotary(k, cos, sin))
        rho = jnp.exp(-jax.nn.softplus(log_decay))
        g = jnp.log(jnp.clip(tg * rho, 1e-06))
        qt = jnp.transpose(qr, (2, 0, 1, 3, 4))
        kt = jnp.transpose(kr, (2, 0, 1, 3, 4))
        vt = jnp.transpose(v, (1, 0, 2, 3))
        gt = jnp.transpose(g, (1, 3, 0, 2))
        bt = jnp.transpose(beta, (1, 3, 0, 2))

        def step(S, inp):
            q_t, k_t, v_t, b_g, b_beta = inp
            S = S * jnp.exp(b_g)[..., None, None]
            kv = jnp.einsum('mbhk,mbhkv->mbhv', k_t, S)
            dv = (v_t[None] - kv) * b_beta[..., None]
            S = S + k_t[..., :, None] * dv[..., None, :]
            o_t = jnp.einsum('mbhk,mbhkv->mbhv', q_t, S)
            return (S, o_t)
        S0 = jnp.zeros((M, B, H, DK, DV), jnp.float32)
        _, ys = jax.lax.scan(step, S0, (qt, kt, vt, gt, bt))
        mode_w = jax.nn.softmax(mode_logits, axis=-1)
        o = jnp.einsum('tmbhv,hm->bthv', ys, mode_w)
        gate = jax.nn.sigmoid((x @ Wg).reshape(B, T, H, DV))
        o = o * gate
        return o.reshape(B, T, H * DV) @ Wo

    def _L0_ffn_ref(x, ln_g, ln_b, Wr, W1, W3, W2, W1s, W3s, W2s):
        import jax, jax.numpy as jnp
        import numpy as np
        import math
        D_MODEL = 128
        D_FF = 512
        NUM_EXPERTS = 8
        NUM_SHARED = 1
        E_ROUTED = NUM_EXPERTS - NUM_SHARED
        TOP_K = 2
        CAP_FACTOR = 1.25
        B, S = (4, 256)
        T = B * S
        CAPACITY = math.ceil(CAP_FACTOR * T * TOP_K / E_ROUTED)
        SHARED_SCALE = 1.0

        def _layernorm(x, g, b, eps=1e-05):
            mu = jnp.mean(x, axis=-1, keepdims=True)
            var = jnp.mean((x - mu) ** 2, axis=-1, keepdims=True)
            return (x - mu) * jax.lax.rsqrt(var + eps) * g + b
        Bx, Sx, D = x.shape
        Tn = Bx * Sx
        h = _layernorm(x, ln_g, ln_b).reshape(Tn, D)
        logits = h @ Wr
        top_vals, top_idx = jax.lax.top_k(logits, TOP_K)
        gates = jax.nn.softmax(top_vals, axis=-1)
        idx = top_idx.T.reshape(-1)
        gat = gates.T.reshape(-1)
        tok = jnp.tile(jnp.arange(Tn), TOP_K)
        onehot = jax.nn.one_hot(idx, E_ROUTED, dtype=jnp.int32)
        pos = jnp.sum(jnp.cumsum(onehot, axis=0) * onehot, axis=-1) - 1
        keep = pos < CAPACITY
        pos_c = jnp.where(keep, pos, CAPACITY)
        xe = jnp.zeros((E_ROUTED, CAPACITY, D), h.dtype).at[idx, pos_c].set(h[tok], mode='drop')
        a = jnp.einsum('ecd,edf->ecf', xe, W1)
        b = jnp.einsum('ecd,edf->ecf', xe, W3)
        ye = jnp.einsum('ecf,efd->ecd', jax.nn.silu(a) * b, W2)
        out_slots = ye[jnp.clip(idx, 0, E_ROUTED - 1), jnp.clip(pos_c, 0, CAPACITY - 1)]
        out_slots = out_slots * (gat * keep.astype(gat.dtype))[:, None]
        routed = jnp.zeros((Tn, D), h.dtype).at[tok].add(out_slots)
        shared = jax.nn.silu(h @ W1s) * (h @ W3s) @ W2s
        out = routed + SHARED_SCALE * shared
        return out.reshape(Bx, Sx, D)
    x = L0_attn_hidden_states
    x = _layernorm(x + _L0_attn_ref(x, L0_attn_Wq, L0_attn_Wk, L0_attn_Wv, L0_attn_Wbeta, L0_attn_Wtg, L0_attn_mode_logits, L0_attn_log_decay, L0_attn_omega_log_scale, L0_attn_Wg, L0_attn_Wo), axis=-1)
    x = _layernorm(x + _L0_ffn_ref(x, L0_ffn_ln_g, L0_ffn_ln_b, L0_ffn_Wr, L0_ffn_W1, L0_ffn_W3, L0_ffn_W2, L0_ffn_W1s, L0_ffn_W3s, L0_ffn_W2s), axis=-1)
    return x

_drawn_inputs = setup_inputs


def setup_inputs(seed=0):
    import zlib

    import numpy as np

    out = dict(_drawn_inputs(seed))
    spreads = {'L0_ffn_ln_g': (1.0, 0.6), 'L0_ffn_ln_b': (0.0, 0.8)}
    factors = {'L0_attn_Wq': 8.0,
     'L0_attn_Wk': 8.0,
     'L0_attn_Wv': 8.0,
     'L0_attn_Wbeta': 8.0,
     'L0_attn_Wtg': 8.0,
     'L0_attn_mode_logits': 8.0,
     'L0_attn_log_decay': 8.0,
     'L0_attn_omega_log_scale': 8.0,
     'L0_attn_Wg': 8.0,
     'L0_attn_Wo': 8.0,
     'L0_ffn_Wr': 8.0,
     'L0_ffn_W1': 8.0,
     'L0_ffn_W3': 8.0,
     'L0_ffn_W2': 8.0,
     'L0_ffn_W1s': 4.396,
     'L0_ffn_W3s': 4.351,
     'L0_ffn_W2s': 4.355}
    for name, (base, spread) in spreads.items():
        noise = np.random.default_rng([zlib.crc32(name.encode()), seed]).standard_normal(out[name].shape)
        drawn = base * np.exp(spread * noise) if base else spread * noise
        out[name] = jnp.asarray(drawn.astype(out[name].dtype))
    for name, factor in factors.items():
        out[name] = (out[name] * factor).astype(out[name].dtype)
    return out
```

```python
from contextlib import ExitStack

import numpy as np

import concourse.bass as bass
from concourse import mybir

F32 = mybir.dt.float32
U32 = mybir.dt.uint32
ALU = mybir.AluOpType
ACT = mybir.ActivationFunctionType
AX = mybir.AxisListType

B, T, D = 16, 512, 128
H, DK, M = 8, 64, 8
N_TOK = B * T
P = 128
C = 32
NCH = T // C
LO = P // C
HI = M // LO
HP = H * HI
GB = P // HP
NG = B // GB
TILES = N_TOK // P
FF, E_R, CAP = 512, 7, 366
CAPP = 3 * P
ROWS = E_R * CAPP
HALF = DK // 2
LN_EPS = 1e-5
MASKED = -1e4
MAGIC = 12582912.0
TWO_PI_A, TWO_PI_B = 6.28125, 0.0019350051879882812
TWO_PI_C = float(2 * np.pi - TWO_PI_A - TWO_PI_B)
PI_SAFE = 3.1415925


class Tally:

    def __init__(self, eng, sem, base=0):
        self.eng, self.sem, self.base, self.n = eng, sem, base, 0

    def did(self, instruction):
        instruction.then_inc(self.sem, 1)
        self.n += 1

    def value(self):
        return self.base + self.n


def constants():
    p = np.arange(P)
    f = np.float32
    return {
        "ident": np.eye(P, dtype=f),
        "fold": (p[:, None] % C == np.arange(C)[None]).astype(f),
        "pick": (p[:, None] % HI == p[None] // DK).astype(f),
        "own": (p[:, None] // HI == np.arange(P // HI)[None]).astype(f),
        "causal": np.broadcast_to(np.where(np.arange(C)[None] <= np.arange(C)[:, None], 0, MASKED)
                                  .astype(f).reshape(1, C * C), (P, C * C)).copy(),
        "pos": (C * np.arange(NCH)[None] + p[:, None] % C).astype(f),
        "freq": np.broadcast_to((f(1.0) / f(10000.0) ** (np.arange(0, DK, 2, dtype=f) / f(DK)))
                                .astype(f)[None], (P, HALF)).copy(),
        "before": (p[:, None] < p[None]).astype(f),
        "lane": np.broadcast_to(np.arange(8, dtype=f)[None], (P, 8)).copy(),
    }


def scratch(nc):
    def dram(name, shape):
        return nc.dram_tensor(name, shape, F32, kind="Internal").ap()

    return {
        "scal": dram("scal", (4, B, H * M, T)),
        "tab": dram("tab", (NCH, P, 2 * HP * HALF)),
        "kd": dram("kd", (B * NCH, P, HP * DK)),
        "qd": dram("qd", (B * NCH, P, H * LO * C)),
        "od": dram("od", (B * NCH, P, HP * 3 * C)),
        "gd": dram("gd", (B * NCH, P, 2 * HP)),
        "sd": dram("sd", (B * NCH, P, H * LO)),
        "oo": dram("oo", (N_TOK, H * DK)),
        "xT": dram("xT", (D, N_TOK)),
        "xe": dram("xe", (ROWS, D)),
        "ye": dram("ye", (ROWS, D)),
    }


def token_scalars(nc, a, s):
    with ExitStack() as ctx:
        def sb(name, shape):
            return ctx.enter_context(nc.sbuf_tensor("ts_" + name, shape, F32))

        def ps(name, shape):
            return ctx.enter_context(nc.psum_tensor("ts_" + name, shape, F32))

        def sem(name):
            return signal(nc, s, "ts_" + name)

        ident = sb("ident", [P, P])
        wq, wk, wz = sb("wq", [P, H * DK]), sb("wk", [P, H * DK]), sb("wz", [P, 2 * H * M])
        decay = sb("decay", [P, H * M])
        modes = sb("modes", [P, H * M])
        row_a, row_b, row_h = sb("row_a", [P, H * M]), sb("row_b", [P, H * M]), sb("row_h", [P, H])
        ln_rho, ln_w = sb("ln_rho", [P, H * M]), sb("ln_w", [P, H * M])
        x_in, x_t = sb("x_in", [P, D]), sb("x_t", [P, P])
        sq, ss, ln_s = sb("sq", [P, 2 * H * DK]), sb("ss", [P, 2 * H]), sb("ln_s", [P, 2 * H])
        zz, ez, nl = sb("zz", [P, 2 * H * M]), sb("ez", [P, 2 * H * M]), sb("nl", [P, 2 * H * M])
        v = sb("v", [P, 4, H * M])
        v_t = sb("v_t", [P, 2 * P])
        p_x, p_q, p_k, p_z, p_v = (ps(n, [P, 512]) for n in ("p_x", "p_q", "p_k", "p_z", "p_v"))

        loaded, mode_ready = sem("loaded"), sem("mode_ready")
        mode_exp = sem("mode_exp")
        x_loaded, x_turned, x_copied = sem("x_loaded"), sem("x_turned"), sem("x_copied")
        projected, squared, summed = sem("projected"), sem("squared"), sem("summed")
        logged, valued, v_turned, v_copied, v_stored = (
            sem(n) for n in ("logged", "valued", "v_turned", "v_copied", "v_stored"))
        act_own, vec_own, xt_stored = sem("act_own"), sem("vec_own"), sem("xt_stored")
        block = ctx.enter_context(nc.Block())

        @block.sync
        def _(sp):
            for dst, src in ((ident[:, :], a["ident"]), (wq[:, :], a["Wq"]), (wk[:, :], a["Wk"]),
                             (wz[:, 0:H * M], a["Wtg"]), (wz[:, H * M:], a["Wbeta"]),
                             (decay[:, :], a["log_decay"].rearrange("h m -> (h m)").partition_broadcast(P)),
                             (modes[:, :], a["mode_logits"].rearrange("h m -> (h m)").partition_broadcast(P))):
                sp.dma_start(dst, src).then_inc(loaded, 16)
            with sp.Fori(0, B) as b:
                with sp.Fori(0, T // P) as q:
                    i = b * (T // P) + q
                    sp.wait_ge(x_turned, i)
                    sp.dma_start(x_in[:, :], a["x"][b, bass.ds(q * P, P), :]).then_inc(x_loaded, 16)
                    sp.wait_ge(x_copied, i + 1)
                    sp.dma_start(s["xT"][:, bass.ds(i * P, P)], x_t[:, :]).then_inc(xt_stored, 16)
                    sp.wait_ge(v_copied, i + 1)
                    for k in range(4):
                        rows = v_t[64 * (k % 2):64 * (k % 2) + 64, P * (k // 2):P * (k // 2) + P]
                        sp.dma_start(s["scal"][k, b, :, bass.ds(q * P, P)], rows).then_inc(v_stored, 16)
            sp.wait_ge(v_stored, 64 * TILES)
            sp.wait_ge(xt_stored, 16 * TILES)

        @block.tensor
        def _(pe):
            pe.wait_ge(loaded, 16 * 7)
            with pe.Fori(0, TILES) as i:
                pe.wait_ge(x_loaded, i * 16 + 16)
                pe.transpose(p_x[:, 0:P], x_in[:, :], ident[:, :]).then_inc(x_turned, 1)
                pe.wait_ge(x_copied, i + 1)
                pe.matmul(p_q[:, :], x_t[:, :], wq[:, :], start=True, stop=True)
                pe.matmul(p_k[:, :], x_t[:, :], wk[:, :], start=True, stop=True)
                pe.matmul(p_z[:, 0:P], x_t[:, :], wz[:, :], start=True, stop=True).then_inc(projected, 1)
                pe.wait_ge(valued, i + 1)
                pe.transpose(p_v[:, 0:P], v[:, 0:2, :], ident[:, :])
                pe.transpose(p_v[:, P:2 * P], v[:, 2:4, :], ident[:, :]).then_inc(v_turned, 1)

        @block.scalar
        def _(act):
            act.wait_ge(loaded, 16 * 7)
            act.activation(row_a[:, :], decay[:, :], ACT.Exp).then_inc(act_own, 1)
            act.wait_ge(act_own, 1)
            act.activation(ln_rho[:, :], row_a[:, :], ACT.Ln, bias=1.0).then_inc(mode_exp, 1)
            act.wait_ge(mode_ready, 1)
            act.activation(row_b[:, :], modes[:, :], ACT.Exp).then_inc(mode_exp, 1)
            act.wait_ge(mode_ready, 2)
            act.activation(ln_w[:, :], row_a[:, :], ACT.Ln).then_inc(mode_exp, 1)
            with act.Fori(0, TILES) as i:
                act.wait_ge(x_turned, i + 1)
                act.wait_ge(projected, i)
                act.wait_ge(xt_stored, i * 16)
                act.activation(x_t[:, :], p_x[:, 0:P], ACT.Copy).then_inc(x_copied, 1)
                act.wait_ge(projected, i + 1)
                act.wait_ge(summed, i)
                act.activation(sq[:, 0:512], p_q[:, :], ACT.Square)
                act.activation(sq[:, 512:], p_k[:, :], ACT.Square).then_inc(squared, 1)
                act.wait_ge(summed, i + 1)
                act.wait_ge(valued, i)
                act.activation(ln_s[:, :], ss[:, :], ACT.Ln)
                act.activation(ez[:, :], zz[:, :], ACT.Exp).then_inc(act_own, 1)
                act.wait_ge(act_own, i + 2)
                act.activation(nl[:, :], ez[:, :], ACT.Ln, bias=1.0).then_inc(logged, 1)
                act.wait_ge(v_turned, i + 1)
                act.wait_ge(v_stored, i * 64)
                act.activation(v_t[:, :], p_v[:, 0:2 * P], ACT.Copy).then_inc(v_copied, 1)

        @block.vector
        def _(ve):
            own = Tally(ve, vec_own)
            ve.wait_ge(loaded, 16 * 7)
            m3 = modes[:, :].rearrange("p (h m) -> p h m", h=H)
            own.did(ve.tensor_reduce(row_h[:, :], m3, AX.X, ALU.max))
            ve.wait_ge(vec_own, own.value())
            ve.tensor_tensor(m3, m3, row_h[:, :].unsqueeze(2).broadcast_to([P, H, M]), ALU.subtract).then_inc(mode_ready, 1)
            ve.wait_ge(mode_exp, 2)
            b3 = row_b[:, :].rearrange("p (h m) -> p h m", h=H)
            own.did(ve.tensor_reduce(row_h[:, :], b3, AX.X, ALU.add))
            ve.wait_ge(vec_own, own.value())
            own.did(ve.reciprocal(row_h[:, :], row_h[:, :]))
            ve.wait_ge(vec_own, own.value())
            own.did(ve.tensor_tensor(b3, b3, row_h[:, :].unsqueeze(2).broadcast_to([P, H, M]), ALU.mult))
            ve.wait_ge(vec_own, own.value())
            ve.tensor_scalar(row_a[:, :], row_b[:, :], DK ** -0.5, 1e-18, ALU.mult, ALU.max).then_inc(mode_ready, 1)
            ve.wait_ge(mode_exp, 3)
            first = own.value()
            PER = 5
            with ve.Fori(0, TILES) as i:
                own = Tally(ve, vec_own, i * PER + first)
                ve.wait_ge(logged, i)
                ve.wait_ge(projected, i + 1)
                ve.tensor_scalar(zz[:, :], p_z[:, 0:P], -1.0, 40.0, ALU.mult, ALU.min)
                ve.wait_ge(squared, i + 1)
                own.did(ve.tensor_reduce(ss[:, :], sq[:, :].rearrange("p (h d) -> p h d", d=DK), AX.X, ALU.add))
                ve.wait_ge(vec_own, own.value())
                ve.tensor_scalar(ss[:, :], ss[:, :], 1e-6, None, ALU.add).then_inc(summed, 1)
                ve.wait_ge(logged, i + 1)
                ve.wait_ge(v_turned, i)
                own.did(ve.tensor_tensor(v[:, 0, :], nl[:, 0:64], ln_rho[:, :], ALU.add))
                v3 = v[:, 2, :].rearrange("p (h m) -> p h m", h=H)
                own.did(ve.tensor_scalar(v3, ln_s[:, H:2 * H].unsqueeze(2).broadcast_to([P, H, M]), -0.5, None, ALU.mult))
                ve.wait_ge(vec_own, own.value())
                own.did(ve.tensor_scalar(v[:, 0, :], v[:, 0, :], -1.0, float(np.log(1e-6)), ALU.mult, ALU.max))
                own.did(ve.tensor_tensor(v[:, 1, :], v[:, 2, :], nl[:, 64:128], ALU.subtract))
                v4 = v[:, 3, :].rearrange("p (h m) -> p h m", h=H)
                lw3 = ln_w[:, :].rearrange("p (h m) -> p h m", h=H)
                ve.scalar_tensor_tensor(v4, ln_s[:, 0:H].unsqueeze(2).broadcast_to([P, H, M]), -0.5, lw3,
                                        ALU.mult, ALU.add).then_inc(valued, 1)
                assert own.n == PER


def rotary_tables(nc, a, s):
    with ExitStack() as ctx:
        def sb(name, shape):
            return ctx.enter_context(nc.sbuf_tensor("rt_" + name, shape, F32))

        def sem(name):
            return signal(nc, s, "rt_" + name)

        NA = HP * HALF
        om, pos, freq = sb("om", [P, HP]), sb("pos", [P, NCH]), sb("freq", [P, HALF])
        at, ang, n, r = sb("at", [P, HP]), sb("ang", [P, NA]), sb("n", [P, 2 * NA]), sb("r", [P, 2 * NA])
        out = sb("out", [P, 2 * NA])
        loaded, omega_ready, reduced, sines, stored, vec_own = (
            sem(x) for x in ("loaded", "omega_ready", "reduced", "sines", "stored", "vec_own"))
        block = ctx.enter_context(nc.Block())

        @block.sync
        def _(sp):
            logs = a["omega_log_scale"].rearrange("h (i l) -> h i l", i=HI)
            for lo in range(LO):
                sp.dma_start(om[C * lo:C * lo + C, :],
                             logs[:, :, lo].rearrange("h i -> (h i)").partition_broadcast(C), allow_slow_non_contiguous=True).then_inc(loaded, 16)
            sp.dma_start(pos[:, :], a["pos"]).then_inc(loaded, 16)
            sp.dma_start(freq[:, :], a["freq"]).then_inc(loaded, 16)
            with sp.Fori(0, NCH) as j:
                sp.wait_ge(sines, j + 1)
                sp.dma_start(s["tab"][j], out[:, :]).then_inc(stored, 16)
            sp.wait_ge(stored, 16 * NCH)

        @block.scalar
        def _(act):
            act.wait_ge(loaded, 16 * 6)
            act.activation(om[:, :], om[:, :], ACT.Exp).then_inc(omega_ready, 1)
            with act.Fori(0, NCH) as j:
                act.wait_ge(reduced, j + 1)
                act.wait_ge(stored, j * 16)
                act.activation(out[:, :], r[:, :], ACT.Sin).then_inc(sines, 1)

        @block.vector
        def _(ve):
            ve.wait_ge(omega_ready, 1)
            ve.wait_ge(loaded, 16 * 6)
            PER = 10
            with ve.Fori(0, NCH) as j:
                own = Tally(ve, vec_own, j * PER)

                def step(instruction):
                    own.did(instruction)
                    ve.wait_ge(vec_own, own.value())

                step(ve.tensor_scalar(at[:, :], om[:, :], pos[:, bass.ds(j, 1)], None, ALU.mult))
                a3 = ang[:, :].rearrange("p (m f) -> p m f", f=HALF)
                step(ve.tensor_tensor(a3, at[:, :].unsqueeze(2).broadcast_to([P, HP, HALF]),
                                      freq[:, :].unsqueeze(1).broadcast_to([P, HP, HALF]), ALU.mult))
                own.did(ve.tensor_scalar(n[:, 0:NA], ang[:, :], 1 / (2 * np.pi), 0.25, ALU.mult, ALU.add))
                step(ve.tensor_scalar(n[:, NA:], ang[:, :], 1 / (2 * np.pi), None, ALU.mult))
                step(ve.tensor_scalar(n[:, :], n[:, :], MAGIC, None, ALU.add))
                step(ve.tensor_scalar(n[:, :], n[:, :], MAGIC, None, ALU.subtract))
                r3, n3 = (x[:, :].rearrange("p (c f) -> p c f", c=2) for x in (r, n))
                ve.wait_ge(sines, j)
                step(ve.scalar_tensor_tensor(r3, n3, -TWO_PI_A, ang[:, :].unsqueeze(1).broadcast_to([P, 2, NA]),
                                             ALU.mult, ALU.add))
                step(ve.scalar_tensor_tensor(r[:, :], n[:, :], -TWO_PI_B, r[:, :], ALU.mult, ALU.add))
                step(ve.scalar_tensor_tensor(r[:, :], n[:, :], -TWO_PI_C, r[:, :], ALU.mult, ALU.add))
                step(ve.tensor_scalar(r[:, 0:NA], r[:, 0:NA], float(np.pi / 2), None, ALU.add))
                ve.tensor_scalar(r[:, :], r[:, :], PI_SAFE, -PI_SAFE, ALU.min, ALU.max).then_inc(reduced, 1)
                assert own.n == PER


def sooner(pair, p, r):
    return (pair[1], r) if p == 0 else (pair[0], r + 1)


def within_chunks(nc, a, s):
    with ExitStack() as ctx:
        def sb(name, shape):
            return ctx.enter_context(nc.sbuf_tensor("wc_" + name, shape, F32))

        def ps(name, shape):
            return ctx.enter_context(nc.psum_tensor("wc_" + name, shape, F32))

        def sem(name):
            return signal(nc, s, "wc_" + name)

        def two(name):
            return [sem(name + "0"), sem(name + "1")]

        ident, own_bh, pick = sb("ident", [P, P]), sb("own_bh", [P, P // HI]), sb("pick", [P, P])
        causal = sb("causal", [P, C, C])
        wq, wk = sb("wq", [P, H * DK]), sb("wk", [P, H * DK])
        x_g = sb("x_g", [P, GB, C])
        tab = sb("tab", [P, 2, H, HI, HALF])
        x_r = [sb(f"x_r{p}", [P, LO, C]) for p in range(2)]
        q_s = [sb(f"q_s{p}", [P, H, 2, HALF]) for p in range(2)]
        k_rot = [sb(f"k_rot{p}", [P, H, HI, 2, HALF]) for p in range(2)]
        q_rot = [sb(f"q_rot{p}", [P, H, HI, 2, HALF]) for p in range(2)]
        k_tmp, q_tmp = sb("k_tmp", [P, 2, H, HI, HALF]), sb("q_tmp", [P, 2, H, HI, HALF])
        kq_t = [sb(f"kq_t{p}", [P, 2, H, LO, C]) for p in range(2)]
        region = sb("region", [P, P * 3 * C])
        kq = region[:, 0:P * 2 * C].rearrange("p (c x) -> p c x", c=P)
        solved = region[:, :].rearrange("p (c x t) -> p c x t", c=P, x=3)
        raw = sb("raw", [P, 2, C, LO, C])
        ea, ep = sb("ea", [P, C, LO, C]), sb("ep", [P, C, LO, C])
        scal = sb("scal", [P, 4, LO, C])
        cg, cs = sb("cg", [P, LO, C]), sb("cs", [P, LO, C])
        sx, fx = sb("sx", [P, 4, LO, C]), sb("fx", [P, 4, LO, C])
        g_c = sb("g_c", [P, LO])
        g_own = sb("g_own", [P, P // HI, LO])
        ones = sb("ones", [P, C])
        g_out = sb("g_out", [P, 4 * P])
        p_k, p_q = ps("p_k", [P, 512]), ps("p_q", [P, 512])
        p_t = [ps(f"p_t{i}", [P, 512]) for i in range(4)]
        p_kk = [ps(f"p_kk{i}", [P, 512]) for i in range(2)]

        loaded = sem("loaded")
        xg_loaded, tab_loaded, scal_loaded = sem("xg_loaded"), sem("tab_loaded"), sem("scal_loaded")
        xr_ready, projected, q_copied = two("xr_ready"), two("projected"), two("q_copied")
        k_turning, q_turning = two("k_rotated"), two("q_rotated")
        kt_turned, qt_turned, kt_copied, qt_copied = (two(x) for x in ("kt_turned", "qt_turned", "kt_copied", "qt_copied"))
        products, low_copied, high_copied = two("products"), two("low_copied"), two("high_copied")
        k_stored, qt_stored = two("k_stored"), two("qt_stored")
        into_chains, into_copied_v, into_copied_a = sem("into_chains"), sem("into_copied_v"), sem("into_copied_a")
        exponents, exps, small_exponents, small_exps = (
            sem(x) for x in ("exponents", "exps", "small_exponents", "small_exps"))
        vec_own, pool_own, pool_setup, vec_solved, pool_solved = (
            sem(x) for x in ("vec_own", "pool_own", "pool_setup", "vec_solved", "pool_solved"))
        a_ready, queries_ready, scaled_ready, decayed_ready = (
            sem(x) for x in ("a_ready", "queries_ready", "scaled_ready", "decayed_ready"))
        t_cleared = sem("t_cleared")
        out_turned, out_copied_v, out_copied_a = sem("out_turned"), sem("out_copied_v"), sem("out_copied_a")
        g_turned, g_copied, gown_ready = sem("g_turned"), sem("g_copied"), sem("gown_ready")
        solved_stored, g_stored = sem("solved_stored"), sem("g_stored")
        pe_passed, po_passed, ve_passed = sem("pe_passed"), sem("po_passed"), sem("ve_passed")
        block = ctx.enter_context(nc.Block())

        PAIRS = GB // 2
        IN_BANKS = 2 * C // 4
        OUT_BANKS = 3 * C // 4
        SPLIT = 3

        @block.sync
        def _(sp):
            for dst, src in ((ident[:, :], a["ident"]), (own_bh[:, :], a["own"]), (pick[:, :], a["pick"]),
                             (causal[:, :, :], a["causal"].rearrange("p (t s) -> p t s", t=C)),
                             (wq[:, :], a["Wq"]), (wk[:, :], a["Wk"])):
                sp.dma_start(dst, src).then_inc(loaded, 16)
            scal_v = s["scal"].rearrange("v (g b) (c l) t -> v g (b c) l t", g=NG, l=LO)
            x_v = s["xT"].rearrange("d (g b j t) -> d g b j t", g=NG, b=GB, j=NCH)
            out_v = {n: s[n].rearrange("(g b j) p f -> g j p b f", g=NG, b=GB) for n in ("od", "gd", "sd")}
            with sp.Fori(0, NG) as g:
                with sp.Fori(0, NCH) as j:
                    grp = g * NCH + j
                    sp.wait_ge(xr_ready[1], grp * PAIRS)
                    sp.dma_start(x_g[:, :, :], x_v[:, g, :, j, :]).then_inc(xg_loaded, 16)
                    sp.wait_ge(k_turning[1], grp * PAIRS)
                    sp.wait_ge(q_turning[1], grp * PAIRS)
                    sp.dma_start(tab[:, :, :, :, :].rearrange("p x h i f -> p (x h i f)"), s["tab"][j]).then_inc(tab_loaded, 16)
                    sp.wait_ge(small_exponents, grp)
                    for k in range(4):
                        sp.dma_start(scal[:, k, :, :], scal_v[k, g, :, :, bass.ds(j * C, C)]).then_inc(scal_loaded, 16)
                    with sp.Fori(0, PAIRS) as bp:
                        r = grp * PAIRS + bp
                        for p in range(2):
                            n = (g * GB + bp * 2 + p) * NCH + j
                            sp.wait_ge(k_turning[p], r + 1)
                            sp.dma_start(s["kd"][n], k_rot[p][:, :, :, :, :].rearrange("p h i x f -> p (h i x f)")).then_inc(k_stored[p], 16)
                            sp.wait_ge(qt_copied[p], r + 1)
                            sp.dma_start(s["qd"][n], kq_t[p][:, 1, :, :, :].rearrange("p h l t -> p (h l t)")).then_inc(qt_stored[p], 16)
                    sp.wait_ge(out_copied_v, grp * (OUT_BANKS // 2) + OUT_BANKS // 2)
                    sp.wait_ge(out_copied_a, grp * (OUT_BANKS // 2) + OUT_BANKS // 2)
                    sp.dma_start(out_v["od"][g, j], region[:, :].rearrange("p (b f) -> p b f", b=GB)).then_inc(solved_stored, 16)
                    sp.wait_ge(g_copied, grp + 1)
                    for k in range(2):
                        sp.dma_start(out_v["gd"][g, j][:, :, k * HP:(k + 1) * HP],
                                     g_out[:, k * P:(k + 1) * P].rearrange("p (b c) -> p b c", b=GB)).then_inc(g_stored, 16)
                    sp.dma_start(out_v["sd"][g, j], g_out[:, 2 * P:].rearrange("p (b c) -> p b c", b=GB)).then_inc(g_stored, 16)
            GRPS = NG * NCH
            for p in range(2):
                sp.wait_ge(k_stored[p], 16 * GRPS * PAIRS)
                sp.wait_ge(qt_stored[p], 16 * GRPS * PAIRS)
            sp.wait_ge(solved_stored, 16 * GRPS)
            sp.wait_ge(g_stored, 48 * GRPS)

        @block.tensor
        def _(pe):
            pe.wait_ge(loaded, 16 * 6)
            pe.wait_ge(pool_setup, 1)
            with pe.Fori(0, NG * NCH) as grp:
                pe.wait_ge(out_copied_v, grp * (OUT_BANKS // 2))
                pe.wait_ge(out_copied_a, grp * (OUT_BANKS // 2))
                pe.wait_ge(g_copied, grp)
                apart(pe, pe_passed)
                with pe.Fori(0, PAIRS) as bp:
                    r = grp * PAIRS + bp

                    def project(p):
                        pe.wait_ge(xr_ready[p], r + 1)
                        pe.wait_ge(*sooner(k_turning, p, r))
                        pe.wait_ge(*sooner(q_copied, p, r))
                        rep = x_r[p][:, :, :].rearrange("p l t -> p (l t)")
                        pe.matmul(p_k[:, :], rep, wk[:, :], start=True, stop=True)
                        pe.matmul(p_q[:, :], rep, wq[:, :], start=True, stop=True).then_inc(projected[p], 1)

                    def turn(p):
                        pe.wait_ge(k_turning[p], r + 1)
                        pe.wait_ge(*sooner(kt_copied, p, r))
                        for h in range(H):
                            last = pe.transpose(p_t[h // 4][:, P * (h % 4):P * (h % 4) + P],
                                                k_rot[p][:, h, :, :, :].rearrange("p i x f -> p (i x f)"), ident[:, :])
                        last.then_inc(kt_turned[p], 1)
                        pe.wait_ge(q_turning[p], r + 1)
                        pe.wait_ge(*sooner(qt_copied, p, r))
                        for h in range(H):
                            last = pe.transpose(p_t[2 + h // 4][:, P * (h % 4):P * (h % 4) + P],
                                                q_rot[p][:, h, :, :, :].rearrange("p i x f -> p (i x f)"), ident[:, :])
                        last.then_inc(qt_turned[p], 1)

                    def multiply(p):
                        pe.wait_ge(kt_copied[p], r + 1)
                        pe.wait_ge(qt_copied[p], r + 1)
                        pe.wait_ge(*sooner(low_copied, p, r))
                        pe.wait_ge(*sooner(high_copied, p, r))
                        apart(pe, pe_passed)
                        for h in range(H):
                            for lo in range(LO):
                                for hi in range(HI):
                                    rows = slice(DK * hi, DK * hi + DK)
                                    last = pe.matmul(p_kk[hi][C * lo:C * lo + C, 2 * C * h:2 * C * h + 2 * C],
                                                     kq_t[p][rows, 0, h, lo, :], kq_t[p][rows, :, h, lo, :],
                                                     start=True, stop=True, tile_position=(DK * hi, C * lo))
                        last.then_inc(products[p], 1)

                    project(0)
                    turn(0)
                    project(1)
                    multiply(0)
                    turn(1)
                    multiply(1)
                pe.wait_ge(low_copied[1], grp * PAIRS + PAIRS)
                pe.wait_ge(high_copied[1], grp * PAIRS + PAIRS)
                pe.wait_ge(kt_copied[1], grp * PAIRS + PAIRS)
                for k in range(IN_BANKS):
                    if k >= 4:
                        pe.wait_ge(into_copied_a if k % 2 else into_copied_v, grp * (IN_BANKS // 2) + (k - 4) // 2 + 1)
                    for i in range(4):
                        last = pe.transpose(p_t[k % 4][:, P * i:P * i + P], kq[:, :, 4 * k + i], ident[:, :])
                    last.then_inc(into_chains, 1)
                pe.wait_ge(small_exps, grp + 1)
                pe.wait_ge(gown_ready, grp + 1)
                for i in range(2):
                    pe.transpose(p_kk[0][:, P * i:P * i + P], fx[:, 2 + i, :, :].rearrange("p l t -> p (l t)"), ident[:, :])
                pe.matmul(p_kk[0][:, 2 * P:4 * P], pick[:, :], g_own[:, :, :].rearrange("p c l -> p (c l)"),
                          start=True, stop=True).then_inc(g_turned, 1)
                for k in range(OUT_BANKS):
                    form, t0 = k // (C // 4), k % (C // 4) * 4
                    if t0 == 0:
                        pe.wait_ge((queries_ready, scaled_ready, decayed_ready)[form], grp + 1)
                    if k >= 4:
                        pe.wait_ge(out_copied_a if k % 2 else out_copied_v, grp * (OUT_BANKS // 2) + (k - 4) // 2 + 1)
                    else:
                        pe.wait_ge(into_copied_a if k % 2 else into_copied_v, grp * (IN_BANKS // 2) + IN_BANKS // 2)
                    src = (raw[:, 1], ea, raw[:, 0])[form]
                    for i in range(4):
                        at = src[:, t0 + i, :, :].rearrange("p l s -> p (l s)")
                        last = pe.transpose(p_t[k % 4][:, P * i:P * i + P], at, ident[:, :])
                    last.then_inc(out_turned, 1)

        @block.scalar
        def _(act):
            act.wait_ge(loaded, 16 * 6)
            with act.Fori(0, NG * NCH) as grp:
                act.wait_ge(xg_loaded, grp * 16 + 16)
                with act.Fori(0, PAIRS) as bp:
                    r = grp * PAIRS + bp

                    def replicate(p):
                        act.wait_ge(projected[p], r)
                        act.activation(x_r[p][:, :, :], x_g[:, bass.ds(bp * 2 + p, 1), :].broadcast_to([P, LO, C]),
                                       ACT.Copy).then_inc(xr_ready[p], 1)

                    def copy_q(p):
                        act.wait_ge(projected[p], r + 1)
                        act.wait_ge(q_turning[p], r)
                        act.activation(q_s[p][:, :, :, :].rearrange("p h x f -> p (h x f)"), p_q[:, :], ACT.Copy).then_inc(q_copied[p], 1)

                    def copy_turned(p):
                        act.wait_ge(qt_turned[p], r + 1)
                        act.wait_ge(products[p], r)
                        act.wait_ge(qt_stored[p], r * 16)
                        for i in range(2):
                            last = act.activation(kq_t[p][:, 1, 4 * i:4 * i + 4, :, :].rearrange("p h l t -> p (h l t)"),
                                                  p_t[2 + i][:, :], ACT.Copy)
                        last.then_inc(qt_copied[p], 1)

                    def copy_products(p):
                        act.wait_ge(products[p], r + 1)
                        base = (bp * 2 + p) * HP
                        act.activation(kq[:, bass.ds(base + 1, H, HI), :],
                                       p_kk[1][:, :].rearrange("p (h x) -> p h x", h=H), ACT.Copy).then_inc(high_copied[p], 1)

                    act.wait_ge(solved_stored, grp * 16)
                    replicate(0)
                    copy_q(0)
                    replicate(1)
                    copy_turned(0)
                    copy_q(1)
                    copy_products(0)
                    copy_turned(1)
                    copy_products(1)
                act.wait_ge(small_exponents, grp + 1)
                act.wait_ge(g_turned, grp)
                act.wait_ge(scaled_ready, grp)
                act.activation(fx[:, :, :, :].rearrange("p k l t -> p (k l t)"),
                               sx[:, :, :, :].rearrange("p k l t -> p (k l t)"), ACT.Exp)
                act.activation(g_c[:, :], cg[:, :, C - 1], ACT.Exp).then_inc(small_exps, 1)
                for k in range(1, IN_BANKS, 2):
                    act.wait_ge(into_chains, grp * IN_BANKS + k + 1)
                    act.activation(raw[:, k // 8, 4 * (k % 8):4 * (k % 8) + 4, :, :].rearrange("p t l s -> p (t l s)"),
                                   p_t[k % 4][:, :], ACT.Copy).then_inc(into_copied_a, 1)
                for i, e in enumerate((ea, ep)):
                    act.wait_ge(exponents, grp * 2 + i + 1)
                    act.activation(e[:, :, :, :].rearrange("p t l s -> p (t l s)"),
                                   e[:, :, :, :].rearrange("p t l s -> p (t l s)"), ACT.Exp).then_inc(exps, 1)
                act.wait_ge(g_turned, grp + 1)
                act.wait_ge(g_stored, grp * 48)
                act.activation(g_out[:, :], p_kk[0][:, :], ACT.Copy).then_inc(g_copied, 1)
                for k in range(1, OUT_BANKS, 2):
                    form, t0 = k // (C // 4), k % (C // 4) * 4
                    act.wait_ge(out_turned, grp * OUT_BANKS + k + 1)
                    if k == 1:
                        act.wait_ge(into_chains, grp * IN_BANKS + IN_BANKS)
                    act.activation(solved[:, :, form, t0:t0 + 4], p_t[k % 4][:, :].rearrange("p (t c) -> p c t", t=4),
                                   ACT.Copy).then_inc(out_copied_a, 1)

        def solve(eng, own, los):
            n = los.stop - los.start
            for i in range(C - 1):
                below, seen = C - 1 - i, i + 1
                part = ep[:, i + 1:C, los, 0:seen]
                eng.wait_ge(own.sem, own.value())
                own.did(eng.tensor_tensor(part, raw[:, 0, i + 1:C, los, i:i + 1].broadcast_to([P, below, n, seen]),
                                          ea[:, i:i + 1, los, 0:seen].broadcast_to([P, below, n, seen]), ALU.mult))
                eng.wait_ge(own.sem, own.value())
                rest = ea[:, i + 1:C, los, 0:seen]
                own.did(eng.tensor_tensor(rest, rest, part, ALU.subtract))

        @block.gpsimd
        def _(po):
            po.memset(ones[:, :], 1.0).then_inc(pool_setup, 1)
            with po.Fori(0, NG * NCH) as grp:
                po.wait_ge(tab_loaded, grp * 16 + 16)
                apart(po, po_passed)
                with po.Fori(0, PAIRS) as bp:
                    r = grp * PAIRS + bp
                    for p in range(2):
                        own = Tally(po, pool_own, grp * (PAIRS * 8) + bp * 8 + p * 4)
                        po.wait_ge(q_copied[p], r + 1)
                        po.wait_ge(qt_turned[p], r)
                        po.wait_ge(*sooner(q_turning, p, r))
                        for x in range(2):
                            own.did(po.tensor_tensor(q_rot[p][:, :, :, x, :],
                                                     q_s[p][:, :, x, :].unsqueeze(2).broadcast_to([P, H, HI, HALF]),
                                                     tab[:, 0, :, :, :], ALU.mult))
                            own.did(po.tensor_tensor(q_tmp[:, x, :, :, :],
                                                     q_s[p][:, :, 1 - x, :].unsqueeze(2).broadcast_to([P, H, HI, HALF]),
                                                     tab[:, 1, :, :, :], ALU.mult))
                        po.wait_ge(pool_own, own.value())
                        for x, op in ((0, ALU.add), (1, ALU.subtract)):
                            last = po.tensor_tensor(q_rot[p][:, :, :, x, :], q_rot[p][:, :, :, x, :], q_tmp[:, x, :, :, :], op)
                        last.then_inc(q_turning[p], 1)
                po.wait_ge(a_ready, grp + 1)
                po.wait_ge(t_cleared, grp * LO + LO)
                po.wait_ge(queries_ready, grp + 1)
                own = Tally(po, pool_solved, grp * 2 * (C - 1))
                solve(po, own, slice(SPLIT, LO))

        @block.vector
        def _(ve):
            ve.wait_ge(loaded, 16 * 6)
            ve.wait_ge(pool_setup, 1)
            STEPS = 10
            with ve.Fori(0, NG * NCH) as grp:
                ve.wait_ge(tab_loaded, grp * 16 + 16)
                apart(ve, ve_passed)
                with ve.Fori(0, PAIRS) as bp:
                    r = grp * PAIRS + bp

                    def rotate(p):
                        own = Tally(ve, vec_own, grp * (STEPS + PAIRS * 8) + bp * 8 + p * 4)
                        ve.wait_ge(projected[p], r + 1)
                        ve.wait_ge(kt_turned[p], r)
                        ve.wait_ge(k_stored[p], r * 16)
                        ve.wait_ge(*sooner(k_turning, p, r))
                        k4 = p_k[:, :].rearrange("p (h x f) -> p h x f", h=H, x=2)
                        for x in range(2):
                            own.did(ve.tensor_tensor(k_rot[p][:, :, :, x, :],
                                                     k4[:, :, x, :].unsqueeze(2).broadcast_to([P, H, HI, HALF]),
                                                     tab[:, 0, :, :, :], ALU.mult))
                            own.did(ve.tensor_tensor(k_tmp[:, x, :, :, :],
                                                     k4[:, :, 1 - x, :].unsqueeze(2).broadcast_to([P, H, HI, HALF]),
                                                     tab[:, 1, :, :, :], ALU.mult))
                        ve.wait_ge(vec_own, own.value())
                        for x, op in ((0, ALU.add), (1, ALU.subtract)):
                            last = ve.tensor_tensor(k_rot[p][:, :, :, x, :], k_rot[p][:, :, :, x, :], k_tmp[:, x, :, :, :], op)
                        last.then_inc(k_turning[p], 1)

                    def copy_turned(p):
                        ve.wait_ge(kt_turned[p], r + 1)
                        ve.wait_ge(products[p], r)
                        for i in range(2):
                            last = ve.tensor_copy(kq_t[p][:, 0, 4 * i:4 * i + 4, :, :].rearrange("p h l t -> p (h l t)"), p_t[i][:, :])
                        last.then_inc(kt_copied[p], 1)

                    def copy_products(p):
                        ve.wait_ge(products[p], r + 1)
                        base = (bp * 2 + p) * HP
                        ve.tensor_copy(kq[:, bass.ds(base, H, HI), :],
                                       p_kk[0][:, :].rearrange("p (h x) -> p h x", h=H)).then_inc(low_copied[p], 1)

                    ve.wait_ge(solved_stored, grp * 16)
                    rotate(0)
                    copy_turned(0)
                    rotate(1)
                    copy_products(0)
                    copy_turned(1)
                    copy_products(1)
                own = Tally(ve, vec_own, grp * (STEPS + PAIRS * 8) + PAIRS * 8)

                def settle():
                    ve.wait_ge(vec_own, own.value())

                ve.wait_ge(scal_loaded, grp * 64 + 64)
                ve.wait_ge(small_exps, grp)
                for lo in range(LO):
                    own.did(ve.tensor_tensor_scan(cg[:, lo, :], ones[:, :], scal[:, 0, lo, :], 0.0, ALU.mult, ALU.add))
                settle()
                own.did(ve.tensor_tensor(cs[:, :, :], cg[:, :, :], scal[:, 2, :, :], ALU.subtract))
                own.did(ve.tensor_tensor(sx[:, 0, :, :], scal[:, 1, :, :], scal[:, 2, :, :], ALU.subtract))
                own.did(ve.tensor_tensor(sx[:, 1, :, :], scal[:, 1, :, :], cg[:, :, :], ALU.add))
                own.did(ve.tensor_tensor(sx[:, 3, :, :], scal[:, 3, :, :], cg[:, :, :], ALU.add))
                settle()
                ve.tensor_tensor(sx[:, 2, :, :], cg[:, :, C - 1:C].broadcast_to([P, LO, C]), cs[:, :, :],
                                 ALU.subtract).then_inc(small_exponents, 1)
                ve.wait_ge(out_turned, grp * OUT_BANKS)
                own.did(ve.tensor_tensor(ep[:, :, :, :], causal[:, :, :].unsqueeze(2).broadcast_to([P, C, LO, C]),
                                         cs[:, :, :].unsqueeze(1).broadcast_to([P, C, LO, C]), ALU.subtract))
                settle()
                by_t = lambda x: x.rearrange("p l t -> p t l").unsqueeze(3).broadcast_to([P, C, LO, C])
                ve.tensor_tensor(ea[:, :, :, :], ep[:, :, :, :], by_t(sx[:, 1, :, :]), ALU.add).then_inc(exponents, 1)
                ve.wait_ge(exponents, grp * 2 + 1)
                ve.tensor_tensor(ep[:, :, :, :], ep[:, :, :, :], by_t(sx[:, 3, :, :]), ALU.add).then_inc(exponents, 1)
                ve.wait_ge(exponents, grp * 2 + 2)
                for k in range(0, IN_BANKS, 2):
                    ve.wait_ge(into_chains, grp * IN_BANKS + k + 1)
                    ve.tensor_copy(raw[:, k // 8, 4 * (k % 8):4 * (k % 8) + 4, :, :].rearrange("p t l s -> p (t l s)"),
                                   p_t[k % 4][:, :]).then_inc(into_copied_v, 1)
                ve.wait_ge(small_exps, grp + 1)
                ve.tensor_tensor(g_own[:, :, :], own_bh[:, :].unsqueeze(2).broadcast_to([P, P // HI, LO]),
                                 g_c[:, :].unsqueeze(1).broadcast_to([P, P // HI, LO]), ALU.mult).then_inc(gown_ready, 1)
                ve.wait_ge(into_copied_v, grp * (IN_BANKS // 2) + IN_BANKS // 2)
                ve.wait_ge(into_copied_a, grp * (IN_BANKS // 2) + IN_BANKS // 2)
                ve.wait_ge(exps, grp * 2 + 1)
                ve.tensor_tensor(raw[:, 0, :, :, :], raw[:, 0, :, :, :], ea[:, :, :, :], ALU.mult).then_inc(a_ready, 1)
                ve.wait_ge(exps, grp * 2 + 2)
                ve.tensor_tensor(raw[:, 1, :, :, :], raw[:, 1, :, :, :], ep[:, :, :, :], ALU.mult).then_inc(queries_ready, 1)
                ve.wait_ge(a_ready, grp + 1)
                own.did(ve.memset(ea[:, :, :, :], 0.0))
                settle()
                flat = ea[:, :, :, :].rearrange("p t l s -> p (t l s)")
                for lo in range(LO):
                    ve.memset(flat[:, C * lo:C * lo + (LO * C + 1) * (C - 1) + 1:LO * C + 1], 1.0).then_inc(t_cleared, 1)
                ve.wait_ge(t_cleared, grp * LO + LO)
                ve.wait_ge(queries_ready, grp + 1)
                solving = Tally(ve, vec_solved, grp * 2 * (C - 1))
                solve(ve, solving, slice(0, SPLIT))
                ve.wait_ge(vec_solved, solving.value())
                ve.wait_ge(pool_solved, grp * 2 * (C - 1) + 2 * (C - 1))
                by_s = lambda x: x.unsqueeze(1).broadcast_to([P, C, LO, C])
                ve.wait_ge(small_exps, grp + 1)
                ve.tensor_tensor(raw[:, 0, :, :, :], ea[:, :, :, :], by_s(fx[:, 1, :, :]), ALU.mult).then_inc(decayed_ready, 1)
                ve.wait_ge(decayed_ready, grp + 1)
                ve.tensor_tensor(ea[:, :, :, :], ea[:, :, :, :], by_s(fx[:, 0, :, :]), ALU.mult).then_inc(scaled_ready, 1)
                assert own.n == STEPS, own.n
                for k in range(0, OUT_BANKS, 2):
                    form, t0 = k // (C // 4), k % (C // 4) * 4
                    ve.wait_ge(out_turned, grp * OUT_BANKS + k + 1)
                    ve.tensor_copy(solved[:, :, form, t0:t0 + 4],
                                   p_t[k % 4][:, :].rearrange("p (t c) -> p c t", t=4)).then_inc(out_copied_v, 1)


def across_chunks(nc, a, s):
    with ExitStack() as ctx:
        def sb(name, shape):
            return ctx.enter_context(nc.sbuf_tensor("ac_" + name, shape, F32))

        def ps(name, shape):
            return ctx.enter_context(nc.psum_tensor("ac_" + name, shape, F32))

        def sem(name):
            return signal(nc, s, "ac_" + name)

        def two(name):
            return [sem(name + "0"), sem(name + "1")]

        HH = H // 2
        wv, fold = sb("wv", [P, H * DK]), sb("fold", [P, C])
        x_c = [sb(f"x_c{p}", [P, C]) for p in range(2)]
        x_r = [sb(f"x_r{p}", [P, LO, C]) for p in range(2)]
        k_in = [sb(f"k_in{p}", [P, HP, DK]) for p in range(2)]
        q_in = [sb(f"q_in{p}", [P, H, LO, C]) for p in range(2)]
        forms = [sb(f"forms{p}", [P, HP, 3, C]) for p in range(2)]
        g_in = [sb(f"g_in{p}", [P, 2, HP]) for p in range(2)]
        decay = [sb(f"decay{p}", [P, H, LO]) for p in range(2)]
        v_s = [sb(f"v_s{p}", [P, H, DK]) for p in range(2)]
        k_s = [sb(f"k_s{p}", [P, HP, DK]) for p in range(2)]
        state = sb("state", [P, H, LO, DK])
        w_t = [sb(f"w_t{h}", [P, HH, LO, C]) for h in range(2)]
        u = [sb(f"u{h}", [P, HI, HH, DK]) for h in range(2)]
        qs = [sb(f"qs{h}", [P, HI, HH, DK]) for h in range(2)]
        o_out = [sb(f"o_out{p}", [C, H * DK]) for p in range(2)]
        p_m = [ps(f"p_m{i}", [P, 512]) for i in range(LO)]
        p_h = [ps(f"p_h{i}", [P, 512]) for i in range(HI)]
        p_o, p_v = ps("p_o", [P, 512]), ps("p_v", [P, 512])
        UPD = [m[:, 0:HH * DK] for m in p_m]
        WT = [m[:, HH * DK:HH * DK + HH * C] for m in p_m]
        US = [m[:, 0:HH * DK] for m in p_h]
        QS = [m[:, HH * DK:] for m in p_h]

        loaded, cleared, pe_passed = sem("loaded"), sem("cleared"), sem("pe_passed")
        x_loaded, in_loaded, scal_loaded = two("x_loaded"), two("in_loaded"), two("scal_loaded")
        replicated, v_done, v_copied, keys_scaled = (sem(x) for x in ("replicated", "v_done", "v_copied", "keys_scaled"))
        w_done, w_copied, u_done, u_copied = two("w_done"), two("w_copied"), two("u_done"), two("u_copied")
        decayed, updated, applied_low = two("decayed"), two("updated"), sem("applied_low")
        turn_over = two("turn_over")
        o_done, o_copied, o_stored = sem("o_done"), sem("o_copied"), two("o_stored")
        block = ctx.enter_context(nc.Block())
        J2 = NCH // 2

        @block.sync
        def _(sp):
            sp.dma_start(wv[:, :], a["Wv"]).then_inc(loaded, 16)
            sp.dma_start(fold[:, :], a["fold"]).then_inc(loaded, 16)
            with sp.Fori(0, B * J2) as r:
                for p in range(2):
                    n = r * 2 + p
                    sp.wait_ge(turn_over[p], r)
                    sp.dma_start(x_c[p][:, :], s["xT"][:, bass.ds(n * C, C)]).then_inc(x_loaded[p], 16)
                    sp.dma_start(k_in[p][:, :, :].rearrange("p c k -> p (c k)"), s["kd"][n]).then_inc(in_loaded[p], 16)
                    sp.dma_start(forms[p][:, :, :, :].rearrange("p c x t -> p (c x t)"), s["od"][n]).then_inc(in_loaded[p], 16)
                    sp.dma_start(q_in[p][:, :, :, :].rearrange("p h l t -> p (h l t)"), s["qd"][n]).then_inc(in_loaded[p], 16)
                    sp.dma_start(g_in[p][:, :, :].rearrange("p x c -> p (x c)"), s["gd"][n]).then_inc(scal_loaded[p], 16)
                    sp.dma_start(decay[p][:, :, :].rearrange("p h l -> p (h l)"), s["sd"][n]).then_inc(scal_loaded[p], 16)

        @block.tensor
        def _(pe):
            pe.wait_ge(loaded, 32)
            with pe.Fori(0, B) as b:
                pe.wait_ge(cleared, b + 1)
                apart(pe, pe_passed)
                with pe.Fori(0, J2) as j:
                    r = b * J2 + j
                    for p in range(2):
                        n = r * 2 + p

                        def units(half):
                            return [(h, half * HH + h) for h in range(HH)]

                        def turn_w(half):
                            if half == 0:
                                pe.wait_ge(in_loaded[p], r * 48 + 48)
                                pe.wait_ge(*sooner(turn_over, p, r))
                            else:
                                pe.wait_ge(w_copied[0], n + 1)
                            apart(pe, pe_passed)
                            for h, head in units(half):
                                for lo in range(LO):
                                    rows = slice(C * lo, C * lo + C)
                                    for hi in range(HI):
                                        last = pe.matmul(WT[lo][DK * hi:DK * hi + DK, C * h:C * h + C],
                                                         k_in[p][rows, head * HI + hi, :], forms[p][rows, head * HI + hi, 2, :],
                                                         start=True, stop=True, tile_position=(C * lo, DK * hi))
                            last.then_inc(w_done[half], 1)

                        def solve_u(half):
                            if half == 0:
                                pe.wait_ge(v_copied, n + 1)
                                pe.wait_ge(u_copied[1], n)
                            else:
                                pe.wait_ge(u_copied[0], n + 1)
                            apart(pe, pe_passed)
                            for h, head in units(half):
                                for hi in range(HI):
                                    for lo in range(LO):
                                        rows = slice(C * lo, C * lo + C)
                                        pe.matmul(US[hi][rows, DK * h:DK * h + DK], forms[p][rows, head * HI + hi, 1, :],
                                                  v_s[p][rows, head, :], start=h == 0, stop=False,
                                                  tile_position=(C * lo, C * lo), skip_group_check=True)
                            if half == 0:
                                pe.wait_ge(applied_low, n)
                            else:
                                pe.wait_ge(*sooner(turn_over, p, r))
                            apart(pe, pe_passed)
                            for h, head in units(half):
                                for lo in range(LO):
                                    for hi in range(HI):
                                        rows = slice(DK * hi, DK * hi + DK)
                                        pe.matmul(QS[hi][C * lo:C * lo + C, DK * h:DK * h + DK], q_in[p][rows, head, lo, :],
                                                  state[rows, head, lo, :], start=False, stop=True,
                                                  tile_position=(DK * hi, C * lo), skip_group_check=True)
                            pe.wait_ge(w_copied[half], n + 1)
                            apart(pe, pe_passed)
                            for h, head in units(half):
                                for lo in range(LO):
                                    for hi in range(HI):
                                        rows = slice(DK * hi, DK * hi + DK)
                                        last = pe.matmul(US[hi][C * lo:C * lo + C, DK * h:DK * h + DK], w_t[half][rows, h, lo, :],
                                                         state[rows, head, lo, :], start=False, stop=True,
                                                         tile_position=(DK * hi, C * lo), skip_group_check=True)
                            last.then_inc(u_done[half], 1)

                        def output(half):
                            pe.wait_ge(u_copied[half], n + 1)
                            if half == 0:
                                pe.wait_ge(o_copied, n)
                            cols = slice(half * HH * DK, (half + 1) * HH * DK)
                            for hi in range(HI):
                                pe.matmul(p_o[0:C, cols], fold[:, :], qs[half][:, hi, :, :].rearrange("p h v -> p (h v)"),
                                          start=hi == 0, stop=False, skip_group_check=True)
                            for h, head in units(half):
                                for hi in range(HI):
                                    last = pe.matmul(p_o[0:C, DK * head:DK * head + DK], forms[p][:, head * HI + hi, 0, :],
                                                     u[half][:, hi, h, :], start=False, stop=True, skip_group_check=True)
                            if half == 1:
                                last.then_inc(o_done, 1)

                        def update(half):
                            if half == 0:
                                pe.wait_ge(keys_scaled, n + 1)
                                pe.wait_ge(w_copied[1], n + 1)
                            else:
                                pe.wait_ge(applied_low, n + 1)
                            apart(pe, pe_passed)
                            for h, head in units(half):
                                for lo in range(LO):
                                    rows = slice(C * lo, C * lo + C)
                                    for hi in range(HI):
                                        last = pe.matmul(UPD[lo][DK * hi:DK * hi + DK, DK * h:DK * h + DK],
                                                         k_s[p][rows, head * HI + hi, :], u[half][rows, hi, h, :],
                                                         start=True, stop=True, tile_position=(C * lo, DK * hi))
                            last.then_inc(updated[half], 1)

                        pe.wait_ge(replicated, n + 1)
                        pe.wait_ge(v_copied, n)
                        pe.matmul(p_v[:, :], x_r[p][:, :, :].rearrange("p l t -> p (l t)"), wv[:, :],
                                  start=True, stop=True).then_inc(v_done, 1)
                        turn_w(0)
                        solve_u(0)
                        turn_w(1)
                        output(0)
                        update(0)
                        solve_u(1)
                        output(1)
                        update(1)

        @block.scalar
        def _(act):
            with act.Fori(0, B * J2) as r:
                for p in range(2):
                    n = r * 2 + p
                    act.wait_ge(x_loaded[p], r * 16 + 16)
                    act.activation(x_r[p][:, :, :], x_c[p][:, :].unsqueeze(1).broadcast_to([P, LO, C]),
                                   ACT.Copy).then_inc(replicated, 1)
                    act.wait_ge(v_done, n + 1)
                    act.activation(v_s[p][:, :, :].rearrange("p h v -> p (h v)"), p_v[:, :], ACT.Copy).then_inc(v_copied, 1)
                    for half in range(2):
                        act.wait_ge(w_done[half], n + 1)
                        act.wait_ge(u_done[half], n)
                        for lo in range(LO):
                            last = act.activation(w_t[half][:, :, lo, :], WT[lo].rearrange("p (h t) -> p h t", h=HH),
                                                  ACT.Copy, scale=-1.0)
                        last.then_inc(w_copied[half], 1)
                    act.wait_ge(o_done, n + 1)
                    act.wait_ge(o_stored[p], r * 16)
                    act.activation(o_out[p][:, :], p_o[0:C, :], ACT.Copy).then_inc(o_copied, 1)
                    act.wait_ge(o_copied, n + 1)
                    act.dma_start(s["oo"][bass.ds(n * C, C), :], o_out[p][:, :]).then_inc(o_stored[p], 16)
            for p in range(2):
                act.wait_ge(o_stored[p], 16 * B * J2)

        @block.gpsimd
        def _(po):
            with po.Fori(0, B * J2) as r:
                for p in range(2):
                    n = r * 2 + p
                    po.wait_ge(in_loaded[p], r * 48 + 48)
                    po.wait_ge(scal_loaded[p], r * 32 + 32)
                    po.tensor_tensor(k_s[p][:, :, :], k_in[p][:, :, :],
                                     g_in[p][:, 0, :].unsqueeze(2).broadcast_to([P, HP, DK]), ALU.mult).then_inc(keys_scaled, 1)
                    for half in range(2):
                        po.wait_ge(u_done[half], n + 1)
                        part = state[:, half * HH:half * HH + HH, :, :]
                        po.tensor_tensor(part, part, decay[p][:, half * HH:half * HH + HH, :].unsqueeze(3)
                                         .broadcast_to([P, HH, LO, DK]), ALU.mult).then_inc(decayed[half], 1)

        @block.vector
        def _(ve):
            ve.memset(state[:, :, :, :], 0.0).then_inc(cleared, 1)
            with ve.Fori(0, B) as b:
                with ve.Fori(0, J2) as j:
                    r = b * J2 + j
                    for p in range(2):
                        n = r * 2 + p

                        def copy_u(half):
                            ve.wait_ge(u_done[half], n + 1)
                            ve.wait_ge(updated[half], n)
                            ve.wait_ge(scal_loaded[p], r * 32 + 32)
                            for hi in range(HI):
                                ve.tensor_copy(u[half][:, hi, :, :].rearrange("p h v -> p (h v)"), US[hi])
                                gq = g_in[p][:, 1, :].rearrange("p (h i) -> p h i", i=HI)[:, half * HH:half * HH + HH, hi]
                                last = ve.tensor_tensor(qs[half][:, hi, :, :], QS[hi].rearrange("p (h v) -> p h v", h=HH),
                                                        gq.unsqueeze(2).broadcast_to([P, HH, DK]), ALU.mult)
                            last.then_inc(u_copied[half], 1)

                        def apply(half):
                            ve.wait_ge(updated[half], n + 1)
                            ve.wait_ge(decayed[half], n + 1)
                            for lo in range(LO):
                                part = state[:, half * HH:half * HH + HH, lo, :]
                                last = ve.tensor_tensor(part, part, UPD[lo].rearrange("p (h v) -> p h v", h=HH), ALU.add)
                            last.then_inc(turn_over[p] if half else applied_low, 1)

                        copy_u(0)
                        apply(0)
                        copy_u(1)
                        apply(1)
                ve.wait_ge(turn_over[1], b * J2 + J2)
                ve.wait_ge(applied_low, b * NCH + NCH)
                ve.memset(state[:, :, :, :], 0.0).then_inc(cleared, 1)



def after_attention(nc, a, s, w):
    with ExitStack() as ctx:
        def sb(name, shape):
            return ctx.enter_context(nc.sbuf_tensor("aa_" + name, shape, F32))

        def ps(name, shape):
            return ctx.enter_context(nc.psum_tensor("aa_" + name, shape, F32))

        def sem(name):
            return signal(nc, s, "aa_" + name)

        def two(name):
            return [sem(name + "0"), sem(name + "1")]

        KO = H * DK // P
        ident, wg, wo = sb("ident", [P, P]), sb("wg", [P, H * DK]), sb("wo", [P, KO, D])
        x_t = [sb(f"x_t{p}", [P, P]) for p in range(2)]
        x_in = [sb(f"x_in{p}", [P, D]) for p in range(2)]
        o_in = [sb(f"o_in{p}", [P, H * DK]) for p in range(2)]
        z = [sb(f"z{p}", [P, H * DK]) for p in range(2)]
        og = [sb(f"og{p}", [P, H * DK]) for p in range(2)]
        og_t = [sb(f"og_t{p}", [P, KO, P]) for p in range(2)]
        p_g, p_t, p_a = ([ps(f"{n}{p}", [P, 512]) for p in range(2)] for n in ("p_g", "p_t", "p_a"))
        loaded = sem("loaded")
        in_loaded = two("in_loaded")
        gate_done, z_ready, gate_ready, gated, turned, copied, out_done, added, act_own = (
            two(x) for x in ("gate_done", "z_ready", "gate_ready", "gated", "turned", "copied", "out_done", "added", "act_own"))
        block = ctx.enter_context(nc.Block())

        @block.sync
        def _(sp):
            sp.dma_start(ident[:, :], a["ident"]).then_inc(loaded, 16)
            sp.dma_start(wg[:, :], a["Wg"]).then_inc(loaded, 16)
            sp.dma_start(wo[:, :, :], a["Wo"].rearrange("(k p) d -> p k d", p=P)).then_inc(loaded, 16)
            x_v = a["x"].rearrange("b (q p) d -> (b q) p d", p=P)
            with sp.Fori(0, TILES // 2) as r:
                for p in range(2):
                    i = r * 2 + p
                    sp.wait_ge(added[p], r)
                    sp.dma_start(x_t[p][:, :], s["xT"][:, bass.ds(i * P, P)]).then_inc(in_loaded[p], 16)
                    sp.dma_start(o_in[p][:, :], s["oo"][bass.ds(i * P, P), :]).then_inc(in_loaded[p], 16)
                    sp.dma_start(x_in[p][:, :], x_v[i]).then_inc(in_loaded[p], 16)

        @block.tensor
        def _(pe):
            pe.wait_ge(loaded, 48)
            with pe.Fori(0, TILES // 2) as r:
                for p in range(2):
                    pe.wait_ge(in_loaded[p], r * 48 + 48)
                    pe.wait_ge(z_ready[p], r)
                    pe.matmul(p_g[p][:, :], x_t[p][:, :], wg[:, :], start=True, stop=True).then_inc(gate_done[p], 1)
                for p in range(2):
                    pe.wait_ge(gated[p], r + 1)
                    pe.wait_ge(copied[p], r)
                    for k in range(KO):
                        last = pe.transpose(p_t[p][:, P * k:P * k + P], og[p][:, P * k:P * k + P], ident[:, :])
                    last.then_inc(turned[p], 1)
                for p in range(2):
                    pe.wait_ge(copied[p], r + 1)
                    pe.wait_ge(added[p], r)
                    for k in range(KO):
                        last = pe.matmul(p_a[p][:, 0:D], og_t[p][:, k, :], wo[:, k, :], start=k == 0, stop=k == KO - 1)
                    last.then_inc(out_done[p], 1)

        @block.scalar
        def _(act):
            with act.Fori(0, TILES // 2) as r:
                for p in range(2):
                    act.wait_ge(z_ready[p], r + 1)
                    act.activation(z[p][:, :], z[p][:, :], ACT.Exp).then_inc(act_own[p], 1)
                    act.wait_ge(act_own[p], r * 2 + 1)
                    act.activation(z[p][:, :], z[p][:, :], ACT.Ln, bias=1.0).then_inc(act_own[p], 1)
                    act.wait_ge(act_own[p], r * 2 + 2)
                    act.activation(z[p][:, :], z[p][:, :], ACT.Exp, scale=-1.0).then_inc(gate_ready[p], 1)
                for p in range(2):
                    act.wait_ge(turned[p], r + 1)
                    act.wait_ge(out_done[p], r)
                    act.activation(og_t[p][:, :, :].rearrange("p k t -> p (k t)"), p_t[p][:, :], ACT.Copy).then_inc(copied[p], 1)

        @block.vector
        def _(ve):
            with ve.Fori(0, TILES // 2) as r:
                for p in range(2):
                    ve.wait_ge(gate_done[p], r + 1)
                    ve.wait_ge(gated[p], r)
                    ve.tensor_scalar(z[p][:, :], p_g[p][:, :], -1.0, 40.0, ALU.mult, ALU.min).then_inc(z_ready[p], 1)
                for p in range(2):
                    ve.wait_ge(gate_ready[p], r + 1)
                    ve.wait_ge(in_loaded[p], r * 48 + 48)
                    ve.wait_ge(turned[p], r)
                    ve.tensor_tensor(og[p][:, :], o_in[p][:, :], z[p][:, :], ALU.mult).then_inc(gated[p], 1)
                for p in range(2):
                    ve.wait_ge(out_done[p], r + 1)
                    ve.tensor_tensor(w["rest"][:, bass.ds(r * 2 + p, 1), :].rearrange("p o d -> p (o d)"),
                                     x_in[p][:, :], p_a[p][:, 0:D], ALU.add).then_inc(added[p], 1)


def layer_norm(ve, own, act_done, requested, dst, src, stats, square, eps_turn):
    n = src.shape[1]
    mean, var, inv = stats

    def step(instruction):
        own.did(instruction)
        ve.wait_ge(own.sem, own.value())

    spread = lambda x: x.unsqueeze(2).broadcast_to([P, n, D])
    step(ve.tensor_reduce(mean, src, AX.X, ALU.add))
    step(ve.tensor_scalar(mean, mean, 1.0 / D, None, ALU.mult))
    step(ve.tensor_tensor(dst, src, spread(mean), ALU.subtract))
    step(ve.tensor_tensor(square, dst, dst, ALU.mult))
    step(ve.tensor_reduce(var, square, AX.X, ALU.add))
    ve.tensor_scalar(inv, var, 1.0 / D, LN_EPS, ALU.mult, ALU.add).then_inc(requested, 1)
    ve.wait_ge(act_done, eps_turn + 1)
    step(ve.tensor_tensor(dst, dst, spread(inv), ALU.mult))


def inverse_roots(act, own, requested, done, inv, turns):
    for k in range(turns):
        act.wait_ge(requested, k + 1)
        act.activation(inv, inv, ACT.Ln).then_inc(own, 1)
        act.wait_ge(own, k + 1)
        act.activation(inv, inv, ACT.Exp, scale=-0.5).then_inc(done, 1)


def norms(nc, a, s, w):
    with ExitStack() as ctx:
        def sb(name, shape):
            return ctx.enter_context(nc.sbuf_tensor("no_" + name, shape, F32))

        def sem(name):
            return signal(nc, s, "no_" + name)

        gain, bias, square = sb("gain", [P, D]), sb("bias", [P, D]), sb("square", [P, TILES, D])
        mean, var, inv = sb("mean", [P, TILES]), sb("var", [P, TILES]), sb("inv", [P, TILES])
        loaded, vec_own, act_own, requested, rooted, zero_ready, zeroed = (
            sem(x) for x in ("loaded", "vec_own", "act_own", "requested", "rooted", "zero_ready", "zeroed"))
        block = ctx.enter_context(nc.Block())
        x1, h = w["rest"][:, :, :], w["h"][:, :, :]

        @block.sync
        def _(sp):
            sp.dma_start(gain[:, :], a["ln_g"].partition_broadcast(P)).then_inc(loaded, 16)
            sp.dma_start(bias[:, :], a["ln_b"].partition_broadcast(P)).then_inc(loaded, 16)
            sp.wait_ge(zero_ready, 1)
            sp.dma_start(s["xe"].rearrange("(t p) d -> p t d", p=P), w["zeros"][:, :, :]).then_inc(zeroed, 16)
            sp.wait_ge(zeroed, 16)

        @block.gpsimd
        def _(po):
            po.memset(w["zeros"][:, :, :], 0.0).then_inc(zero_ready, 1)

        @block.scalar
        def _(act):
            inverse_roots(act, act_own, requested, rooted, inv[:, :], 2)

        @block.vector
        def _(ve):
            own = Tally(ve, vec_own)
            stats = (mean[:, :], var[:, :], inv[:, :])
            layer_norm(ve, own, rooted, requested, x1, x1, stats, square[:, :, :], 0)
            layer_norm(ve, own, rooted, requested, h, x1, stats, square[:, :, :], 1)
            ve.wait_ge(loaded, 32)
            own.did(ve.tensor_tensor(h, h, gain[:, :].unsqueeze(1).broadcast_to([P, TILES, D]), ALU.mult))
            ve.wait_ge(vec_own, own.value())
            own.did(ve.tensor_tensor(h, h, bias[:, :].unsqueeze(1).broadcast_to([P, TILES, D]), ALU.add))


def routing(nc, a, s, w):
    with ExitStack() as ctx:
        def sb(name, shape, dt=F32):
            return ctx.enter_context(nc.sbuf_tensor("ro_" + name, shape, dt))

        def ps(name, shape):
            return ctx.enter_context(nc.psum_tensor("ro_" + name, shape, F32))

        def sem(name):
            return signal(nc, s, "ro_" + name)

        def two(name):
            return [sem(name + "0"), sem(name + "1")]

        E8 = 8
        ident, before, lane = sb("ident", [P, P]), sb("before", [P, P]), sb("lane", [P, E8])
        ones = sb("ones", [P, P])
        wr = sb("wr", [P, E_R])
        h_s = [sb(f"h_s{p}", [P, D]) for p in range(2)]
        h_t = [sb(f"h_t{p}", [P, P]) for p in range(2)]
        logits = sb("logits", [P, TILES, E8])
        cand = sb("cand", [P, TILES, E8])
        picked = [sb(f"picked{c}", [P, TILES, E8]) for c in range(2)]
        total = [sb(f"total{c}", [P, TILES, E8]) for c in range(2)]
        running = [sb(f"running{c}", [P, E8, TILES]) for c in range(2)]
        place = sb("place", [P, TILES, E8])
        best = [sb(f"best{c}", [P, TILES]) for c in range(2)]
        expert = [sb(f"expert{c}", [P, TILES]) for c in range(2)]
        spot, keep, den, odds = sb("spot", [P, TILES]), sb("keep", [P, TILES]), sb("den", [P, TILES]), sb("odds", [P, TILES])
        p_t = [ps(f"p_t{p}", [P, 512]) for p in range(2)]
        p_l = [ps(f"p_l{p}", [P, 512]) for p in range(2)]
        p_c = [ps(f"p_c{c}", [P, 512]) for c in range(4)]
        loaded, setup = sem("loaded"), sem("setup")
        staged, turned, copied, scored, kept = (two(x) for x in ("staged", "turned", "copied", "scored", "kept"))
        vec_own, odds_asked, odds_ready, picked_ready, counted = (
            sem(x) for x in ("vec_own", "odds_asked", "odds_ready", "picked_ready", "counted"))
        block = ctx.enter_context(nc.Block())

        @block.sync
        def _(sp):
            for dst, src in ((ident, "ident"), (before, "before"), (lane, "lane"), (wr, "Wr")):
                sp.dma_start(dst[:, :], a[src]).then_inc(loaded, 16)

        @block.gpsimd
        def _(po):
            po.memset(ones[:, :], 1.0).then_inc(setup, 1)
            with po.Fori(0, TILES // 2) as r:
                for p in range(2):
                    po.wait_ge(turned[p], r)
                    po.tensor_copy(h_s[p][:, :], w["h"][:, bass.ds(r * 2 + p, 1), :].rearrange("p o d -> p (o d)")).then_inc(staged[p], 1)

        @block.tensor
        def _(pe):
            pe.wait_ge(loaded, 64)
            with pe.Fori(0, TILES // 2) as r:
                for p in range(2):
                    pe.wait_ge(staged[p], r + 1)
                    pe.wait_ge(copied[p], r)
                    pe.transpose(p_t[p][:, 0:P], h_s[p][:, :], ident[:, :]).then_inc(turned[p], 1)
                for p in range(2):
                    pe.wait_ge(copied[p], r + 1)
                    pe.wait_ge(kept[p], r)
                    pe.matmul(p_l[p][:, 0:E_R], h_t[p][:, :], wr[:, :], start=True, stop=True).then_inc(scored[p], 1)
            pe.wait_ge(setup, 1)
            for c in range(2):
                pe.wait_ge(picked_ready, c + 1)
                flat = picked[c][:, :, :].rearrange("p t e -> p (t e)")
                pe.matmul(p_c[2 * c][:, :], before[:, :], flat, start=True, stop=True)
                pe.matmul(p_c[2 * c + 1][:, :], ones[:, :], flat, start=True, stop=True).then_inc(counted, 1)

        @block.scalar
        def _(act):
            with act.Fori(0, TILES // 2) as r:
                for p in range(2):
                    act.wait_ge(turned[p], r + 1)
                    act.wait_ge(scored[p], r)
                    act.activation(w["hT"][:, bass.ds((r * 2 + p) * P, P)], p_t[p][:, 0:P], ACT.Copy)
                    act.activation(h_t[p][:, :], p_t[p][:, 0:P], ACT.Copy).then_inc(copied[p], 1)
            act.wait_ge(odds_asked, 1)
            act.activation(odds[:, :], odds[:, :], ACT.Exp).then_inc(odds_ready, 1)

        @block.vector
        def _(ve):
            own = Tally(ve, vec_own)

            def step(instruction):
                own.did(instruction)
                ve.wait_ge(vec_own, own.value())

            ve.wait_ge(loaded, 64)
            ve.wait_ge(setup, 1)
            step(ve.memset(logits[:, :, E_R:E8], -1e30))
            with ve.Fori(0, TILES // 2) as r:
                for p in range(2):
                    ve.wait_ge(scored[p], r + 1)
                    ve.tensor_copy(logits[:, bass.ds(r * 2 + p, 1), 0:E_R].rearrange("p o e -> p (o e)"), p_l[p][:, 0:E_R]).then_inc(kept[p], 1)
            for p in range(2):
                ve.wait_ge(kept[p], TILES // 2)
            per_tile = lambda x: x[:, :].unsqueeze(2).broadcast_to([P, TILES, E8])
            lanes = lane[:, :].unsqueeze(1).broadcast_to([P, TILES, E8])
            for c in range(2):
                step(ve.tensor_reduce(best[c][:, :], logits[:, :, :], AX.X, ALU.max))
                step(ve.tensor_tensor(cand[:, :, :], logits[:, :, :], per_tile(best[c]), ALU.is_lt))
                step(ve.scalar_tensor_tensor(cand[:, :, :], cand[:, :, :], float(E8), lanes, ALU.mult, ALU.add))
                step(ve.tensor_reduce(expert[c][:, :], cand[:, :, :], AX.X, ALU.min))
                ve.tensor_tensor(picked[c][:, :, :], lanes, per_tile(expert[c]), ALU.is_equal).then_inc(picked_ready, 1)
                ve.wait_ge(picked_ready, c + 1)
                if c == 0:
                    step(ve.scalar_tensor_tensor(logits[:, :, :], picked[0][:, :, :], -1e30, logits[:, :, :], ALU.mult, ALU.add))
            ve.tensor_tensor(odds[:, :], best[1][:, :], best[0][:, :], ALU.subtract).then_inc(odds_asked, 1)
            ve.wait_ge(odds_ready, 1)
            step(ve.tensor_scalar(den[:, :], odds[:, :], 1.0, None, ALU.add))
            step(ve.reciprocal(w["gate"][:, 0, :], den[:, :]))
            step(ve.tensor_tensor(w["gate"][:, 1, :], odds[:, :], w["gate"][:, 0, :], ALU.mult))
            for c in range(2):
                ve.wait_ge(counted, c + 1)
                step(ve.tensor_copy(total[c][:, :, :].rearrange("p t e -> p (t e)"), p_c[2 * c + 1][:, :]))
                for e in range(E8):
                    own.did(ve.tensor_tensor_scan(running[c][:, e, :], ones[:, 0:TILES], total[c][:, :, e], 0.0, ALU.mult, ALU.add))
                ve.wait_ge(vec_own, own.value())
                turned_back = running[c][:, :, :].rearrange("p e t -> p t e")
                step(ve.tensor_tensor(place[:, :, :], turned_back, total[c][:, :, :], ALU.subtract))
                step(ve.tensor_tensor(place[:, :, :], place[:, :, :], p_c[2 * c][:, :].rearrange("p (t e) -> p t e", e=E8), ALU.add))
                if c == 1:
                    step(ve.tensor_tensor(place[:, :, :], place[:, :, :],
                                          running[0][:, :, TILES - 1].unsqueeze(1).broadcast_to([P, TILES, E8]), ALU.add))
                step(ve.tensor_tensor(place[:, :, :], place[:, :, :], picked[c][:, :, :], ALU.mult))
                step(ve.tensor_reduce(spot[:, :], place[:, :, :], AX.X, ALU.add))
                step(ve.tensor_scalar(keep[:, :], spot[:, :], float(CAP), None, ALU.is_lt))
                step(ve.tensor_tensor(w["gate"][:, c, :], w["gate"][:, c, :], keep[:, :], ALU.mult))
                step(ve.scalar_tensor_tensor(spot[:, :], expert[c][:, :], float(CAPP), spot[:, :], ALU.mult, ALU.add))
                step(ve.tensor_scalar(keep[:, :], keep[:, :], -float(2 * ROWS), float(2 * ROWS), ALU.mult, ALU.add))
                step(ve.tensor_tensor(spot[:, :], spot[:, :], keep[:, :], ALU.add))
                step(ve.tensor_copy(w["slot"][:, :, c], spot[:, :]))


def dispatch(nc, a, s, w):
    with ExitStack() as ctx:
        def sem(name):
            return signal(nc, s, "di_" + name)

        h_s = [ctx.enter_context(nc.sbuf_tensor(f"di_h_s{p}", [P, D], F32)) for p in range(2)]
        ix = [ctx.enter_context(nc.sbuf_tensor(f"di_ix{p}", [P, 2], U32)) for p in range(2)]
        po_passed = sem("po_passed")
        staged, sent = ([sem(n + "0"), sem(n + "1")] for n in ("staged", "sent"))
        block = ctx.enter_context(nc.Block())

        @block.vector
        def _(ve):
            with ve.Fori(0, TILES // 2) as r:
                for p in range(2):
                    i = r * 2 + p
                    ve.wait_ge(sent[p], r * 32)
                    ve.tensor_copy(h_s[p][:, :], w["h"][:, bass.ds(i, 1), :].rearrange("p o d -> p (o d)")).then_inc(staged[p], 1)
                    ve.tensor_copy(ix[p][:, :], w["slot"][:, bass.ds(i, 1), :].rearrange("p o c -> p (o c)")).then_inc(staged[p], 1)

        @block.gpsimd
        def _(po):
            with po.Fori(0, TILES // 2) as r:
                for p in range(2):
                    po.wait_ge(staged[p], r * 2 + 2)
                    apart(po, po_passed)
                    for c in range(2):
                        po.indirect_dma_start(s["xe"][:, :], bass.IndirectOffsetOnAxis(ap=ix[p][:, c:c + 1], axis=0),
                                              h_s[p][:, :], None, bounds_check=ROWS - 1, oob_is_err=False).then_inc(sent[p], 16)
            for p in range(2):
                po.wait_ge(sent[p], 32 * (TILES // 2))


def experts(nc, a, s, w):
    with ExitStack() as ctx:
        def sb(name, shape):
            return ctx.enter_context(nc.sbuf_tensor("ex_" + name, shape, F32))

        def ps(name, shape):
            return ctx.enter_context(nc.psum_tensor("ex_" + name, shape, F32))

        def sem(name):
            return signal(nc, s, "ex_" + name)

        KF, RT = FF // P, CAPP // P
        ident = sb("ident", [P, P])
        w1, w3, w2 = sb("w1", [P, FF]), sb("w3", [P, FF]), sb("w2", [P, KF, D])
        x_e, x_t, y_e = sb("x_e", [P, RT, D]), sb("x_t", [P, CAPP]), sb("y_e", [P, RT, D])
        act_a, g_t = sb("act_a", [P, KF, CAPP]), sb("g_t", [P, KF, CAPP])
        p_t, p_y = ps("p_t", [P, 512]), ps("p_y", [P, 512])
        p_a = [ps(f"p_a{i}", [P, 512]) for i in range(2)]
        p_b = [ps(f"p_b{i}", [P, 512]) for i in range(2)]
        const_loaded, loaded, turned, copied, a_done, b_done, silu_done, g_done, y_done, y_copied, stored = (
            sem(x) for x in ("const_loaded", "loaded", "turned", "copied", "a_done", "b_done", "silu_done", "g_done",
                             "y_done", "y_copied", "stored"))
        block = ctx.enter_context(nc.Block())

        @block.sync
        def _(sp):
            sp.dma_start(ident[:, :], a["ident"]).then_inc(const_loaded, 16)
            x_v = s["xe"].rearrange("(e t p) d -> e p t d", p=P, t=RT)
            y_v = s["ye"].rearrange("(e t p) d -> e p t d", p=P, t=RT)
            with sp.Fori(0, E_R) as e:
                sp.wait_ge(y_done, e)
                sp.dma_start(x_e[:, :, :], x_v[e]).then_inc(loaded, 16)
                sp.dma_start(w1[:, :], a["W1"][e]).then_inc(loaded, 16)
                sp.dma_start(w3[:, :], a["W3"][e]).then_inc(loaded, 16)
                sp.dma_start(w2[:, :, :], a["W2"].rearrange("e (k p) d -> e p k d", p=P)[e]).then_inc(loaded, 16)
                sp.wait_ge(y_copied, e + 1)
                sp.dma_start(y_v[e], y_e[:, :, :]).then_inc(stored, 16)
            sp.wait_ge(stored, 16 * E_R)

        @block.tensor
        def _(pe):
            pe.wait_ge(const_loaded, 16)
            with pe.Fori(0, E_R) as e:
                pe.wait_ge(loaded, e * 64 + 64)
                for t in range(RT):
                    last = pe.transpose(p_t[:, P * t:P * t + P], x_e[:, t, :], ident[:, :])
                last.then_inc(turned, 1)
                pe.wait_ge(copied, e + 1)
                for k in range(KF):
                    if k < 2:
                        pe.wait_ge(g_done, e * KF)
                    else:
                        pe.wait_ge(g_done, e * KF + k - 1)
                    pe.matmul(p_a[k % 2][:, 0:CAPP], w1[:, P * k:P * k + P], x_t[:, :], start=True, stop=True).then_inc(a_done, 1)
                    pe.matmul(p_b[k % 2][:, 0:CAPP], w3[:, P * k:P * k + P], x_t[:, :], start=True, stop=True).then_inc(b_done, 1)
                pe.wait_ge(g_done, e * KF + KF)
                pe.wait_ge(y_copied, e)
                for t in range(RT):
                    for k in range(KF):
                        last = pe.matmul(p_y[:, P * t:P * t + P], g_t[:, k, P * t:P * t + P], w2[:, k, :],
                                         start=k == 0, stop=k == KF - 1)
                last.then_inc(y_done, 1)

        @block.scalar
        def _(act):
            with act.Fori(0, E_R) as e:
                act.wait_ge(turned, e + 1)
                act.activation(x_t[:, :], p_t[:, 0:CAPP], ACT.Copy).then_inc(copied, 1)
                for k in range(KF):
                    act.wait_ge(a_done, e * KF + k + 1)
                    act.wait_ge(g_done, e * KF)
                    act.activation(act_a[:, k, :], p_a[k % 2][:, 0:CAPP], ACT.Silu).then_inc(silu_done, 1)
                act.wait_ge(y_done, e + 1)
                act.wait_ge(stored, e * 16)
                act.activation(y_e[:, :, :].rearrange("p t d -> p (t d)"), p_y[:, 0:CAPP], ACT.Copy).then_inc(y_copied, 1)

        @block.vector
        def _(ve):
            with ve.Fori(0, E_R) as e:
                for k in range(KF):
                    ve.wait_ge(silu_done, e * KF + k + 1)
                    ve.wait_ge(b_done, e * KF + k + 1)
                    ve.wait_ge(y_done, e)
                    ve.tensor_tensor(g_t[:, k, :], act_a[:, k, :], p_b[k % 2][:, 0:CAPP], ALU.mult).then_inc(g_done, 1)


def shared_and_sum(nc, a, s, w):
    with ExitStack() as ctx:
        def sb(name, shape, dt=F32):
            return ctx.enter_context(nc.sbuf_tensor("sh_" + name, shape, dt))

        def ps(name, shape):
            return ctx.enter_context(nc.psum_tensor("sh_" + name, shape, F32))

        def sem(name):
            return signal(nc, s, "sh_" + name)

        KF, Q4 = FF // P, 4
        GROUPS = TILES // Q4
        w1, w3, w2 = sb("w1", [P, FF]), sb("w3", [P, FF]), sb("w2", [P, KF, D])
        act_a, g_t = sb("act_a", [P, KF, Q4 * P]), sb("g_t", [P, KF, Q4 * P])
        ix = [[sb(f"ix{q}{c}", [P, 1], U32) for c in range(2)] for q in range(Q4)]
        rows = [[sb(f"rows{q}{c}", [P, D]) for c in range(2)] for q in range(Q4)]
        p_y = [ps(f"p_y{i}", [P, 512]) for i in range(2)]
        p_a = [ps(f"p_a{i}", [P, 512]) for i in range(2)]
        p_b = [ps(f"p_b{i}", [P, 512]) for i in range(2)]
        loaded, a_done, b_done, silu_done, g_done, y_done = (
            sem(x) for x in ("loaded", "a_done", "b_done", "silu_done", "g_done", "y_done"))
        cleared, staged, gathered, summed, vec_own, po_passed = (
            sem(x) for x in ("cleared", "staged", "gathered", "summed", "vec_own", "po_passed"))
        block = ctx.enter_context(nc.Block())

        @block.sync
        def _(sp):
            sp.dma_start(w1[:, :], a["W1s"]).then_inc(loaded, 16)
            sp.dma_start(w3[:, :], a["W3s"]).then_inc(loaded, 16)
            sp.dma_start(w2[:, :, :], a["W2s"].rearrange("(k p) d -> p k d", p=P)).then_inc(loaded, 16)

        @block.gpsimd
        def _(po):
            po.wait_ge(cleared, 2 * Q4)
            with po.Fori(0, GROUPS) as i:
                po.wait_ge(summed, i)
                po.wait_ge(staged, i * 2 * Q4 + 2 * Q4)
                apart(po, po_passed)
                for q in range(Q4):
                    for c in range(2):
                        po.indirect_dma_start(rows[q][c][:, :], None, s["ye"][:, :],
                                              bass.IndirectOffsetOnAxis(ap=ix[q][c][:, :], axis=0),
                                              bounds_check=ROWS - 1, oob_is_err=False).then_inc(gathered, 16)

        @block.tensor
        def _(pe):
            pe.wait_ge(loaded, 48)
            with pe.Fori(0, GROUPS) as i:
                h_t = w["hT"][:, bass.ds(i * (Q4 * P), Q4 * P)]
                for k in range(KF):
                    if k < 2:
                        pe.wait_ge(g_done, i * KF)
                    else:
                        pe.wait_ge(g_done, i * KF + k - 1)
                    pe.matmul(p_a[k % 2][:, :], w1[:, P * k:P * k + P], h_t, start=True, stop=True).then_inc(a_done, 1)
                    pe.matmul(p_b[k % 2][:, :], w3[:, P * k:P * k + P], h_t, start=True, stop=True).then_inc(b_done, 1)
                pe.wait_ge(g_done, i * KF + KF)
                pe.wait_ge(summed, i)
                for t in range(Q4):
                    for k in range(KF):
                        last = pe.matmul(p_y[0][:, P * t:P * t + P], g_t[:, k, P * t:P * t + P], w2[:, k, :],
                                         start=k == 0, stop=k == KF - 1)
                last.then_inc(y_done, 1)

        @block.scalar
        def _(act):
            with act.Fori(0, GROUPS) as i:
                for k in range(KF):
                    act.wait_ge(a_done, i * KF + k + 1)
                    act.wait_ge(g_done, i * KF)
                    act.activation(act_a[:, k, :], p_a[k % 2][:, :], ACT.Silu).then_inc(silu_done, 1)

        @block.vector
        def _(ve):
            for q in range(Q4):
                for c in range(2):
                    ve.memset(rows[q][c][:, :], 0.0).then_inc(cleared, 1)
            PER = 2 * Q4 + 1
            with ve.Fori(0, GROUPS) as i:
                own = Tally(ve, vec_own, i * PER)
                ve.wait_ge(gathered, i * (32 * Q4))
                for q in range(Q4):
                    for c in range(2):
                        ve.tensor_copy(ix[q][c][:, :], w["slot"][:, bass.ds(i * Q4 + q, 1), c]).then_inc(staged, 1)
                for k in range(KF):
                    ve.wait_ge(silu_done, i * KF + k + 1)
                    ve.wait_ge(b_done, i * KF + k + 1)
                    ve.wait_ge(y_done, i)
                    ve.tensor_tensor(g_t[:, k, :], act_a[:, k, :], p_b[k % 2][:, :], ALU.mult).then_inc(g_done, 1)
                ve.wait_ge(y_done, i + 1)
                part = w["rest"][:, bass.ds(i * Q4, Q4), :]
                own.did(ve.tensor_tensor(part, part, p_y[0][:, :].rearrange("p (t d) -> p t d", t=Q4), ALU.add))
                ve.wait_ge(vec_own, own.value())
                ve.wait_ge(gathered, i * (32 * Q4) + 32 * Q4)
                for c in range(2):
                    for q in range(Q4):
                        one = w["rest"][:, bass.ds(i * Q4 + q, 1), :].rearrange("p o d -> p (o d)")
                        own.did(ve.scalar_tensor_tensor(one, rows[q][c][:, :], w["gate"][:, c, bass.ds(i * Q4 + q, 1)],
                                                        one, ALU.mult, ALU.add))
                    ve.wait_ge(vec_own, own.value())
                ve.memset(ix[0][0][:, :], 0).then_inc(summed, 1)
                ve.wait_ge(summed, i + 1)
                assert own.n == PER


def last_norm(nc, a, s, w, out):
    with ExitStack() as ctx:
        def sb(name, shape):
            return ctx.enter_context(nc.sbuf_tensor("ln_" + name, shape, F32))

        def sem(name):
            return signal(nc, s, "ln_" + name)

        square = sb("square", [P, TILES, D])
        mean, var, inv = sb("mean", [P, TILES]), sb("var", [P, TILES]), sb("inv", [P, TILES])
        vec_own, act_own, requested, rooted, stored = (sem(x) for x in ("vec_own", "act_own", "requested", "rooted", "stored"))
        block = ctx.enter_context(nc.Block())
        STEPS = 6

        @block.scalar
        def _(act):
            inverse_roots(act, act_own, requested, rooted, inv[:, :], 1)

        @block.vector
        def _(ve):
            own = Tally(ve, vec_own)
            layer_norm(ve, own, rooted, requested, w["rest"][:, :, :], w["rest"][:, :, :],
                       (mean[:, :], var[:, :], inv[:, :]), square[:, :, :], 0)
            assert own.n == STEPS, own.n

        @block.sync
        def _(sp):
            sp.wait_ge(vec_own, STEPS)
            sp.dma_start(out.rearrange("b (q p) d -> p (b q) d", p=P), w["rest"][:, :, :]).then_inc(stored, 16)
            sp.wait_ge(stored, 16)


def apart(eng, passed):
    eng.sem_inc(passed, 1)


def signal(nc, s, name):
    s["signals"].append(nc.alloc_semaphore(name=name))
    return s["signals"][-1]


def phase(nc, a, s, body, *more):
    s["signals"] = []
    body(nc, a, s, *more)
    nc.clear_and_free_semaphores(s["signals"])
    nc.all_engine_barrier()


def build(nc, a, s, out, stop=9, start=0):
    if start < 1:
        phase(nc, a, s, token_scalars)
        phase(nc, a, s, rotary_tables)
    if stop > 1 and start < 2:
        phase(nc, a, s, within_chunks)
    if stop > 2 and start < 3:
        phase(nc, a, s, across_chunks)
    if stop > 3:
        with ExitStack() as ctx:
            def sb(name, shape, dt=F32):
                return ctx.enter_context(nc.sbuf_tensor(name, shape, dt))

            w = {"rest": sb("rest", [P, TILES, D]), "h": sb("h", [P, TILES, D]),
                 "gate": sb("gate", [P, 2, TILES]), "slot": sb("slot", [P, TILES, 2], U32)}
            with nc.sbuf_tensor("zeros", [P, ROWS // P, D], F32) as zeros:
                w["zeros"] = zeros
                phase(nc, a, s, after_attention, w)
                phase(nc, a, s, norms, w)
            w["hT"] = sb("hT", [P, N_TOK])
            phase(nc, a, s, routing, w)
            phase(nc, a, s, dispatch, w)
            phase(nc, a, s, experts, w)
            phase(nc, a, s, shared_and_sum, w)
            phase(nc, a, s, last_norm, w, out)


_INS = ["L0_attn_" + n for n in ("hidden_states", "Wq", "Wk", "Wv", "Wbeta", "Wtg", "mode_logits", "log_decay",
                                 "omega_log_scale", "Wg", "Wo")] + \
       ["L0_ffn_" + n for n in ("ln_g", "ln_b", "Wr", "W1", "W3", "W2", "W1s", "W3s", "W2s")]


def kernel(**inputs):
    import numpy as _np
    import concourse.bacc as _bacc
    from concourse import mybir as _mybir
    from concourse.bass_utils import run_bass_kernel_spmd as _run

    nc = _bacc.Bacc("TRN2", target_bir_lowering=False, num_devices=1)
    arrays, args = {}, {}
    named = {n.split("_", 2)[2]: _np.ascontiguousarray(inputs[n]) for n in _INS}
    named["x"] = named.pop("hidden_states")
    named.update(constants())
    for name, value in named.items():
        arrays[f"in_{name}_dram"] = value
        args[name] = nc.dram_tensor(f"in_{name}_dram", value.shape, _mybir.dt.from_np(value.dtype), kind="ExternalInput").ap()
    out = nc.dram_tensor("out_0_dram", (B, T, D), F32, kind="ExternalOutput").ap()
    build(nc, args, scratch(nc), out)
    r = _run(nc, [arrays], core_ids=[0])
    return r.results[0]["out_0_dram"]
```

```python
from contextlib import ExitStack

import numpy as np

import concourse.bass as bass
from concourse import mybir

F32 = mybir.dt.float32
U32 = mybir.dt.uint32
ALU = mybir.AluOpType
ACT = mybir.ActivationFunctionType
AX = mybir.AxisListType

B, T, D = 16, 512, 128
H, DK, M = 8, 64, 8
N_TOK = B * T
P = 128
C = 32
NCH = T // C
LO = P // C
HI = M // LO
HP = H * HI
GB = P // HP
NG = B // GB
TILES = N_TOK // P
FF, E_R, CAP = 512, 7, 366
CAPP = 3 * P
ROWS = E_R * CAPP
HALF = DK // 2
LN_EPS = 1e-5
MASKED = -1e4
MAGIC = 12582912.0
TWO_PI_A, TWO_PI_B = 6.28125, 0.0019350051879882812
TWO_PI_C = float(2 * np.pi - TWO_PI_A - TWO_PI_B)
PI_SAFE = 3.1415925


class Tally:

    def __init__(self, eng, sem, base=0):
        self.eng, self.sem, self.base, self.n = eng, sem, base, 0

    def did(self, instruction):
        instruction.then_inc(self.sem, 1)
        self.n += 1

    def value(self):
        return self.base + self.n


def constants():
    p = np.arange(P)
    f = np.float32
    return {
        "ident": np.eye(P, dtype=f),
        "fold": (p[:, None] % C == np.arange(C)[None]).astype(f),
        "pick": (p[:, None] % HI == p[None] // DK).astype(f),
        "own": (p[:, None] // HI == np.arange(P // HI)[None]).astype(f),
        "causal": np.broadcast_to(np.where(np.arange(C)[None] <= np.arange(C)[:, None], 0, MASKED)
                                  .astype(f).reshape(1, C * C), (P, C * C)).copy(),
        "pos": (C * np.arange(NCH)[None] + p[:, None] % C).astype(f),
        "freq": np.broadcast_to((f(1.0) / f(10000.0) ** (np.arange(0, DK, 2, dtype=f) / f(DK)))
                                .astype(f)[None], (P, HALF)).copy(),
        "before": (p[:, None] < p[None]).astype(f),
        "lane": np.broadcast_to(np.arange(8, dtype=f)[None], (P, 8)).copy(),
    }


def scratch(nc):
    def dram(name, shape):
        return nc.dram_tensor(name, shape, F32, kind="Internal").ap()

    return {
        "scal": dram("scal", (4, B, H * M, T)),
        "tab": dram("tab", (NCH, P, 2 * HP * HALF)),
        "kd": dram("kd", (NG * NCH * GB, P, HP * DK)),
        "qd": dram("qd", (NG * NCH * GB, P, 2 * H * LO * C)),
        "od": dram("od", (NG * NCH, P, GB * HP * 2 * C)),
        "gd": dram("gd", (NG * NCH, P, GB * 3 * HP)),
        "sd": dram("sd", (NG * NCH, P, GB * H * LO)),
        "oo": dram("oo", (N_TOK, H * DK)),
        "xT": dram("xT", (D, N_TOK)),
        "xe": dram("xe", (ROWS, D)),
        "ye": dram("ye", (ROWS, D)),
    }


def token_scalars(nc, a, s):
    with ExitStack() as ctx:
        def sb(name, shape):
            return ctx.enter_context(nc.sbuf_tensor("ts_" + name, shape, F32))

        def ps(name, shape):
            return ctx.enter_context(nc.psum_tensor("ts_" + name, shape, F32))

        def sem(name):
            return signal(nc, s, "ts_" + name)

        def two(name):
            return [sem(name + "0"), sem(name + "1")]

        assert NCH == B
        Q = T // P
        HM, NA = H * M, HP * HALF
        ident = sb("ident", [P, P])
        wq, wk, wz = sb("wq", [P, H * DK]), sb("wk", [P, H * DK]), sb("wz", [P, 2 * HM])
        decay, modes = sb("decay", [P, HM]), sb("modes", [P, HM])
        row_a, row_b, row_h = sb("row_a", [P, HM]), sb("row_b", [P, HM]), sb("row_h", [P, H])
        ln_rho, ln_w = sb("ln_rho", [P, HM]), sb("ln_w", [P, HM])
        x_in, x_t = sb("x_in", [P, Q, D]), sb("x_t", [P, Q * P])
        sq = [sb(f"sq{p}", [P, 2, H * DK]) for p in range(2)]
        ss, ln_s = sb("ss", [P, Q, 2 * H]), sb("ln_s", [P, Q, 2 * H])
        zz, ez, nl = (sb(x, [P, Q, 2 * HM]) for x in ("zz", "ez", "nl"))
        v, v_t = sb("v", [P, Q, 4, HM]), sb("v_t", [P, 2, T])
        p_x, p_z = ps("p_x", [P, 512]), ps("p_z", [P, 512])
        p_q, p_k, p_v = ([ps(f"{n}{p}", [P, 512]) for p in range(2)] for n in ("p_q", "p_k", "p_v"))
        om, pos, freq = sb("om", [P, HP]), sb("pos", [P, NCH]), sb("freq", [P, HALF])
        at, r = sb("at", [P, HP]), sb("r", [P, 2 * NA])
        ang, turns = [sb(f"ang{p}", [P, NA]) for p in range(2)], [sb(f"turns{p}", [P, 2 * NA]) for p in range(2)]
        tables = sb("tables", [P, NCH, 2 * NA])

        loaded, mode_ready, mode_exp = sem("loaded"), sem("mode_ready"), sem("mode_exp")
        x_loaded, x_turned, x_copied, xt_stored = (sem(x) for x in ("x_loaded", "x_turned", "x_copied", "xt_stored"))
        projected, squared, summed = two("projected"), two("squared"), two("summed")
        z_done, z_taken, sums_ready = sem("z_done"), sem("z_taken"), sem("sums_ready")
        logged, valued, v_turned, v_copied, v_stored = (
            sem(x) for x in ("logged", "valued", "v_turned", "v_copied", "v_stored"))
        act_own, vec_own, pool_own, po_passed = (sem(x) for x in ("act_own", "vec_own", "pool_own", "po_passed"))
        pos_loaded, omega_ready, sines, tab_stored, tab_own = (
            sem(x) for x in ("pos_loaded", "omega_ready", "sines", "tab_stored", "tab_own"))
        counted, reduced = two("counted"), two("reduced")
        block = ctx.enter_context(nc.Block())

        def groups(eng, body):
            body(0, False, True)
            with eng.Fori(1, B - 1) as i:
                body(i, True, True)
            body(B - 1, True, False)

        @block.sync
        def _(sp):
            sp.dma_start(ident[:, :], a["ident"]).then_inc(loaded, 16)
            x_v = a["x"].rearrange("b (q p) d -> b p q d", p=P)
            sp.dma_start(x_in[:, :, :], x_v[0]).then_inc(x_loaded, 16)
            for dst, src in ((wq[:, :], a["Wq"]), (wk[:, :], a["Wk"]),
                             (wz[:, 0:HM], a["Wtg"]), (wz[:, HM:], a["Wbeta"]),
                             (decay[:, :], a["log_decay"].rearrange("h m -> (h m)").partition_broadcast(P)),
                             (modes[:, :], a["mode_logits"].rearrange("h m -> (h m)").partition_broadcast(P))):
                sp.dma_start(dst, src).then_inc(loaded, 16)
            logs = a["omega_log_scale"].rearrange("h (i l) -> h i l", i=HI)
            for lo in range(LO):
                sp.dma_start(om[C * lo:C * lo + C, :],
                             logs[:, :, lo].rearrange("h i -> (h i)").partition_broadcast(C), allow_slow_non_contiguous=True).then_inc(pos_loaded, 16)
            sp.dma_start(pos[:, :], a["pos"]).then_inc(pos_loaded, 16)
            sp.dma_start(freq[:, :], a["freq"]).then_inc(pos_loaded, 16)

            def store_scalars(b):
                sp.wait_ge(v_copied, b + 1)
                for k in range(4):
                    sp.dma_start(s["scal"][k, b], v_t[HM * (k % 2):HM * (k % 2) + HM, k // 2, :]).then_inc(v_stored, 16)

            def group(i, before, after):
                if after:
                    sp.wait_ge(x_turned, i + 1)
                    sp.dma_start(x_in[:, :, :], x_v[i + 1]).then_inc(x_loaded, 16)
                sp.wait_ge(x_copied, i + 1)
                sp.dma_start(s["xT"][:, bass.ds(i * T, T)], x_t[:, :]).then_inc(xt_stored, 16)
                if before:
                    store_scalars(i - 1)

            groups(sp, group)
            store_scalars(B - 1)
            with sp.Fori(0, NCH) as j:
                sp.wait_ge(sines, j + 1)
                sp.dma_start(s["tab"][j], tables[:, bass.ds(j, 1), :].rearrange("p o x -> p (o x)")).then_inc(tab_stored, 16)
            sp.wait_ge(v_stored, 64 * B)
            sp.wait_ge(xt_stored, 16 * B)
            sp.wait_ge(tab_stored, 16 * NCH)

        @block.tensor
        def _(pe):
            pe.wait_ge(loaded, 16 * 7)

            def turn_x(i):
                pe.wait_ge(x_loaded, i * 16 + 16)
                pe.wait_ge(x_copied, i)
                for t in range(Q):
                    last = pe.transpose(p_x[:, P * t:P * t + P], x_in[:, t, :], ident[:, :])
                last.then_inc(x_turned, 1)

            def turn_scalars(i):
                pe.wait_ge(valued, i + 1)
                pe.wait_ge(v_copied, i)
                for k in range(2):
                    for t in range(Q):
                        last = pe.transpose(p_v[k][:, P * t:P * t + P], v[:, t, 2 * k:2 * k + 2, :].rearrange("p k m -> p (k m)"), ident[:, :])
                last.then_inc(v_turned, 1)

            def group(i, before, after):
                pe.wait_ge(x_copied, i + 1)
                for t in range(Q):
                    p = t % 2
                    pe.wait_ge(squared[p], i * (Q // 2) + t // 2)
                    x = x_t[:, P * t:P * t + P]
                    pe.matmul(p_q[p][:, :], x, wq[:, :], start=True, stop=True)
                    pe.matmul(p_k[p][:, :], x, wk[:, :], start=True, stop=True).then_inc(projected[p], 1)
                pe.wait_ge(z_taken, i)
                for t in range(Q):
                    last = pe.matmul(p_z[:, P * t:P * t + P], x_t[:, P * t:P * t + P], wz[:, :], start=True, stop=True)
                last.then_inc(z_done, 1)
                if after:
                    turn_x(i + 1)
                if before:
                    turn_scalars(i - 1)

            turn_x(0)
            groups(pe, group)
            turn_scalars(B - 1)

        @block.scalar
        def _(act):
            act.wait_ge(pos_loaded, 16 * 6)
            act.activation(om[:, :], om[:, :], ACT.Exp).then_inc(omega_ready, 1)
            act.wait_ge(loaded, 16 * 7)
            act.activation(row_a[:, :], decay[:, :], ACT.Exp).then_inc(act_own, 1)
            act.wait_ge(act_own, 1)
            act.activation(ln_rho[:, :], row_a[:, :], ACT.Ln, bias=1.0).then_inc(mode_exp, 1)
            act.wait_ge(mode_ready, 1)
            act.activation(row_b[:, :], modes[:, :], ACT.Exp).then_inc(mode_exp, 1)
            act.wait_ge(mode_ready, 2)
            act.activation(ln_w[:, :], row_a[:, :], ACT.Ln).then_inc(mode_exp, 1)

            def logarithms(i):
                act.wait_ge(sums_ready, i + 1)
                act.wait_ge(valued, i)
                act.activation(ez[:, :, :], zz[:, :, :], ACT.Exp).then_inc(act_own, 1)
                act.activation(ln_s[:, :, :], ss[:, :, :], ACT.Ln)
                act.wait_ge(act_own, i + 2)
                act.activation(nl[:, :, :], ez[:, :, :], ACT.Ln, bias=1.0).then_inc(logged, 1)

            def copy_scalars(i):
                act.wait_ge(v_turned, i + 1)
                act.wait_ge(v_stored, i * 64)
                for k in range(2):
                    last = act.activation(v_t[:, k, :], p_v[k][:, :], ACT.Copy)
                last.then_inc(v_copied, 1)

            def group(i, before, after):
                act.wait_ge(x_turned, i + 1)
                act.wait_ge(z_done, i)
                act.wait_ge(xt_stored, i * 16)
                act.activation(x_t[:, :], p_x[:, :], ACT.Copy).then_inc(x_copied, 1)
                if before:
                    logarithms(i - 1)
                for t in range(Q):
                    p = t % 2
                    act.wait_ge(projected[p], i * (Q // 2) + t // 2 + 1)
                    act.wait_ge(summed[p], i * (Q // 2) + t // 2)
                    act.activation(sq[p][:, 0, :], p_q[p][:, :], ACT.Square)
                    act.activation(sq[p][:, 1, :], p_k[p][:, :], ACT.Square).then_inc(squared[p], 1)
                if before:
                    copy_scalars(i - 1)

            groups(act, group)
            logarithms(B - 1)
            copy_scalars(B - 1)
            for p in range(2):
                act.wait_ge(reduced[p], NCH // 2)
            with act.Fori(0, NCH) as j:
                row = tables[:, bass.ds(j, 1), :]
                act.activation(row, row, ACT.Sin).then_inc(sines, 1)

        @block.vector
        def _(ve):
            own = Tally(ve, vec_own)
            ve.wait_ge(loaded, 16 * 7)
            m3 = modes[:, :].rearrange("p (h m) -> p h m", h=H)
            own.did(ve.tensor_reduce(row_h[:, :], m3, AX.X, ALU.max))
            ve.wait_ge(vec_own, own.value())
            ve.tensor_tensor(m3, m3, row_h[:, :].unsqueeze(2).broadcast_to([P, H, M]), ALU.subtract).then_inc(mode_ready, 1)
            ve.wait_ge(mode_exp, 2)
            b3 = row_b[:, :].rearrange("p (h m) -> p h m", h=H)
            own.did(ve.tensor_reduce(row_h[:, :], b3, AX.X, ALU.add))
            ve.wait_ge(vec_own, own.value())
            own.did(ve.reciprocal(row_h[:, :], row_h[:, :]))
            ve.wait_ge(vec_own, own.value())
            own.did(ve.tensor_tensor(b3, b3, row_h[:, :].unsqueeze(2).broadcast_to([P, H, M]), ALU.mult))
            ve.wait_ge(vec_own, own.value())
            ve.tensor_scalar(row_a[:, :], row_b[:, :], DK ** -0.5, 1e-18, ALU.mult, ALU.max).then_inc(mode_ready, 1)
            ve.wait_ge(mode_exp, 3)
            setup = own.value()
            VALUES, REDUCE = 5, 4
            split = lambda x: x.rearrange("p t (h m) -> p t h m", h=H)
            per_mode = lambda x: x.unsqueeze(3).broadcast_to([P, Q, H, M])

            def values(i, base):
                own = Tally(ve, vec_own, base)
                ve.wait_ge(logged, i + 1)
                ve.wait_ge(v_turned, i)
                own.did(ve.tensor_tensor(v[:, :, 0, :], nl[:, :, 0:HM], ln_rho[:, :].unsqueeze(1).broadcast_to([P, Q, HM]), ALU.add))
                own.did(ve.tensor_scalar(split(v[:, :, 2, :]), per_mode(ln_s[:, :, H:2 * H]), -0.5, None, ALU.mult))
                own.did(ve.tensor_scalar(split(v[:, :, 3, :]), per_mode(ln_s[:, :, 0:H]), -0.5, None, ALU.mult))
                ve.wait_ge(vec_own, own.value())
                own.did(ve.tensor_scalar(v[:, :, 0, :], v[:, :, 0, :], -1.0, float(np.log(1e-6)), ALU.mult, ALU.max))
                own.did(ve.tensor_tensor(v[:, :, 1, :], v[:, :, 2, :], nl[:, :, HM:], ALU.subtract))
                ve.tensor_tensor(v[:, :, 3, :], v[:, :, 3, :], ln_w[:, :].unsqueeze(1).broadcast_to([P, Q, HM]), ALU.add).then_inc(valued, 1)
                assert own.n == VALUES

            def group(i, before, after):
                if before:
                    values(i - 1, setup + (i - 1) * VALUES)
                for t in range(Q):
                    p = t % 2
                    ve.wait_ge(squared[p], i * (Q // 2) + t // 2 + 1)
                    if t == 0:
                        ve.wait_ge(logged, i)
                    ve.tensor_reduce(ss[:, t, :], sq[p][:, :, :].rearrange("p x (h d) -> p (x h) d", d=DK),
                                     AX.X, ALU.add).then_inc(summed[p], 1)
                ve.wait_ge(z_done, i + 1)
                ve.tensor_scalar(zz[:, :, :].rearrange("p t z -> p (t z)"), p_z[:, :], -1.0, 40.0, ALU.mult, ALU.min).then_inc(z_taken, 1)
                for p in range(2):
                    ve.wait_ge(summed[p], i * (Q // 2) + Q // 2)
                ve.tensor_scalar(ss[:, :, :], ss[:, :, :], 1e-6, None, ALU.add).then_inc(sums_ready, 1)

            def reduce_angles(half, p):
                own = Tally(ve, tab_own, (half * 2 + p) * REDUCE)

                def step(instruction):
                    own.did(instruction)
                    ve.wait_ge(tab_own, own.value())

                ve.wait_ge(counted[p], half + 1)
                r3, n3 = (x[:, :].rearrange("p (c f) -> p c f", c=2) for x in (r, turns[p]))
                step(ve.scalar_tensor_tensor(r3, n3, -TWO_PI_A, ang[p][:, :].unsqueeze(1).broadcast_to([P, 2, NA]),
                                             ALU.mult, ALU.add))
                step(ve.scalar_tensor_tensor(r[:, :], turns[p][:, :], -TWO_PI_B, r[:, :], ALU.mult, ALU.add))
                step(ve.scalar_tensor_tensor(r[:, :], turns[p][:, :], -TWO_PI_C, r[:, :], ALU.mult, ALU.add))
                step(ve.tensor_scalar(r[:, 0:NA], r[:, 0:NA], float(np.pi / 2), None, ALU.add))
                ve.tensor_scalar(tables[:, bass.ds(half * 2 + p, 1), :].rearrange("p o x -> p (o x)"), r[:, :],
                                 PI_SAFE, -PI_SAFE, ALU.min, ALU.max).then_inc(reduced[p], 1)
                assert own.n == REDUCE, own.n

            group(0, False, True)
            reduce_angles(0, 0)
            with ve.Fori(0, B // 2 - 1) as half:
                for p in range(2):
                    group(half * 2 + p + 1, True, True)
                    reduce_angles(half + p, 1 - p)
            group(B - 1, True, False)
            reduce_angles(NCH // 2 - 1, 1)
            values(B - 1, setup + (B - 1) * VALUES)

        @block.gpsimd
        def _(po):
            po.wait_ge(omega_ready, 1)
            po.wait_ge(pos_loaded, 16 * 6)
            PER = 5
            with po.Fori(0, NCH // 2) as half:
                for p in range(2):
                    own = Tally(po, pool_own, (half * 2 + p) * PER)

                    def step(instruction):
                        own.did(instruction)
                        po.wait_ge(pool_own, own.value())
                        apart(po, po_passed)

                    step(po.tensor_tensor(at[:, :], om[:, :], pos[:, bass.ds(half * 2 + p, 1)].broadcast_to([P, HP]), ALU.mult))
                    po.wait_ge(reduced[p], half)
                    step(po.tensor_tensor(ang[p][:, :].rearrange("p (m f) -> p m f", f=HALF),
                                          at[:, :].unsqueeze(2).broadcast_to([P, HP, HALF]),
                                          freq[:, :].unsqueeze(1).broadcast_to([P, HP, HALF]), ALU.mult))
                    own.did(po.tensor_scalar(turns[p][:, 0:NA], ang[p][:, :], 1 / (2 * np.pi), 0.25, ALU.mult, ALU.add))
                    step(po.tensor_scalar(turns[p][:, NA:], ang[p][:, :], 1 / (2 * np.pi), None, ALU.mult))
                    step(po.tensor_scalar(turns[p][:, :], turns[p][:, :], MAGIC, None, ALU.add))
                    po.tensor_scalar(turns[p][:, :], turns[p][:, :], MAGIC, None, ALU.subtract).then_inc(counted[p], 1)
                    assert own.n == PER, own.n


def sooner(pair, p, r):
    return (pair[1], r) if p == 0 else (pair[0], r + 1)


def within_chunks(nc, a, s):
    with ExitStack() as ctx:
        def sb(name, shape):
            return ctx.enter_context(nc.sbuf_tensor("wc_" + name, shape, F32))

        def ps(name, shape):
            return ctx.enter_context(nc.psum_tensor("wc_" + name, shape, F32))

        def sem(name):
            return signal(nc, s, "wc_" + name)

        def two(name):
            return [sem(name + "0"), sem(name + "1")]

        ident, own_bh, pick = sb("ident", [P, P]), sb("own_bh", [P, P // HI]), sb("pick", [P, P])
        causal = sb("causal", [P, C, C])
        wq, wk = sb("wq", [P, H * DK]), sb("wk", [P, H * DK])
        tab = sb("tab", [P, 2, H, HI, HALF])
        x_r = [sb(f"x_r{p}", [P, LO, C]) for p in range(2)]
        q_s = sb("q_s", [P, H, 2, HALF])
        k_rot = [sb(f"k_rot{p}", [P, H, HI, 2, HALF]) for p in range(2)]
        q_rot = sb("q_rot", [P, H, HI, 2, HALF])
        k_tmp, q_tmp = sb("k_tmp", [P, 2, H, HI, HALF]), sb("q_tmp", [P, 2, H, HI, HALF])
        kq_t = [sb(f"kq_t{p}", [P, 2, H, LO, C]) for p in range(2)]
        kq = sb("kq", [P, P, 2 * C])
        solved = sb("solved", [P, P, 2, C])
        raw = sb("raw", [P, 2, C, LO, C])
        ea, ep = sb("ea", [P, C, LO, C]), sb("ep", [P, C, LO, C])
        scal = sb("scal", [P, 4, LO, C])
        cg, cs = sb("cg", [P, LO, C]), sb("cs", [P, LO, C])
        sx = sb("sx", [P, 5, LO, C])
        g_c = sb("g_c", [P, LO])
        g_own = sb("g_own", [P, P // HI, LO])
        ones = sb("ones", [P, C])
        g_out = sb("g_out", [P, GB, 3, HP])
        d_out = sb("d_out", [P, GB * H * LO])
        p_k, p_q = ps("p_k", [P, 512]), ps("p_q", [P, 512])
        p_t = [ps(f"p_t{i}", [P, 512]) for i in range(2)]
        p_c = [ps(f"p_c{i}", [P, 512]) for i in range(2)]
        p_kk = [ps(f"p_kk{i}", [P, 512]) for i in range(2)]

        loaded = sem("loaded")
        x_loaded, tab_loaded, scal_loaded = two("x_loaded"), sem("tab_loaded"), sem("scal_loaded")
        projected, q_copied, k_rotated, q_rotated = two("projected"), two("q_copied"), two("k_rotated"), two("q_rotated")
        kt_turned, qt_turned, kt_copied, qt_copied = (two(x) for x in ("kt_turned", "qt_turned", "kt_copied", "qt_copied"))
        products, products_copied = two("products"), two("products_copied")
        k_stored, kq_stored = two("k_stored"), two("kq_stored")
        chain_turned, chain_copied = sem("chain_turned"), sem("chain_copied")
        exponents, exps, small_exps = (sem(x) for x in ("exponents", "exps", "small_exps"))
        vec_rot, vec_own, pool_rot, pool_setup, vec_solved, pool_solved = (
            sem(x) for x in ("vec_rot", "vec_own", "pool_rot", "pool_setup", "vec_solved", "pool_solved"))
        a_ready, queries_ready, t_started, scaled_ready, gown_ready = (
            sem(x) for x in ("a_ready", "queries_ready", "t_started", "scaled_ready", "gown_ready"))
        solved_stored, g_stored = sem("solved_stored"), sem("g_stored")
        pe_passed, po_passed, ve_passed = sem("pe_passed"), sem("po_passed"), sem("ve_passed")
        block = ctx.enter_context(nc.Block())

        GROUPS = NG * NCH
        PAIRS = GB // 2
        IN_BANKS = 2 * C // 4
        G_BANKS = 2
        FORM_BANKS = C // 4
        BANKS = IN_BANKS + G_BANKS + 2 * FORM_BANKS
        SPLIT = 3
        SLICE_BANKS = [range(0, 16), range(0), range(16, 18), range(18, 20), range(20, 22), range(22, 24),
                       range(24, 26), range(26, 34)]
        SLICE_ROWS = [range(0), range(0, 4), range(4, 10), range(10, 15), range(15, 20), range(20, 26), range(26, C - 1),
                      range(0)]

        def grouped(eng, turn, chain_slice, between=None, last=None):
            for k in range(GB):
                turn(0, k, first=k == 0)
            with eng.Fori(1, GROUPS) as grp:
                for k in range(GB):
                    turn(grp, k, chain=lambda: chain_slice(grp - 1, k))
            if last:
                last()
            for k in range(GB):
                chain_slice(GROUPS - 1, k)

        @block.sync
        def _(sp):
            for dst, src in ((ident[:, :], a["ident"]), (own_bh[:, :], a["own"]), (pick[:, :], a["pick"]),
                             (causal[:, :, :], a["causal"].rearrange("p (t s) -> p t s", t=C)),
                             (wq[:, :], a["Wq"]), (wk[:, :], a["Wk"])):
                sp.dma_start(dst, src).then_inc(loaded, 16)
            scal_v = s["scal"].rearrange("v (g b) (c l) t -> v g (b c) l t", g=NG, l=LO)
            with sp.Fori(0, NG) as g:
                with sp.Fori(0, NCH) as j:
                    grp = g * NCH + j
                    sp.wait_ge(k_rotated[1], grp * PAIRS)
                    sp.wait_ge(q_rotated[1], grp * PAIRS)
                    sp.dma_start(tab[:, :, :, :, :].rearrange("p x h i f -> p (x h i f)"), s["tab"][j]).then_inc(tab_loaded, 16)
                    for k in range(GB):
                        r, p = grp * PAIRS + k // 2, k % 2
                        sp.wait_ge(projected[p], r)
                        cols = s["xT"][:, bass.ds((g * GB + k) * T + j * C, C)]
                        sp.dma_start(x_r[p][:, :, :], cols.unsqueeze(1).broadcast_to([P, LO, C])).then_inc(x_loaded[p], 16)
                        if k == 4:
                            sp.wait_ge(small_exps, grp)
                            for v in range(4):
                                sp.dma_start(scal[:, v, :, :], scal_v[v, g, :, :, bass.ds(j * C, C)]).then_inc(scal_loaded, 16)

        @block.tensor
        def _(pe):
            pe.wait_ge(loaded, 16 * 6)
            pe.wait_ge(pool_setup, 1)

            def multiply(r, p):
                pe.wait_ge(kt_copied[p], r + 1)
                pe.wait_ge(qt_copied[p], r + 1)
                pe.wait_ge(*sooner(products_copied, p, r))
                apart(pe, pe_passed)
                for h in range(H):
                    for lo in range(LO):
                        for hi in range(HI):
                            rows = slice(DK * hi, DK * hi + DK)
                            last = pe.matmul(p_kk[hi][C * lo:C * lo + C, 2 * C * h:2 * C * h + 2 * C],
                                             kq_t[p][rows, 0, h, lo, :], kq_t[p][rows, :, h, lo, :],
                                             start=True, stop=True, tile_position=(DK * hi, C * lo))
                last.then_inc(products[p], 1)

            def turn(grp, k, first=False, chain=None):
                r, p = grp * PAIRS + k // 2, k % 2
                pe.wait_ge(x_loaded[p], r * 16 + 16)
                if not first:
                    pe.wait_ge(*sooner(k_rotated, p, r))
                    pe.wait_ge(*sooner(q_copied, p, r))
                rep = x_r[p][:, :, :].rearrange("p l t -> p (l t)")
                pe.matmul(p_q[:, :], rep, wq[:, :], start=True, stop=True)
                pe.matmul(p_k[:, :], rep, wk[:, :], start=True, stop=True).then_inc(projected[p], 1)
                if not first:
                    multiply(*((r, 0) if p else (r - 1, 1)))
                pe.wait_ge(k_rotated[p], r + 1)
                if not first:
                    pe.wait_ge(*sooner(qt_copied, p, r))
                for h in range(H):
                    last = pe.transpose(p_t[h // 4][:, P * (h % 4):P * (h % 4) + P],
                                        k_rot[p][:, h, :, :, :].rearrange("p i x f -> p (i x f)"), ident[:, :])
                last.then_inc(kt_turned[p], 1)
                if chain:
                    chain()
                pe.wait_ge(q_rotated[p], r + 1)
                pe.wait_ge(kt_copied[p], r + 1)
                for h in range(H):
                    last = pe.transpose(p_t[h // 4][:, P * (h % 4):P * (h % 4) + P],
                                        q_rot[:, h, :, :, :].rearrange("p i x f -> p (i x f)"), ident[:, :])
                last.then_inc(qt_turned[p], 1)

            def chain_slice(grp, k):
                for m in SLICE_BANKS[k]:
                    bank = p_c[m % 2]
                    if m == 0:
                        pe.wait_ge(products_copied[1], grp * PAIRS + PAIRS)
                    pe.wait_ge(chain_copied, grp * BANKS + max(m - 1, 0))
                    if m < IN_BANKS:
                        for i in range(4):
                            last = pe.transpose(bank[:, P * i:P * i + P], kq[:, :, 4 * m + i], ident[:, :])
                    elif m == IN_BANKS:
                        pe.wait_ge(small_exps, grp + 1)
                        for i in range(3):
                            last = pe.transpose(bank[:, P * i:P * i + P], sx[:, 2 + i, :, :].rearrange("p l t -> p (l t)"), ident[:, :])
                    elif m == IN_BANKS + 1:
                        pe.wait_ge(gown_ready, grp + 1)
                        last = pe.matmul(bank[:, 0:2 * P], pick[:, :], g_own[:, :, :].rearrange("p c l -> p (c l)"),
                                         start=True, stop=True)
                    else:
                        form, t0 = (m - IN_BANKS - G_BANKS) // FORM_BANKS, (m - IN_BANKS - G_BANKS) % FORM_BANKS * 4
                        if t0 == 0:
                            pe.wait_ge((queries_ready, scaled_ready)[form], grp + 1)
                        src = (raw[:, 1], ea)[form]
                        for i in range(4):
                            last = pe.transpose(bank[:, P * i:P * i + P],
                                                src[:, t0 + i, :, :].rearrange("p l s -> p (l s)"), ident[:, :])
                    last.then_inc(chain_turned, 1)

            grouped(pe, turn, chain_slice, last=lambda: multiply(GROUPS * PAIRS - 1, 1))

        @block.scalar
        def _(act):
            act.wait_ge(loaded, 16 * 6)

            def copy_products(grp, k):
                r, p = grp * PAIRS + k // 2, k % 2
                act.wait_ge(products[p], r + 1)
                for hi in range(HI):
                    last = act.activation(kq[:, HP * k + hi:HP * k + HP:HI, :],
                                          p_kk[hi][:, :].rearrange("p (h x) -> p h x", h=H), ACT.Copy)
                last.then_inc(products_copied[p], 1)

            def turn(grp, k, first=False, chain=None):
                r, p = grp * PAIRS + k // 2, k % 2
                act.wait_ge(projected[p], r + 1)
                if not first:
                    act.wait_ge(*sooner(q_rotated, p, r))
                act.activation(q_s[:, :, :, :].rearrange("p h x f -> p (h x f)"), p_q[:, :], ACT.Copy).then_inc(q_copied[p], 1)
                if k:
                    copy_products(grp, k - 1)
                elif not first:
                    copy_products(grp - 1, GB - 1)
                act.wait_ge(kt_turned[p], r + 1)
                act.wait_ge(products[p], r)
                act.wait_ge(kq_stored[p], r * 16)
                for i in range(2):
                    last = act.activation(kq_t[p][:, 0, 4 * i:4 * i + 4, :, :].rearrange("p h l t -> p (h l t)"),
                                          p_t[i][:, :], ACT.Copy)
                last.then_inc(kt_copied[p], 1)
                act.dma_start(s["kd"][grp * GB + k], k_rot[p][:, :, :, :, :].rearrange("p h i x f -> p (h i x f)")).then_inc(k_stored[p], 16)
                if chain:
                    chain()
                act.wait_ge(qt_turned[p], r + 1)
                for i in range(2):
                    last = act.activation(kq_t[p][:, 1, 4 * i:4 * i + 4, :, :].rearrange("p h l t -> p (h l t)"),
                                          p_t[i][:, :], ACT.Copy)
                last.then_inc(qt_copied[p], 1)
                act.wait_ge(qt_copied[p], r + 1)
                act.wait_ge(kt_copied[p], r + 1)
                act.dma_start(s["qd"][grp * GB + k], kq_t[p][:, :, :, :, :].rearrange("p x h l t -> p (x h l t)")).then_inc(kq_stored[p], 16)

            def chain_slice(grp, k):
                for m in SLICE_BANKS[k]:
                    bank = p_c[m % 2]
                    act.wait_ge(chain_turned, grp * BANKS + m + 1)
                    if m < IN_BANKS:
                        last = act.activation(raw[:, m // 8, 4 * (m % 8):4 * (m % 8) + 4, :, :].rearrange("p t l s -> p (t l s)"),
                                              bank[:, :], ACT.Copy)
                    elif m == IN_BANKS:
                        act.wait_ge(g_stored, grp * 32)
                        last = act.activation(g_out[:, :, :, :].rearrange("p b x c -> p x b c"),
                                              bank[:, 0:3 * P].rearrange("p (x b c) -> p x b c", x=3, b=GB), ACT.Copy)
                    elif m == IN_BANKS + 1:
                        last = act.activation(d_out[:, :], bank[:, 0:2 * P], ACT.Copy)
                    else:
                        form, t0 = (m - IN_BANKS - G_BANKS) // FORM_BANKS, (m - IN_BANKS - G_BANKS) % FORM_BANKS * 4
                        if form == 0 and t0 == 0:
                            act.wait_ge(solved_stored, grp * 16)
                        last = act.activation(solved[:, :, form, t0:t0 + 4], bank[:, :].rearrange("p (t c) -> p c t", t=4), ACT.Copy)
                    last.then_inc(chain_copied, 1)
                if k == 0:
                    for i, e in enumerate((ea, ep)):
                        act.wait_ge(exponents, grp * 2 + i + 1)
                        act.activation(e[:, :, :, :].rearrange("p t l s -> p (t l s)"),
                                       e[:, :, :, :].rearrange("p t l s -> p (t l s)"), ACT.Exp).then_inc(exps, 1)
                    act.activation(sx[:, :, :, :].rearrange("p k l t -> p (k l t)"),
                                   sx[:, :, :, :].rearrange("p k l t -> p (k l t)"), ACT.Exp)
                    act.activation(g_c[:, :], cg[:, :, C - 1], ACT.Exp).then_inc(small_exps, 1)
                if k == 2:
                    act.wait_ge(chain_copied, grp * BANKS + IN_BANKS + G_BANKS)
                    act.dma_start(s["gd"][grp], g_out[:, :, :, :].rearrange("p b x c -> p (b x c)")).then_inc(g_stored, 16)
                    act.dma_start(s["sd"][grp], d_out[:, :]).then_inc(g_stored, 16)
                if k == GB - 1:
                    act.wait_ge(chain_copied, grp * BANKS + BANKS)
                    act.dma_start(s["od"][grp], solved[:, :, :, :].rearrange("p c x t -> p (c x t)")).then_inc(solved_stored, 16)

            grouped(act, turn, chain_slice, last=lambda: copy_products(GROUPS - 1, GB - 1))
            for p in range(2):
                act.wait_ge(k_stored[p], 16 * GROUPS * PAIRS)
                act.wait_ge(kq_stored[p], 16 * GROUPS * PAIRS)
            act.wait_ge(solved_stored, 16 * GROUPS)
            act.wait_ge(g_stored, 32 * GROUPS)

        def rotate(eng, own, src, dst, tmp, done):
            for x in range(2):
                own.did(eng.tensor_tensor(dst[:, :, :, x, :], src[:, :, x, :].unsqueeze(2).broadcast_to([P, H, HI, HALF]),
                                          tab[:, 0, :, :, :], ALU.mult))
                own.did(eng.tensor_tensor(tmp[:, x, :, :, :], src[:, :, 1 - x, :].unsqueeze(2).broadcast_to([P, H, HI, HALF]),
                                          tab[:, 1, :, :, :], ALU.mult))
            eng.wait_ge(own.sem, own.value())
            for x, op in ((0, ALU.add), (1, ALU.subtract)):
                last = eng.tensor_tensor(dst[:, :, :, x, :], dst[:, :, :, x, :], tmp[:, x, :, :, :], op)
            last.then_inc(done, 1)

        def solve(eng, sem, grp, rows, los):
            n = los.stop - los.start
            own = Tally(eng, sem, grp * 2 * (C - 1) + 2 * rows.start)
            for i in rows:
                below, seen = C - 1 - i, i + 1
                part = ep[:, i + 1:C, los, 0:seen]
                eng.wait_ge(sem, own.value())
                own.did(eng.tensor_tensor(part, raw[:, 0, i + 1:C, los, i:i + 1].broadcast_to([P, below, n, seen]),
                                          ea[:, i:i + 1, los, 0:seen].broadcast_to([P, below, n, seen]), ALU.mult))
                eng.wait_ge(sem, own.value())
                rest = ea[:, i + 1:C, los, 0:seen]
                own.did(eng.tensor_tensor(rest, rest, part, ALU.subtract))

        @block.gpsimd
        def _(po):
            po.memset(ones[:, :], 1.0).then_inc(pool_setup, 1)

            def turn(grp, k, first=False, chain=None):
                r, p = grp * PAIRS + k // 2, k % 2
                own = Tally(po, pool_rot, grp * (GB * 4) + k * 4)
                if k == 0:
                    po.wait_ge(tab_loaded, grp * 16 + 16)
                po.wait_ge(q_copied[p], r + 1)
                if not first:
                    po.wait_ge(*sooner(qt_turned, p, r))
                    po.wait_ge(*sooner(q_rotated, p, r))
                rotate(po, own, q_s, q_rot, q_tmp, q_rotated[p])
                if chain:
                    chain()

            def chain_slice(grp, k):
                if k == 1:
                    po.wait_ge(a_ready, grp + 1)
                    po.wait_ge(t_started, grp * LO + LO)
                    po.wait_ge(queries_ready, grp + 1)
                solve(po, pool_solved, grp, SLICE_ROWS[k], slice(SPLIT, LO))

            grouped(po, turn, chain_slice)

        @block.vector
        def _(ve):
            ve.wait_ge(loaded, 16 * 6)
            ve.wait_ge(pool_setup, 1)
            STEPS = 12

            def turn(grp, k, first=False, chain=None):
                r, p = grp * PAIRS + k // 2, k % 2
                own = Tally(ve, vec_rot, grp * (GB * 4) + k * 4)
                if k == 0:
                    ve.wait_ge(tab_loaded, grp * 16 + 16)
                ve.wait_ge(projected[p], r + 1)
                ve.wait_ge(kt_turned[p], r)
                ve.wait_ge(k_stored[p], r * 16)
                if not first:
                    ve.wait_ge(*sooner(k_rotated, p, r))
                k4 = p_k[:, :].rearrange("p (h x f) -> p h x f", h=H, x=2)
                rotate(ve, own, k4, k_rot[p], k_tmp, k_rotated[p])
                if chain:
                    chain()

            def prepare(grp):
                own = Tally(ve, vec_own, grp * STEPS)

                def settle():
                    ve.wait_ge(vec_own, own.value())

                ve.wait_ge(scal_loaded, grp * 64 + 64)
                ve.wait_ge(small_exps, grp)
                ve.wait_ge(scaled_ready, grp)
                ve.wait_ge(chain_turned, grp * BANKS)
                for lo in range(LO):
                    own.did(ve.tensor_tensor_scan(cg[:, lo, :], ones[:, :], scal[:, 0, lo, :], 0.0, ALU.mult, ALU.add))
                settle()
                own.did(ve.tensor_tensor(cs[:, :, :], cg[:, :, :], scal[:, 2, :, :], ALU.subtract))
                own.did(ve.tensor_tensor(sx[:, 0, :, :], scal[:, 1, :, :], scal[:, 2, :, :], ALU.subtract))
                own.did(ve.tensor_tensor(sx[:, 1, :, :], scal[:, 1, :, :], cg[:, :, :], ALU.add))
                own.did(ve.tensor_tensor(sx[:, 3, :, :], scal[:, 3, :, :], cg[:, :, :], ALU.add))
                own.did(ve.tensor_tensor(sx[:, 4, :, :], scal[:, 2, :, :], cg[:, :, :], ALU.add))
                settle()
                own.did(ve.tensor_tensor(sx[:, 2, :, :], cg[:, :, C - 1:C].broadcast_to([P, LO, C]), cs[:, :, :], ALU.subtract))
                own.did(ve.tensor_tensor(ep[:, :, :, :], causal[:, :, :].unsqueeze(2).broadcast_to([P, C, LO, C]),
                                         cs[:, :, :].unsqueeze(1).broadcast_to([P, C, LO, C]), ALU.subtract))
                settle()
                by_t = lambda x: x.rearrange("p l t -> p t l").unsqueeze(3).broadcast_to([P, C, LO, C])
                ve.tensor_tensor(ea[:, :, :, :], ep[:, :, :, :], by_t(sx[:, 1, :, :]), ALU.add).then_inc(exponents, 1)
                ve.wait_ge(exponents, grp * 2 + 1)
                ve.tensor_tensor(ep[:, :, :, :], ep[:, :, :, :], by_t(sx[:, 3, :, :]), ALU.add).then_inc(exponents, 1)
                ve.wait_ge(exponents, grp * 2 + 2)
                assert own.n == STEPS - 1, own.n

            def start_triangle(grp):
                own = Tally(ve, vec_own, grp * STEPS + STEPS - 1)
                ve.wait_ge(chain_copied, grp * BANKS + IN_BANKS)
                ve.wait_ge(exps, grp * 2 + 1)
                ve.tensor_tensor(raw[:, 0, :, :, :], raw[:, 0, :, :, :], ea[:, :, :, :], ALU.mult).then_inc(a_ready, 1)
                ve.wait_ge(exps, grp * 2 + 2)
                ve.tensor_tensor(raw[:, 1, :, :, :], raw[:, 1, :, :, :], ep[:, :, :, :], ALU.mult).then_inc(queries_ready, 1)
                ve.wait_ge(a_ready, grp + 1)
                own.did(ve.memset(ea[:, :, :, :], 0.0))
                ve.wait_ge(small_exps, grp + 1)
                ve.tensor_tensor(g_own[:, :, :], own_bh[:, :].unsqueeze(2).broadcast_to([P, P // HI, LO]),
                                 g_c[:, :].unsqueeze(1).broadcast_to([P, P // HI, LO]), ALU.mult).then_inc(gown_ready, 1)
                ve.wait_ge(vec_own, own.value())
                flat = ea[:, :, :, :].rearrange("p t l s -> p (t l s)")
                for lo in range(LO):
                    ve.memset(flat[:, C * lo:C * lo + (LO * C + 1) * (C - 1) + 1:LO * C + 1], 1.0).then_inc(t_started, 1)
                ve.wait_ge(t_started, grp * LO + LO)
                ve.wait_ge(queries_ready, grp + 1)

            def chain_slice(grp, k):
                if k == 0:
                    prepare(grp)
                if k == 1:
                    start_triangle(grp)
                solve(ve, vec_solved, grp, SLICE_ROWS[k], slice(0, SPLIT))
                if k == GB - 2:
                    ve.wait_ge(vec_solved, grp * 2 * (C - 1) + 2 * (C - 1))
                    ve.wait_ge(pool_solved, grp * 2 * (C - 1) + 2 * (C - 1))
                    ve.tensor_tensor(ea[:, :, :, :], ea[:, :, :, :], sx[:, 0, :, :].unsqueeze(1).broadcast_to([P, C, LO, C]),
                                     ALU.mult).then_inc(scaled_ready, 1)

            grouped(ve, turn, chain_slice)


class Turn:

    def __init__(self, seq, t, step=0):
        self.p = t % 2
        self.same = seq * (NCH // 2) + t // 2 + step
        self.all = seq * NCH + t + step * 2
        self.first, self.last = t == 0, t == NCH - 1
        self.stated = seq * (NCH - 1) + (0 if self.first else t - 1) + step * 2
        self.updating = seq * (NCH - 1) + t + step * 2
        self.both = seq * (NCH - 2) + (0 if self.first else t - 1) + step * 2
        self.both_same = seq * (NCH // 2 - 1) + (0 if self.first else (t - 1) // 2) + step


def across_chunks(nc, a, s):
    with ExitStack() as ctx:
        def sb(name, shape):
            return ctx.enter_context(nc.sbuf_tensor("ac_" + name, shape, F32))

        def ps(name, shape):
            return ctx.enter_context(nc.psum_tensor("ac_" + name, shape, F32))

        def sem(name):
            return signal(nc, s, "ac_" + name)

        def two(name):
            return [sem(name + "0"), sem(name + "1")]

        HH = H // 2
        wv, fold = sb("wv", [P, H * DK]), sb("fold", [P, C])
        x_r = [sb(f"x_r{p}", [P, LO, C]) for p in range(2)]
        k_in = [sb(f"k_in{p}", [P, HP, DK]) for p in range(2)]
        kq_in = [sb(f"kq_in{p}", [P, 2, H, LO, C]) for p in range(2)]
        forms = [sb(f"forms{p}", [P, HP, 2, C]) for p in range(2)]
        g_in = [sb(f"g_in{p}", [P, 3, HP]) for p in range(2)]
        decay = [sb(f"decay{p}", [P, H, LO]) for p in range(2)]
        v_s = sb("v_s", [P, H, DK])
        k_s = [sb(f"k_s{p}", [P, HP, DK]) for p in range(2)]
        state = sb("state", [P, H, LO, HI, DK])
        rest = [sb(f"rest{h}", [P, HI, HH, DK]) for h in range(2)]
        u = [sb(f"u{h}", [P, HI, HH, DK]) for h in range(2)]
        u_wide = [sb(f"u_wide{h}", [P, HI, HH, LO, DK]) for h in range(2)]
        qs = [sb(f"qs{h}", [P, HI, HH, DK]) for h in range(2)]
        o_out = [sb(f"o_out{p}", [P, 2 * DK]) for p in range(2)]
        p_m = [[ps(f"p_m{h}{i}", [P, 512]) for i in range(HH // 2)] for h in range(2)]
        p_h = [ps(f"p_h{i}", [P, 512]) for i in range(2)]
        p_u, p_o = ps("p_u", [P, 512]), ps("p_o", [P, 512])

        loaded = sem("loaded")
        x_loaded, in_loaded, scal_loaded = two("x_loaded"), two("in_loaded"), two("scal_loaded")
        v_done, v_copied, keys_scaled = (sem(x) for x in ("v_done", "v_copied", "keys_scaled"))
        products, rest_ready, qs_ready, vec_own = two("products"), two("rest_ready"), two("qs_ready"), sem("vec_own")
        u_done, u_copied, u_spread, cleared = two("u_done"), two("u_copied"), two("u_spread"), sem("cleared")
        out_low, out_high, o_copied, o_stored = sem("out_low"), two("out_high"), sem("o_copied"), two("o_stored")
        updated, applied, decayed_low, decayed_high = two("updated"), two("applied"), sem("decayed_low"), two("decayed_high")
        pe_passed, sp_passed = sem("pe_passed"), sem("sp_passed")
        block = ctx.enter_context(nc.Block())

        def sequences(eng, body):
            with eng.Fori(0, NG) as g:
                with eng.Fori(0, GB) as b:
                    seq = g * GB + b
                    body(Turn(seq, 0), g * NCH, b, None)
                    body(Turn(seq, 1), g * NCH + 1, b, Turn(seq, 0))
                    with eng.Fori(0, NCH // 2 - 2) as j:
                        for t in (2, 3):
                            body(Turn(seq, t, j), g * NCH + j * 2 + t, b, Turn(seq, t - 1, j))
                    for t in (NCH - 2, NCH - 1):
                        body(Turn(seq, t), g * NCH + t, b, Turn(seq, t - 1))

        @block.sync
        def _(sp):
            sp.dma_start(wv[:, :], a["Wv"]).then_inc(loaded, 16)
            sp.dma_start(fold[:, :], a["fold"]).then_inc(loaded, 16)

            def turn(n, grp, b, before):
                p = n.p
                sp.wait_ge(out_high[p], n.same)
                apart(sp, sp_passed)
                sp.wait_ge(decayed_high[p], n.both_same)
                apart(sp, sp_passed)
                cols = s["xT"][:, bass.ds(n.all * C, C)]
                sp.dma_start(x_r[p][:, :, :], cols.unsqueeze(1).broadcast_to([P, LO, C])).then_inc(x_loaded[p], 16)
                sp.dma_start(kq_in[p][:, :, :, :, :].rearrange("p x h l t -> p (x h l t)"), s["qd"][grp * GB + b]).then_inc(in_loaded[p], 16)
                sp.dma_start(g_in[p][:, :, :].rearrange("p x c -> p (x c)"),
                             s["gd"][grp][:, bass.ds(b * (3 * HP), 3 * HP)]).then_inc(scal_loaded[p], 16)
                sp.dma_start(decay[p][:, :, :].rearrange("p h l -> p (h l)"),
                             s["sd"][grp][:, bass.ds(b * (H * LO), H * LO)]).then_inc(scal_loaded[p], 16)
                sp.dma_start(k_in[p][:, :, :].rearrange("p c k -> p (c k)"), s["kd"][grp * GB + b]).then_inc(in_loaded[p], 16)
                sp.dma_start(forms[p][:, :, :, :].rearrange("p c x t -> p (c x t)"),
                             s["od"][grp][:, bass.ds(b * (HP * 2 * C), HP * 2 * C)]).then_inc(in_loaded[p], 16)

            sequences(sp, turn)

        @block.tensor
        def _(pe):
            pe.wait_ge(loaded, 32)
            pe.wait_ge(cleared, 3)

            def heads(half):
                return [(h, half * HH + h) for h in range(HH)]

            def read_state(n, half):
                pe.wait_ge(in_loaded[n.p], n.same * 48 + 48)
                if half == 0:
                    pe.wait_ge(qs_ready[1], n.stated)
                else:
                    pe.wait_ge(qs_ready[0], n.stated + 1)
                for h, head in heads(half):
                    if h % 2 == 0:
                        pe.wait_ge(applied[half], (n.updating - 1) * 2 + h // 2 + 1)
                    for x in range(2):
                        for lo in range(LO):
                            last = pe.matmul(p_h[x][C * lo:C * lo + C, HI * DK * h:HI * DK * h + HI * DK],
                                             kq_in[n.p][:, x, head, lo, :],
                                             state[:, head, lo, :, :].rearrange("p i v -> p (i v)"),
                                             start=True, stop=True, tile_position=(0, C * lo))
                last.then_inc(products[half], 1)

            def values(n):
                pe.wait_ge(x_loaded[n.p], n.same * 16 + 16)
                pe.wait_ge(u_copied[1], n.all)
                pe.matmul(p_u[:, :], x_r[n.p][:, :, :].rearrange("p l t -> p (l t)"), wv[:, :],
                          start=True, stop=True).then_inc(v_done, 1)

            def solve(n, half):
                pe.wait_ge(v_copied, n.all + 1)
                if half:
                    pe.wait_ge(u_copied[0], n.all + 1)
                if n.first:
                    pe.wait_ge(in_loaded[n.p], n.same * 48 + 48)
                else:
                    pe.wait_ge(rest_ready[half], n.stated + 1)
                apart(pe, pe_passed)
                for h, head in heads(half):
                    for hi in range(HI):
                        for lo in range(LO):
                            rows = slice(C * lo, C * lo + C)
                            src = v_s[rows, head, :] if n.first else rest[half][rows, hi, h, :]
                            at = DK * (hi * HH + h)
                            last = pe.matmul(p_u[rows, at:at + DK], forms[n.p][rows, head * HI + hi, 1, :], src,
                                             start=True, stop=True, tile_position=(C * lo, C * lo))
                last.then_inc(u_done[half], 1)

            def output(n, half):
                pe.wait_ge(u_copied[half], n.all + 1)
                if half == 0:
                    pe.wait_ge(o_copied, n.all)
                if not n.first:
                    pe.wait_ge(qs_ready[half], n.stated + 1)
                    for hi in range(HI):
                        for q in range(2):
                            quarter = C * (2 * half + q)
                            pe.matmul(p_o[quarter:quarter + C, 0:2 * DK], fold[:, :],
                                      qs[half][:, hi, 2 * q:2 * q + 2, :].rearrange("p h v -> p (h v)"),
                                      start=hi == 0, stop=False, tile_position=(0, quarter), skip_group_check=True)
                for h2 in range(2):
                    for hi in range(HI):
                        for q in range(2):
                            h = 2 * q + h2
                            quarter = C * (2 * half + q)
                            last = pe.matmul(p_o[quarter:quarter + C, DK * h2:DK * h2 + DK],
                                             forms[n.p][:, (half * HH + h) * HI + hi, 0, :], u[half][:, hi, h, :],
                                             start=n.first and hi == 0 and h2 == 0, stop=hi == HI - 1,
                                             tile_position=(0, quarter), skip_group_check=True)
                last.then_inc(out_high[n.p] if half else out_low, 1)

            def update(n, half):
                if half == 0:
                    pe.wait_ge(keys_scaled, n.updating + 1)
                pe.wait_ge(u_spread[half], n.updating + 1)
                pe.wait_ge(applied[half], n.updating * 2)
                for h, head in heads(half):
                    for hi in range(HI):
                        at = LO * DK * (h % 2)
                        last = pe.matmul(p_m[half][h // 2][DK * hi:DK * hi + DK, at:at + LO * DK],
                                         k_s[n.p][:, head * HI + hi, :],
                                         u_wide[half][:, hi, h, :, :].rearrange("p l v -> p (l v)"),
                                         start=True, stop=True, tile_position=(0, DK * hi))
                    if h % 2:
                        last.then_inc(updated[half], 1)

            def turn(n, grp, b, before):
                if not n.first:
                    read_state(n, 0)
                values(n)
                if before:
                    output(before, 1)
                    update(before, 1)
                solve(n, 0)
                if not n.first:
                    read_state(n, 1)
                output(n, 0)
                if not n.last:
                    update(n, 0)
                solve(n, 1)
                if n.last:
                    output(n, 1)

            sequences(pe, turn)

        @block.scalar
        def _(act):
            act.wait_ge(cleared, 3)

            def copy_o(n):
                act.wait_ge(out_high[n.p], n.same + 1)
                act.wait_ge(o_stored[n.p], n.same * 64)
                act.activation(o_out[n.p][:, :], p_o[:, 0:2 * DK], ACT.Copy).then_inc(o_copied, 1)
                act.wait_ge(o_copied, n.all + 1)
                for q in range(4):
                    act.dma_start(s["oo"][bass.ds(n.all * C, C), 2 * DK * q:2 * DK * q + 2 * DK],
                                  o_out[n.p][C * q:C * q + C, :]).then_inc(o_stored[n.p], 16)

            def copy_u(n, half):
                act.wait_ge(u_done[half], n.all + 1)
                act.wait_ge(out_high[1 - n.p] if half else out_low, (n.same + n.p) if half else n.all)
                act.activation(u[half][:, :, :, :].rearrange("p i h v -> p (i h v)"), p_u[:, :], ACT.Copy).then_inc(u_copied[half], 1)
                if n.last:
                    return
                act.wait_ge(u_copied[half], n.all + 1)
                act.wait_ge(updated[half], n.updating * 2)
                for lo in range(LO):
                    rows = slice(C * lo, C * lo + C)
                    last = act.activation(u_wide[half][rows, :, :, lo, :].rearrange("p i h v -> p (i h) v"),
                                          u[half][rows, :, :, :].rearrange("p i h v -> p (i h) v"), ACT.Copy)
                last.then_inc(u_spread[half], 1)

            def turn(n, grp, b, before):
                act.wait_ge(v_done, n.all + 1)
                act.wait_ge(u_done[1], n.all)
                if not n.first:
                    act.wait_ge(rest_ready[1], n.stated)
                act.activation(v_s[:, :, :].rearrange("p h v -> p (h v)"), p_u[:, :], ACT.Copy).then_inc(v_copied, 1)
                if before:
                    copy_o(before)
                copy_u(n, 0)
                copy_u(n, 1)
                if n.last:
                    copy_o(n)

            sequences(act, turn)
            for p in range(2):
                act.wait_ge(o_stored[p], 64 * B * NCH // 2)

        @block.gpsimd
        def _(po):
            for x in (state, u_wide[0], u_wide[1]):
                po.memset(x[:, :, :, :, :], 0.0).then_inc(cleared, 1)
            po.wait_ge(cleared, 3)

            def turn(n, grp, b, before):
                p = n.p
                po.wait_ge(scal_loaded[p], n.same * 32 + 32)
                if not n.last:
                    po.wait_ge(in_loaded[p], n.same * 48 + 48)
                    if n.first:
                        po.wait_ge(updated[1], n.updating * 2)
                    po.tensor_tensor(k_s[p][:, :, :], k_in[p][:, :, :],
                                     g_in[p][:, 0, :].unsqueeze(2).broadcast_to([P, HP, DK]), ALU.mult).then_inc(keys_scaled, 1)
                if n.first or n.last:
                    return
                for half in range(2):
                    po.wait_ge(products[half], n.stated + 1)
                    part = state[:, half * HH:half * HH + HH, :, :, :].rearrange("p h l i v -> p (h l) (i v)")
                    po.tensor_tensor(part, part, decay[p][:, half * HH:half * HH + HH, :].rearrange("p h l -> p (h l)").unsqueeze(2)
                                     .broadcast_to([P, HH * LO, HI * DK]), ALU.mult).then_inc(decayed_high[p] if half else decayed_low, 1)

            sequences(po, turn)

        @block.vector
        def _(ve):
            ve.wait_ge(cleared, 3)

            def read(n, half):
                p = n.p
                ve.wait_ge(products[half], n.stated + 1)
                ve.wait_ge(u_done[half], n.all)
                ve.wait_ge(out_high[1 - p] if half else out_low, (n.same + p) if half else n.all)
                ve.wait_ge(scal_loaded[p], n.same * 32 + 32)
                own = Tally(ve, vec_own, n.stated * 2 + half)
                scalar = [g_in[p][:, x, :].rearrange("p (h i) -> p h i", i=HI)[:, half * HH:half * HH + HH, :] for x in range(3)]
                by_hi = lambda x: x.rearrange("p (h i v) -> p i h v", h=HH, i=HI)
                per_row = lambda x: x.rearrange("p h i -> p i h").unsqueeze(3).broadcast_to([P, HI, HH, DK])
                own.did(ve.tensor_tensor(rest[half][:, :, :, :], by_hi(p_h[0][:, :]), per_row(scalar[2]), ALU.mult))
                ve.tensor_tensor(qs[half][:, :, :, :], by_hi(p_h[1][:, :]), per_row(scalar[1]), ALU.mult).then_inc(qs_ready[half], 1)
                ve.wait_ge(vec_own, own.value())
                ve.wait_ge(v_copied, n.all + 1)
                last = ve.tensor_tensor(rest[half][:, :, :, :],
                                        v_s[:, half * HH:half * HH + HH, :].unsqueeze(1).broadcast_to([P, HI, HH, DK]),
                                        rest[half][:, :, :, :], ALU.subtract)
                last.then_inc(rest_ready[half], 1)

            def apply(n, half):
                if n.first:
                    ve.wait_ge(products[half], n.stated)
                else:
                    ve.wait_ge(decayed_high[n.p] if half else decayed_low, (n.both_same if half else n.both) + 1)
                for i in range(HH // 2):
                    ve.wait_ge(updated[half], n.updating * 2 + i + 1)
                    for hi in range(HI):
                        rows, first_head = slice(DK * hi, DK * hi + DK), half * HH + 2 * i
                        part = state[rows, first_head:first_head + 2, :, hi, :].rearrange("p h l v -> p (h l) v")
                        fresh = p_m[half][i][rows, :].rearrange("p (x v) -> p x v", v=DK)
                        last = ve.tensor_copy(part, fresh) if n.first else ve.tensor_tensor(part, part, fresh, ALU.add)
                    last.then_inc(applied[half], 1)

            def turn(n, grp, b, before):
                if not n.first:
                    read(n, 0)
                if before:
                    apply(before, 1)
                if not n.first:
                    read(n, 1)
                if not n.last:
                    apply(n, 0)

            sequences(ve, turn)


def after_attention(nc, a, s, w):
    with ExitStack() as ctx:
        def sb(name, shape):
            return ctx.enter_context(nc.sbuf_tensor("aa_" + name, shape, F32))

        def ps(name, shape):
            return ctx.enter_context(nc.psum_tensor("aa_" + name, shape, F32))

        def sem(name):
            return signal(nc, s, "aa_" + name)

        def two(name):
            return [sem(name + "0"), sem(name + "1")]

        KO = H * DK // P
        ident, wg, wo = sb("ident", [P, P]), sb("wg", [P, H * DK]), sb("wo", [P, KO, D])
        x_t = [sb(f"x_t{p}", [P, P]) for p in range(2)]
        x_in = [sb(f"x_in{p}", [P, D]) for p in range(2)]
        o_in = [sb(f"o_in{p}", [P, H * DK]) for p in range(2)]
        z = [sb(f"z{p}", [P, H * DK]) for p in range(2)]
        og = [sb(f"og{p}", [P, H * DK]) for p in range(2)]
        og_t = [sb(f"og_t{p}", [P, KO, P]) for p in range(2)]
        p_g, p_t, p_a = ([ps(f"{n}{p}", [P, 512]) for p in range(2)] for n in ("p_g", "p_t", "p_a"))
        loaded = sem("loaded")
        t_loaded, o_loaded, x_loaded = two("t_loaded"), two("o_loaded"), two("x_loaded")
        gate_done, exp_ready, gated, turned, copied, out_done, added = (
            two(x) for x in ("gate_done", "exp_ready", "gated", "turned", "copied", "out_done", "added"))
        vec_own = sem("vec_own")
        block = ctx.enter_context(nc.Block())
        HALF_TILES = TILES // 2

        def stages(eng, first, second=None, third=None):
            first and first(0, 0)
            first and first(0, 1)
            second and second(0, 0)
            with eng.Fori(1, HALF_TILES) as r:
                for p in range(2):
                    first and first(r, p)
                    second and second(*((r, 0) if p else (r - 1, 1)))
                    third and third(r - 1, p)
            second and second(HALF_TILES - 1, 1)
            for p in range(2):
                third and third(HALF_TILES - 1, p)

        @block.sync
        def _(sp):
            sp.dma_start(wg[:, :], a["Wg"]).then_inc(loaded, 16)
            x_v = a["x"].rearrange("b (q p) d -> (b q) p d", p=P)

            def load(r, p):
                i = r * 2 + p
                sp.wait_ge(gate_done[p], r)
                sp.dma_start(x_t[p][:, :], s["xT"][:, bass.ds(i * P, P)]).then_inc(t_loaded[p], 16)
                sp.wait_ge(gated[p], r)
                sp.dma_start(o_in[p][:, :], s["oo"][bass.ds(i * P, P), :]).then_inc(o_loaded[p], 16)

            def load_x(r, p):
                sp.wait_ge(added[p], r)
                sp.dma_start(x_in[p][:, :], x_v[r * 2 + p]).then_inc(x_loaded[p], 16)

            for p in range(2):
                load(0, p)
            sp.dma_start(ident[:, :], a["ident"]).then_inc(loaded, 16)
            sp.dma_start(wo[:, :, :], a["Wo"].rearrange("(k p) d -> p k d", p=P)).then_inc(loaded, 16)
            load_x(0, 0)
            with sp.Fori(1, HALF_TILES) as r:
                for p in range(2):
                    load(r, p)
                    load_x(*((r, 0) if p else (r - 1, 1)))
            load_x(HALF_TILES - 1, 1)

        @block.tensor
        def _(pe):
            pe.wait_ge(loaded, 48)

            def gate(r, p):
                pe.wait_ge(t_loaded[p], r * 16 + 16)
                pe.wait_ge(exp_ready[p], r)
                pe.matmul(p_g[p][:, :], x_t[p][:, :], wg[:, :], start=True, stop=True).then_inc(gate_done[p], 1)

            def turn(r, p):
                pe.wait_ge(gated[p], r + 1)
                pe.wait_ge(copied[p], r)
                for k in range(KO):
                    last = pe.transpose(p_t[p][:, P * k:P * k + P], og[p][:, P * k:P * k + P], ident[:, :])
                last.then_inc(turned[p], 1)

            def project(r, p):
                pe.wait_ge(copied[p], r + 1)
                pe.wait_ge(added[p], r)
                for k in range(KO):
                    last = pe.matmul(p_a[p][:, 0:D], og_t[p][:, k, :], wo[:, k, :], start=k == 0, stop=k == KO - 1)
                last.then_inc(out_done[p], 1)

            stages(pe, gate, turn, project)

        @block.scalar
        def _(act):
            def exponential(r, p):
                act.wait_ge(gate_done[p], r + 1)
                act.wait_ge(gated[p], r)
                act.activation(z[p][:, :], p_g[p][:, :], ACT.Sigmoid).then_inc(exp_ready[p], 1)

            def copy(r, p):
                act.wait_ge(turned[p], r + 1)
                act.wait_ge(out_done[p], r)
                act.activation(og_t[p][:, :, :].rearrange("p k t -> p (k t)"), p_t[p][:, :], ACT.Copy).then_inc(copied[p], 1)

            stages(act, exponential, copy)

        @block.vector
        def _(ve):
            def apply_gate(r, p):
                ve.wait_ge(exp_ready[p], r + 1)
                ve.wait_ge(o_loaded[p], r * 16 + 16)
                ve.wait_ge(turned[p], r)
                ve.tensor_tensor(og[p][:, :], o_in[p][:, :], z[p][:, :], ALU.mult).then_inc(gated[p], 1)

            def add(r, p):
                ve.wait_ge(out_done[p], r + 1)
                ve.wait_ge(x_loaded[p], r * 16 + 16)
                ve.tensor_tensor(w["rest"][:, bass.ds(r * 2 + p, 1), :].rearrange("p o d -> p (o d)"),
                                 x_in[p][:, :], p_a[p][:, 0:D], ALU.add).then_inc(added[p], 1)

            stages(ve, apply_gate, None, add)


def layer_norm(ve, own, act_done, requested, dst, src, stats, square, eps_turn):
    n = src.shape[1]
    mean, var, inv = stats

    def step(instruction):
        own.did(instruction)
        ve.wait_ge(own.sem, own.value())

    spread = lambda x: x.unsqueeze(2).broadcast_to([P, n, D])
    step(ve.tensor_reduce(mean, src, AX.X, ALU.add))
    step(ve.tensor_scalar(mean, mean, 1.0 / D, None, ALU.mult))
    step(ve.tensor_tensor(dst, src, spread(mean), ALU.subtract))
    step(ve.tensor_tensor(square, dst, dst, ALU.mult))
    step(ve.tensor_reduce(var, square, AX.X, ALU.add))
    ve.tensor_scalar(inv, var, 1.0 / D, LN_EPS, ALU.mult, ALU.add).then_inc(requested, 1)
    ve.wait_ge(act_done, eps_turn + 1)
    step(ve.tensor_tensor(dst, dst, spread(inv), ALU.mult))


def inverse_roots(act, own, requested, done, inv, turns):
    for k in range(turns):
        act.wait_ge(requested, k + 1)
        act.activation(inv, inv, ACT.Ln).then_inc(own, 1)
        act.wait_ge(own, k + 1)
        act.activation(inv, inv, ACT.Exp, scale=-0.5).then_inc(done, 1)


def norms(nc, a, s, w):
    with ExitStack() as ctx:
        def sb(name, shape):
            return ctx.enter_context(nc.sbuf_tensor("no_" + name, shape, F32))

        def sem(name):
            return signal(nc, s, "no_" + name)

        gain, bias, square = sb("gain", [P, D]), sb("bias", [P, D]), sb("square", [P, TILES, D])
        mean, var, inv = sb("mean", [P, TILES]), sb("var", [P, TILES]), sb("inv", [P, TILES])
        loaded, vec_own, act_own, requested, rooted, zero_ready, zeroed = (
            sem(x) for x in ("loaded", "vec_own", "act_own", "requested", "rooted", "zero_ready", "zeroed"))
        block = ctx.enter_context(nc.Block())
        x1, h = w["rest"][:, :, :], w["h"][:, :, :]

        @block.sync
        def _(sp):
            sp.dma_start(gain[:, :], a["ln_g"].partition_broadcast(P)).then_inc(loaded, 16)
            sp.dma_start(bias[:, :], a["ln_b"].partition_broadcast(P)).then_inc(loaded, 16)
            sp.wait_ge(zero_ready, 1)
            sp.dma_start(s["xe"].rearrange("(t p) d -> p t d", p=P), w["zeros"][:, :, :]).then_inc(zeroed, 16)
            sp.wait_ge(zeroed, 16)

        @block.gpsimd
        def _(po):
            po.memset(w["zeros"][:, :, :], 0.0).then_inc(zero_ready, 1)

        @block.scalar
        def _(act):
            inverse_roots(act, act_own, requested, rooted, inv[:, :], 2)

        @block.vector
        def _(ve):
            own = Tally(ve, vec_own)
            stats = (mean[:, :], var[:, :], inv[:, :])
            layer_norm(ve, own, rooted, requested, x1, x1, stats, square[:, :, :], 0)
            layer_norm(ve, own, rooted, requested, h, x1, stats, square[:, :, :], 1)
            ve.wait_ge(loaded, 32)
            own.did(ve.tensor_tensor(h, h, gain[:, :].unsqueeze(1).broadcast_to([P, TILES, D]), ALU.mult))
            ve.wait_ge(vec_own, own.value())
            own.did(ve.tensor_tensor(h, h, bias[:, :].unsqueeze(1).broadcast_to([P, TILES, D]), ALU.add))


def routing(nc, a, s, w):
    with ExitStack() as ctx:
        def sb(name, shape, dt=F32):
            return ctx.enter_context(nc.sbuf_tensor("ro_" + name, shape, dt))

        def ps(name, shape):
            return ctx.enter_context(nc.psum_tensor("ro_" + name, shape, F32))

        def sem(name):
            return signal(nc, s, "ro_" + name)

        def two(name):
            return [sem(name + "0"), sem(name + "1")]

        E8 = 8
        ident, before, lane = sb("ident", [P, P]), sb("before", [P, P]), sb("lane", [P, E8])
        ones = sb("ones", [P, P])
        wr = sb("wr", [P, E_R])
        h_s = [sb(f"h_s{p}", [P, D]) for p in range(2)]
        h_t = [sb(f"h_t{p}", [P, P]) for p in range(2)]
        logits = sb("logits", [P, TILES, E8])
        cand = sb("cand", [P, TILES, E8])
        picked = [sb(f"picked{c}", [P, TILES, E8]) for c in range(2)]
        total = [sb(f"total{c}", [P, TILES, E8]) for c in range(2)]
        running = [sb(f"running{c}", [P, E8, TILES]) for c in range(2)]
        place = sb("place", [P, TILES, E8])
        best = [sb(f"best{c}", [P, TILES]) for c in range(2)]
        expert = [sb(f"expert{c}", [P, TILES]) for c in range(2)]
        spot, keep, den, odds = sb("spot", [P, TILES]), sb("keep", [P, TILES]), sb("den", [P, TILES]), sb("odds", [P, TILES])
        p_t = [ps(f"p_t{p}", [P, 512]) for p in range(2)]
        p_l = [ps(f"p_l{p}", [P, 512]) for p in range(2)]
        p_c = [ps(f"p_c{c}", [P, 512]) for c in range(4)]
        loaded, setup = sem("loaded"), sem("setup")
        staged, turned, copied, scored, kept = (two(x) for x in ("staged", "turned", "copied", "scored", "kept"))
        vec_own, odds_asked, odds_ready, picked_ready, counted = (
            sem(x) for x in ("vec_own", "odds_asked", "odds_ready", "picked_ready", "counted"))
        block = ctx.enter_context(nc.Block())

        @block.sync
        def _(sp):
            for dst, src in ((ident, "ident"), (before, "before"), (lane, "lane"), (wr, "Wr")):
                sp.dma_start(dst[:, :], a[src]).then_inc(loaded, 16)

        @block.gpsimd
        def _(po):
            po.memset(ones[:, :], 1.0).then_inc(setup, 1)
            with po.Fori(0, TILES // 2) as r:
                for p in range(2):
                    po.wait_ge(turned[p], r)
                    po.tensor_copy(h_s[p][:, :], w["h"][:, bass.ds(r * 2 + p, 1), :].rearrange("p o d -> p (o d)")).then_inc(staged[p], 1)

        @block.tensor
        def _(pe):
            pe.wait_ge(loaded, 64)
            with pe.Fori(0, TILES // 2) as r:
                for p in range(2):
                    pe.wait_ge(staged[p], r + 1)
                    pe.wait_ge(copied[p], r)
                    pe.transpose(p_t[p][:, 0:P], h_s[p][:, :], ident[:, :]).then_inc(turned[p], 1)
                for p in range(2):
                    pe.wait_ge(copied[p], r + 1)
                    pe.wait_ge(kept[p], r)
                    pe.matmul(p_l[p][:, 0:E_R], h_t[p][:, :], wr[:, :], start=True, stop=True).then_inc(scored[p], 1)
            pe.wait_ge(setup, 1)
            for c in range(2):
                pe.wait_ge(picked_ready, c + 1)
                flat = picked[c][:, :, :].rearrange("p t e -> p (t e)")
                pe.matmul(p_c[2 * c][:, :], before[:, :], flat, start=True, stop=True)
                pe.matmul(p_c[2 * c + 1][:, :], ones[:, :], flat, start=True, stop=True).then_inc(counted, 1)

        @block.scalar
        def _(act):
            with act.Fori(0, TILES // 2) as r:
                for p in range(2):
                    act.wait_ge(turned[p], r + 1)
                    act.wait_ge(scored[p], r)
                    act.activation(w["hT"][:, bass.ds((r * 2 + p) * P, P)], p_t[p][:, 0:P], ACT.Copy)
                    act.activation(h_t[p][:, :], p_t[p][:, 0:P], ACT.Copy).then_inc(copied[p], 1)
            act.wait_ge(odds_asked, 1)
            act.activation(odds[:, :], odds[:, :], ACT.Exp).then_inc(odds_ready, 1)

        @block.vector
        def _(ve):
            own = Tally(ve, vec_own)

            def step(instruction):
                own.did(instruction)
                ve.wait_ge(vec_own, own.value())

            ve.wait_ge(loaded, 64)
            ve.wait_ge(setup, 1)
            step(ve.memset(logits[:, :, E_R:E8], -1e30))
            with ve.Fori(0, TILES // 2) as r:
                for p in range(2):
                    ve.wait_ge(scored[p], r + 1)
                    ve.tensor_copy(logits[:, bass.ds(r * 2 + p, 1), 0:E_R].rearrange("p o e -> p (o e)"), p_l[p][:, 0:E_R]).then_inc(kept[p], 1)
            for p in range(2):
                ve.wait_ge(kept[p], TILES // 2)
            per_tile = lambda x: x[:, :].unsqueeze(2).broadcast_to([P, TILES, E8])
            lanes = lane[:, :].unsqueeze(1).broadcast_to([P, TILES, E8])
            for c in range(2):
                step(ve.tensor_reduce(best[c][:, :], logits[:, :, :], AX.X, ALU.max))
                step(ve.tensor_tensor(cand[:, :, :], logits[:, :, :], per_tile(best[c]), ALU.is_lt))
                step(ve.scalar_tensor_tensor(cand[:, :, :], cand[:, :, :], float(E8), lanes, ALU.mult, ALU.add))
                step(ve.tensor_reduce(expert[c][:, :], cand[:, :, :], AX.X, ALU.min))
                ve.tensor_tensor(picked[c][:, :, :], lanes, per_tile(expert[c]), ALU.is_equal).then_inc(picked_ready, 1)
                ve.wait_ge(picked_ready, c + 1)
                if c == 0:
                    step(ve.scalar_tensor_tensor(logits[:, :, :], picked[0][:, :, :], -1e30, logits[:, :, :], ALU.mult, ALU.add))
            ve.tensor_tensor(odds[:, :], best[1][:, :], best[0][:, :], ALU.subtract).then_inc(odds_asked, 1)
            ve.wait_ge(odds_ready, 1)
            step(ve.tensor_scalar(den[:, :], odds[:, :], 1.0, None, ALU.add))
            step(ve.reciprocal(w["gate"][:, 0, :], den[:, :]))
            step(ve.tensor_tensor(w["gate"][:, 1, :], odds[:, :], w["gate"][:, 0, :], ALU.mult))
            for c in range(2):
                ve.wait_ge(counted, c + 1)
                step(ve.tensor_copy(total[c][:, :, :].rearrange("p t e -> p (t e)"), p_c[2 * c + 1][:, :]))
                for e in range(E8):
                    own.did(ve.tensor_tensor_scan(running[c][:, e, :], ones[:, 0:TILES], total[c][:, :, e], 0.0, ALU.mult, ALU.add))
                ve.wait_ge(vec_own, own.value())
                turned_back = running[c][:, :, :].rearrange("p e t -> p t e")
                step(ve.tensor_tensor(place[:, :, :], turned_back, total[c][:, :, :], ALU.subtract))
                step(ve.tensor_tensor(place[:, :, :], place[:, :, :], p_c[2 * c][:, :].rearrange("p (t e) -> p t e", e=E8), ALU.add))
                if c == 1:
                    step(ve.tensor_tensor(place[:, :, :], place[:, :, :],
                                          running[0][:, :, TILES - 1].unsqueeze(1).broadcast_to([P, TILES, E8]), ALU.add))
                step(ve.tensor_tensor(place[:, :, :], place[:, :, :], picked[c][:, :, :], ALU.mult))
                step(ve.tensor_reduce(spot[:, :], place[:, :, :], AX.X, ALU.add))
                step(ve.tensor_scalar(keep[:, :], spot[:, :], float(CAP), None, ALU.is_lt))
                step(ve.tensor_tensor(w["gate"][:, c, :], w["gate"][:, c, :], keep[:, :], ALU.mult))
                step(ve.scalar_tensor_tensor(spot[:, :], expert[c][:, :], float(CAPP), spot[:, :], ALU.mult, ALU.add))
                step(ve.tensor_scalar(keep[:, :], keep[:, :], -float(2 * ROWS), float(2 * ROWS), ALU.mult, ALU.add))
                step(ve.tensor_tensor(spot[:, :], spot[:, :], keep[:, :], ALU.add))
                step(ve.tensor_copy(w["slot"][:, :, c], spot[:, :]))


def dispatch(nc, a, s, w):
    with ExitStack() as ctx:
        def sem(name):
            return signal(nc, s, "di_" + name)

        h_s = [ctx.enter_context(nc.sbuf_tensor(f"di_h_s{p}", [P, D], F32)) for p in range(2)]
        ix = [ctx.enter_context(nc.sbuf_tensor(f"di_ix{p}", [P, 2], U32)) for p in range(2)]
        po_passed = sem("po_passed")
        staged, sent = ([sem(n + "0"), sem(n + "1")] for n in ("staged", "sent"))
        block = ctx.enter_context(nc.Block())

        @block.vector
        def _(ve):
            with ve.Fori(0, TILES // 2) as r:
                for p in range(2):
                    i = r * 2 + p
                    ve.wait_ge(sent[p], r * 32)
                    ve.tensor_copy(h_s[p][:, :], w["h"][:, bass.ds(i, 1), :].rearrange("p o d -> p (o d)")).then_inc(staged[p], 1)
                    ve.tensor_copy(ix[p][:, :], w["slot"][:, bass.ds(i, 1), :].rearrange("p o c -> p (o c)")).then_inc(staged[p], 1)

        @block.gpsimd
        def _(po):
            with po.Fori(0, TILES // 2) as r:
                for p in range(2):
                    po.wait_ge(staged[p], r * 2 + 2)
                    apart(po, po_passed)
                    for c in range(2):
                        po.indirect_dma_start(s["xe"][:, :], bass.IndirectOffsetOnAxis(ap=ix[p][:, c:c + 1], axis=0),
                                              h_s[p][:, :], None, bounds_check=ROWS - 1, oob_is_err=False).then_inc(sent[p], 16)
            for p in range(2):
                po.wait_ge(sent[p], 32 * (TILES // 2))


def experts(nc, a, s, w):
    with ExitStack() as ctx:
        def sb(name, shape):
            return ctx.enter_context(nc.sbuf_tensor("ex_" + name, shape, F32))

        def ps(name, shape):
            return ctx.enter_context(nc.psum_tensor("ex_" + name, shape, F32))

        def sem(name):
            return signal(nc, s, "ex_" + name)

        KF, RT = FF // P, CAPP // P
        ident = sb("ident", [P, P])
        w1, w3, w2 = sb("w1", [P, FF]), sb("w3", [P, FF]), sb("w2", [P, KF, D])
        x_e, x_t, y_e = sb("x_e", [P, RT, D]), sb("x_t", [P, CAPP]), sb("y_e", [P, RT, D])
        act_a, g_t = sb("act_a", [P, KF, CAPP]), sb("g_t", [P, KF, CAPP])
        p_t, p_y = ps("p_t", [P, 512]), ps("p_y", [P, 512])
        p_a = [ps(f"p_a{i}", [P, 512]) for i in range(2)]
        p_b = [ps(f"p_b{i}", [P, 512]) for i in range(2)]
        const_loaded, loaded, turned, copied, a_done, b_done, silu_done, g_done, y_done, y_copied, stored = (
            sem(x) for x in ("const_loaded", "loaded", "turned", "copied", "a_done", "b_done", "silu_done", "g_done",
                             "y_done", "y_copied", "stored"))
        block = ctx.enter_context(nc.Block())

        @block.sync
        def _(sp):
            sp.dma_start(ident[:, :], a["ident"]).then_inc(const_loaded, 16)
            x_v = s["xe"].rearrange("(e t p) d -> e p t d", p=P, t=RT)
            y_v = s["ye"].rearrange("(e t p) d -> e p t d", p=P, t=RT)
            with sp.Fori(0, E_R) as e:
                sp.wait_ge(y_done, e)
                sp.dma_start(x_e[:, :, :], x_v[e]).then_inc(loaded, 16)
                sp.dma_start(w1[:, :], a["W1"][e]).then_inc(loaded, 16)
                sp.dma_start(w3[:, :], a["W3"][e]).then_inc(loaded, 16)
                sp.dma_start(w2[:, :, :], a["W2"].rearrange("e (k p) d -> e p k d", p=P)[e]).then_inc(loaded, 16)
                sp.wait_ge(y_copied, e + 1)
                sp.dma_start(y_v[e], y_e[:, :, :]).then_inc(stored, 16)
            sp.wait_ge(stored, 16 * E_R)

        @block.tensor
        def _(pe):
            pe.wait_ge(const_loaded, 16)
            with pe.Fori(0, E_R) as e:
                pe.wait_ge(loaded, e * 64 + 64)
                for t in range(RT):
                    last = pe.transpose(p_t[:, P * t:P * t + P], x_e[:, t, :], ident[:, :])
                last.then_inc(turned, 1)
                pe.wait_ge(copied, e + 1)
                for k in range(KF):
                    if k < 2:
                        pe.wait_ge(g_done, e * KF)
                    else:
                        pe.wait_ge(g_done, e * KF + k - 1)
                    pe.matmul(p_a[k % 2][:, 0:CAPP], w1[:, P * k:P * k + P], x_t[:, :], start=True, stop=True).then_inc(a_done, 1)
                    pe.matmul(p_b[k % 2][:, 0:CAPP], w3[:, P * k:P * k + P], x_t[:, :], start=True, stop=True).then_inc(b_done, 1)
                pe.wait_ge(g_done, e * KF + KF)
                pe.wait_ge(y_copied, e)
                for t in range(RT):
                    for k in range(KF):
                        last = pe.matmul(p_y[:, P * t:P * t + P], g_t[:, k, P * t:P * t + P], w2[:, k, :],
                                         start=k == 0, stop=k == KF - 1)
                last.then_inc(y_done, 1)

        @block.scalar
        def _(act):
            with act.Fori(0, E_R) as e:
                act.wait_ge(turned, e + 1)
                act.activation(x_t[:, :], p_t[:, 0:CAPP], ACT.Copy).then_inc(copied, 1)
                for k in range(KF):
                    act.wait_ge(a_done, e * KF + k + 1)
                    act.wait_ge(g_done, e * KF)
                    act.activation(act_a[:, k, :], p_a[k % 2][:, 0:CAPP], ACT.Silu).then_inc(silu_done, 1)
                act.wait_ge(y_done, e + 1)
                act.wait_ge(stored, e * 16)
                act.activation(y_e[:, :, :].rearrange("p t d -> p (t d)"), p_y[:, 0:CAPP], ACT.Copy).then_inc(y_copied, 1)

        @block.vector
        def _(ve):
            with ve.Fori(0, E_R) as e:
                for k in range(KF):
                    ve.wait_ge(silu_done, e * KF + k + 1)
                    ve.wait_ge(b_done, e * KF + k + 1)
                    ve.wait_ge(y_done, e)
                    ve.tensor_tensor(g_t[:, k, :], act_a[:, k, :], p_b[k % 2][:, 0:CAPP], ALU.mult).then_inc(g_done, 1)


def shared_and_sum(nc, a, s, w):
    with ExitStack() as ctx:
        def sb(name, shape, dt=F32):
            return ctx.enter_context(nc.sbuf_tensor("sh_" + name, shape, dt))

        def ps(name, shape):
            return ctx.enter_context(nc.psum_tensor("sh_" + name, shape, F32))

        def sem(name):
            return signal(nc, s, "sh_" + name)

        KF, Q4 = FF // P, 4
        GROUPS = TILES // Q4
        w1, w3, w2 = sb("w1", [P, FF]), sb("w3", [P, FF]), sb("w2", [P, KF, D])
        act_a, g_t = sb("act_a", [P, KF, Q4 * P]), sb("g_t", [P, KF, Q4 * P])
        ix = [[sb(f"ix{q}{c}", [P, 1], U32) for c in range(2)] for q in range(Q4)]
        rows = [[sb(f"rows{q}{c}", [P, D]) for c in range(2)] for q in range(Q4)]
        p_y = [ps(f"p_y{i}", [P, 512]) for i in range(2)]
        p_a = [ps(f"p_a{i}", [P, 512]) for i in range(2)]
        p_b = [ps(f"p_b{i}", [P, 512]) for i in range(2)]
        loaded, a_done, b_done, silu_done, g_done, y_done = (
            sem(x) for x in ("loaded", "a_done", "b_done", "silu_done", "g_done", "y_done"))
        cleared, staged, gathered, summed, vec_own, po_passed = (
            sem(x) for x in ("cleared", "staged", "gathered", "summed", "vec_own", "po_passed"))
        block = ctx.enter_context(nc.Block())

        @block.sync
        def _(sp):
            sp.dma_start(w1[:, :], a["W1s"]).then_inc(loaded, 16)
            sp.dma_start(w3[:, :], a["W3s"]).then_inc(loaded, 16)
            sp.dma_start(w2[:, :, :], a["W2s"].rearrange("(k p) d -> p k d", p=P)).then_inc(loaded, 16)

        @block.gpsimd
        def _(po):
            po.wait_ge(cleared, 2 * Q4)
            with po.Fori(0, GROUPS) as i:
                po.wait_ge(summed, i)
                po.wait_ge(staged, i * 2 * Q4 + 2 * Q4)
                apart(po, po_passed)
                for q in range(Q4):
                    for c in range(2):
                        po.indirect_dma_start(rows[q][c][:, :], None, s["ye"][:, :],
                                              bass.IndirectOffsetOnAxis(ap=ix[q][c][:, :], axis=0),
                                              bounds_check=ROWS - 1, oob_is_err=False).then_inc(gathered, 16)

        @block.tensor
        def _(pe):
            pe.wait_ge(loaded, 48)
            with pe.Fori(0, GROUPS) as i:
                h_t = w["hT"][:, bass.ds(i * (Q4 * P), Q4 * P)]
                for k in range(KF):
                    if k < 2:
                        pe.wait_ge(g_done, i * KF)
                    else:
                        pe.wait_ge(g_done, i * KF + k - 1)
                    pe.matmul(p_a[k % 2][:, :], w1[:, P * k:P * k + P], h_t, start=True, stop=True).then_inc(a_done, 1)
                    pe.matmul(p_b[k % 2][:, :], w3[:, P * k:P * k + P], h_t, start=True, stop=True).then_inc(b_done, 1)
                pe.wait_ge(g_done, i * KF + KF)
                pe.wait_ge(summed, i)
                for t in range(Q4):
                    for k in range(KF):
                        last = pe.matmul(p_y[0][:, P * t:P * t + P], g_t[:, k, P * t:P * t + P], w2[:, k, :],
                                         start=k == 0, stop=k == KF - 1)
                last.then_inc(y_done, 1)

        @block.scalar
        def _(act):
            with act.Fori(0, GROUPS) as i:
                for k in range(KF):
                    act.wait_ge(a_done, i * KF + k + 1)
                    act.wait_ge(g_done, i * KF)
                    act.activation(act_a[:, k, :], p_a[k % 2][:, :], ACT.Silu).then_inc(silu_done, 1)

        @block.vector
        def _(ve):
            for q in range(Q4):
                for c in range(2):
                    ve.memset(rows[q][c][:, :], 0.0).then_inc(cleared, 1)
            PER = 2 * Q4 + 1
            with ve.Fori(0, GROUPS) as i:
                own = Tally(ve, vec_own, i * PER)
                ve.wait_ge(gathered, i * (32 * Q4))
                for q in range(Q4):
                    for c in range(2):
                        ve.tensor_copy(ix[q][c][:, :], w["slot"][:, bass.ds(i * Q4 + q, 1), c]).then_inc(staged, 1)
                for k in range(KF):
                    ve.wait_ge(silu_done, i * KF + k + 1)
                    ve.wait_ge(b_done, i * KF + k + 1)
                    ve.wait_ge(y_done, i)
                    ve.tensor_tensor(g_t[:, k, :], act_a[:, k, :], p_b[k % 2][:, :], ALU.mult).then_inc(g_done, 1)
                ve.wait_ge(y_done, i + 1)
                part = w["rest"][:, bass.ds(i * Q4, Q4), :]
                own.did(ve.tensor_tensor(part, part, p_y[0][:, :].rearrange("p (t d) -> p t d", t=Q4), ALU.add))
                ve.wait_ge(vec_own, own.value())
                ve.wait_ge(gathered, i * (32 * Q4) + 32 * Q4)
                for c in range(2):
                    for q in range(Q4):
                        one = w["rest"][:, bass.ds(i * Q4 + q, 1), :].rearrange("p o d -> p (o d)")
                        own.did(ve.scalar_tensor_tensor(one, rows[q][c][:, :], w["gate"][:, c, bass.ds(i * Q4 + q, 1)],
                                                        one, ALU.mult, ALU.add))
                    ve.wait_ge(vec_own, own.value())
                ve.memset(ix[0][0][:, :], 0).then_inc(summed, 1)
                ve.wait_ge(summed, i + 1)
                assert own.n == PER


def last_norm(nc, a, s, w, out):
    with ExitStack() as ctx:
        def sb(name, shape):
            return ctx.enter_context(nc.sbuf_tensor("ln_" + name, shape, F32))

        def sem(name):
            return signal(nc, s, "ln_" + name)

        square = sb("square", [P, TILES, D])
        mean, var, inv = sb("mean", [P, TILES]), sb("var", [P, TILES]), sb("inv", [P, TILES])
        vec_own, act_own, requested, rooted, stored = (sem(x) for x in ("vec_own", "act_own", "requested", "rooted", "stored"))
        block = ctx.enter_context(nc.Block())
        STEPS = 6

        @block.scalar
        def _(act):
            inverse_roots(act, act_own, requested, rooted, inv[:, :], 1)

        @block.vector
        def _(ve):
            own = Tally(ve, vec_own)
            layer_norm(ve, own, rooted, requested, w["rest"][:, :, :], w["rest"][:, :, :],
                       (mean[:, :], var[:, :], inv[:, :]), square[:, :, :], 0)
            assert own.n == STEPS, own.n

        @block.sync
        def _(sp):
            sp.wait_ge(vec_own, STEPS)
            sp.dma_start(out.rearrange("b (q p) d -> p (b q) d", p=P), w["rest"][:, :, :]).then_inc(stored, 16)
            sp.wait_ge(stored, 16)


def apart(eng, passed):
    eng.sem_inc(passed, 1)


def signal(nc, s, name):
    s["signals"].append(nc.alloc_semaphore(name=name))
    return s["signals"][-1]


def phase(nc, a, s, body, *more):
    s["signals"] = []
    body(nc, a, s, *more)
    nc.clear_and_free_semaphores(s["signals"])
    nc.all_engine_barrier()


def build(nc, a, s, out, stop=9, start=0):
    if start < 1:
        phase(nc, a, s, token_scalars)
    if stop > 1 and start < 2:
        phase(nc, a, s, within_chunks)
    if stop > 2 and start < 3:
        phase(nc, a, s, across_chunks)
    if stop > 3:
        with ExitStack() as ctx:
            def sb(name, shape, dt=F32):
                return ctx.enter_context(nc.sbuf_tensor(name, shape, dt))

            w = {"rest": sb("rest", [P, TILES, D]), "h": sb("h", [P, TILES, D]),
                 "gate": sb("gate", [P, 2, TILES]), "slot": sb("slot", [P, TILES, 2], U32)}
            with nc.sbuf_tensor("zeros", [P, ROWS // P, D], F32) as zeros:
                w["zeros"] = zeros
                phase(nc, a, s, after_attention, w)
                phase(nc, a, s, norms, w)
            w["hT"] = sb("hT", [P, N_TOK])
            phase(nc, a, s, routing, w)
            phase(nc, a, s, dispatch, w)
            phase(nc, a, s, experts, w)
            phase(nc, a, s, shared_and_sum, w)
            phase(nc, a, s, last_norm, w, out)


_INS = ["L0_attn_" + n for n in ("hidden_states", "Wq", "Wk", "Wv", "Wbeta", "Wtg", "mode_logits", "log_decay",
                                 "omega_log_scale", "Wg", "Wo")] + \
       ["L0_ffn_" + n for n in ("ln_g", "ln_b", "Wr", "W1", "W3", "W2", "W1s", "W3s", "W2s")]


def kernel(**inputs):
    import numpy as _np
    import concourse.bacc as _bacc
    from concourse import mybir as _mybir
    from concourse.bass_utils import run_bass_kernel_spmd as _run

    nc = _bacc.Bacc("TRN2", target_bir_lowering=False, num_devices=1)
    arrays, args = {}, {}
    named = {n.split("_", 2)[2]: _np.ascontiguousarray(inputs[n]) for n in _INS}
    named["x"] = named.pop("hidden_states")
    named.update(constants())
    for name, value in named.items():
        arrays[f"in_{name}_dram"] = value
        args[name] = nc.dram_tensor(f"in_{name}_dram", value.shape, _mybir.dt.from_np(value.dtype), kind="ExternalInput").ap()
    out = nc.dram_tensor("out_0_dram", (B, T, D), F32, kind="ExternalOutput").ap()
    build(nc, args, scratch(nc), out)
    r = _run(nc, [arrays], core_ids=[0])
    return r.results[0]["out_0_dram"]
```

```python
from contextlib import ExitStack

import numpy as np

import concourse.bass as bass
from concourse import mybir

F32 = mybir.dt.float32
U32 = mybir.dt.uint32
ALU = mybir.AluOpType
ACT = mybir.ActivationFunctionType
AX = mybir.AxisListType

B, T, D = 16, 512, 128
H, DK, M = 8, 64, 8
N_TOK = B * T
P = 128
C = 32
NCH = T // C
LO = P // C
HI = M // LO
HP = H * HI
GB = P // HP
NG = B // GB
TILES = N_TOK // P
FF, E_R, CAP = 512, 7, 366
CAPP = 3 * P
ROWS = E_R * CAPP
HALF = DK // 2
LN_EPS = 1e-5
MASKED = -1e4
MAGIC = 12582912.0
TWO_PI_A, TWO_PI_B = 6.28125, 0.0019350051879882812
TWO_PI_C = float(2 * np.pi - TWO_PI_A - TWO_PI_B)
PI_SAFE = 3.1415925


class Tally:

    def __init__(self, eng, sem, base=0):
        self.eng, self.sem, self.base, self.n = eng, sem, base, 0

    def did(self, instruction):
        instruction.then_inc(self.sem, 1)
        self.n += 1

    def value(self):
        return self.base + self.n


def constants():
    p = np.arange(P)
    f = np.float32
    return {
        "ident": np.eye(P, dtype=f),
        "fold": (p[:, None] % C == np.arange(C)[None]).astype(f),
        "pick": (p[:, None] % HI == p[None] // DK).astype(f),
        "own": (p[:, None] // HI == np.arange(P // HI)[None]).astype(f),
        "causal": np.broadcast_to(np.where(np.arange(C)[None] <= np.arange(C)[:, None], 0, MASKED)
                                  .astype(f).reshape(1, C * C), (P, C * C)).copy(),
        "pos": (C * np.arange(NCH)[None] + p[:, None] % C).astype(f),
        "freq": np.broadcast_to((f(1.0) / f(10000.0) ** (np.arange(0, DK, 2, dtype=f) / f(DK)))
                                .astype(f)[None], (P, HALF)).copy(),
        "before": (p[:, None] < p[None]).astype(f),
        "lane": np.broadcast_to(np.arange(8, dtype=f)[None], (P, 8)).copy(),
    }


def scratch(nc):
    def dram(name, shape):
        return nc.dram_tensor(name, shape, F32, kind="Internal").ap()

    return {
        "scal": dram("scal", (4, B, H * M, T)),
        "tab": dram("tab", (NCH, P, 2 * HP * HALF)),
        "kd": dram("kd", (NG * NCH * GB, P, HP * DK)),
        "qd": dram("qd", (NG * NCH * GB, P, 2 * H * LO * C)),
        "od": dram("od", (NG * NCH, P, GB * HP * 2 * C)),
        "gd": dram("gd", (NG * NCH, P, GB * 3 * HP)),
        "sd": dram("sd", (NG * NCH, P, GB * H * LO)),
        "oo": dram("oo", (N_TOK, H * DK)),
        "xT": dram("xT", (D, N_TOK)),
        "xe": dram("xe", (ROWS, D)),
        "ye": dram("ye", (ROWS, D)),
    }


def token_scalars(nc, a, s):
    with ExitStack() as ctx:
        def sb(name, shape):
            return ctx.enter_context(nc.sbuf_tensor("ts_" + name, shape, F32))

        def ps(name, shape):
            return ctx.enter_context(nc.psum_tensor("ts_" + name, shape, F32))

        def sem(name):
            return signal(nc, s, "ts_" + name)

        def two(name):
            return [sem(name + "0"), sem(name + "1")]

        assert NCH == B
        Q = T // P
        HM, NA = H * M, HP * HALF
        ident = sb("ident", [P, P])
        wq, wk, wz = sb("wq", [P, H * DK]), sb("wk", [P, H * DK]), sb("wz", [P, 2 * HM])
        decay, modes = sb("decay", [P, HM]), sb("modes", [P, HM])
        row_a, row_b, row_h = sb("row_a", [P, HM]), sb("row_b", [P, HM]), sb("row_h", [P, H])
        ln_rho, ln_w = sb("ln_rho", [P, HM]), sb("ln_w", [P, HM])
        x_in, x_t = sb("x_in", [P, Q, D]), sb("x_t", [P, Q * P])
        sq = [sb(f"sq{p}", [P, 2, H * DK]) for p in range(2)]
        ss, ln_s = sb("ss", [P, Q, 2 * H]), sb("ln_s", [P, Q, 2 * H])
        zz, ez, nl = (sb(x, [P, Q, 2 * HM]) for x in ("zz", "ez", "nl"))
        v, v_t = sb("v", [P, Q, 4, HM]), sb("v_t", [P, 2, T])
        p_x, p_z = ps("p_x", [P, 512]), ps("p_z", [P, 512])
        p_q, p_k, p_v = ([ps(f"{n}{p}", [P, 512]) for p in range(2)] for n in ("p_q", "p_k", "p_v"))
        om, pos, freq = sb("om", [P, HP]), sb("pos", [P, NCH]), sb("freq", [P, HALF])
        at, r = sb("at", [P, HP]), sb("r", [P, 2 * NA])
        ang, turns = [sb(f"ang{p}", [P, NA]) for p in range(2)], [sb(f"turns{p}", [P, 2 * NA]) for p in range(2)]
        tables = sb("tables", [P, NCH, 2 * NA])

        loaded, mode_ready, mode_exp = sem("loaded"), sem("mode_ready"), sem("mode_exp")
        x_loaded, x_turned, x_copied, xt_stored = (sem(x) for x in ("x_loaded", "x_turned", "x_copied", "xt_stored"))
        projected, squared, summed = two("projected"), two("squared"), two("summed")
        z_done, z_taken, sums_ready = sem("z_done"), sem("z_taken"), sem("sums_ready")
        logged, valued, v_turned, v_copied, v_stored = (
            sem(x) for x in ("logged", "valued", "v_turned", "v_copied", "v_stored"))
        act_own, vec_own, pool_own, po_passed = (sem(x) for x in ("act_own", "vec_own", "pool_own", "po_passed"))
        pos_loaded, omega_ready, sines, tab_stored, tab_own = (
            sem(x) for x in ("pos_loaded", "omega_ready", "sines", "tab_stored", "tab_own"))
        counted, reduced = two("counted"), two("reduced")
        block = ctx.enter_context(nc.Block())

        def groups(eng, body):
            body(0, False, True)
            with eng.Fori(1, B - 1) as i:
                body(i, True, True)
            body(B - 1, True, False)

        @block.sync
        def _(sp):
            sp.dma_start(ident[:, :], a["ident"]).then_inc(loaded, 16)
            x_v = a["x"].rearrange("b (q p) d -> b p q d", p=P)
            sp.dma_start(x_in[:, :, :], x_v[0]).then_inc(x_loaded, 16)
            for dst, src in ((wq[:, :], a["Wq"]), (wk[:, :], a["Wk"]),
                             (wz[:, 0:HM], a["Wtg"]), (wz[:, HM:], a["Wbeta"]),
                             (decay[:, :], a["log_decay"].rearrange("h m -> (h m)").partition_broadcast(P)),
                             (modes[:, :], a["mode_logits"].rearrange("h m -> (h m)").partition_broadcast(P))):
                sp.dma_start(dst, src).then_inc(loaded, 16)
            logs = a["omega_log_scale"].rearrange("h (i l) -> h i l", i=HI)
            for lo in range(LO):
                sp.dma_start(om[C * lo:C * lo + C, :],
                             logs[:, :, lo].rearrange("h i -> (h i)").partition_broadcast(C), allow_slow_non_contiguous=True).then_inc(pos_loaded, 16)
            sp.dma_start(pos[:, :], a["pos"]).then_inc(pos_loaded, 16)
            sp.dma_start(freq[:, :], a["freq"]).then_inc(pos_loaded, 16)

            def store_scalars(b):
                sp.wait_ge(v_copied, b + 1)
                for k in range(4):
                    sp.dma_start(s["scal"][k, b], v_t[HM * (k % 2):HM * (k % 2) + HM, k // 2, :]).then_inc(v_stored, 16)

            def group(i, before, after):
                if after:
                    sp.wait_ge(x_turned, i + 1)
                    sp.dma_start(x_in[:, :, :], x_v[i + 1]).then_inc(x_loaded, 16)
                sp.wait_ge(x_copied, i + 1)
                sp.dma_start(s["xT"][:, bass.ds(i * T, T)], x_t[:, :]).then_inc(xt_stored, 16)
                if before:
                    store_scalars(i - 1)

            groups(sp, group)
            store_scalars(B - 1)
            with sp.Fori(0, NCH) as j:
                sp.wait_ge(sines, j + 1)
                sp.dma_start(s["tab"][j], tables[:, bass.ds(j, 1), :].rearrange("p o x -> p (o x)")).then_inc(tab_stored, 16)
            sp.wait_ge(v_stored, 64 * B)
            sp.wait_ge(xt_stored, 16 * B)
            sp.wait_ge(tab_stored, 16 * NCH)

        @block.tensor
        def _(pe):
            pe.wait_ge(loaded, 16 * 7)

            def turn_x(i):
                pe.wait_ge(x_loaded, i * 16 + 16)
                pe.wait_ge(x_copied, i)
                for t in range(Q):
                    last = pe.transpose(p_x[:, P * t:P * t + P], x_in[:, t, :], ident[:, :])
                last.then_inc(x_turned, 1)

            def turn_scalars(i):
                pe.wait_ge(valued, i + 1)
                pe.wait_ge(v_copied, i)
                for k in range(2):
                    for t in range(Q):
                        last = pe.transpose(p_v[k][:, P * t:P * t + P], v[:, t, 2 * k:2 * k + 2, :].rearrange("p k m -> p (k m)"), ident[:, :])
                last.then_inc(v_turned, 1)

            def group(i, before, after):
                pe.wait_ge(x_copied, i + 1)
                for t in range(Q):
                    p = t % 2
                    pe.wait_ge(squared[p], i * (Q // 2) + t // 2)
                    x = x_t[:, P * t:P * t + P]
                    pe.matmul(p_q[p][:, :], x, wq[:, :], start=True, stop=True)
                    pe.matmul(p_k[p][:, :], x, wk[:, :], start=True, stop=True).then_inc(projected[p], 1)
                pe.wait_ge(z_taken, i)
                for t in range(Q):
                    last = pe.matmul(p_z[:, P * t:P * t + P], x_t[:, P * t:P * t + P], wz[:, :], start=True, stop=True)
                last.then_inc(z_done, 1)
                if after:
                    turn_x(i + 1)
                if before:
                    turn_scalars(i - 1)

            turn_x(0)
            groups(pe, group)
            turn_scalars(B - 1)

        @block.scalar
        def _(act):
            act.wait_ge(pos_loaded, 16 * 6)
            act.activation(om[:, :], om[:, :], ACT.Exp).then_inc(omega_ready, 1)
            act.wait_ge(loaded, 16 * 7)
            act.activation(row_a[:, :], decay[:, :], ACT.Exp).then_inc(act_own, 1)
            act.wait_ge(act_own, 1)
            act.activation(ln_rho[:, :], row_a[:, :], ACT.Ln, bias=1.0).then_inc(mode_exp, 1)
            act.wait_ge(mode_ready, 1)
            act.activation(row_b[:, :], modes[:, :], ACT.Exp).then_inc(mode_exp, 1)
            act.wait_ge(mode_ready, 2)
            act.activation(ln_w[:, :], row_a[:, :], ACT.Ln).then_inc(mode_exp, 1)

            def logarithms(i):
                act.wait_ge(sums_ready, i + 1)
                act.wait_ge(valued, i)
                act.activation(ez[:, :, :], zz[:, :, :], ACT.Exp).then_inc(act_own, 1)
                act.activation(ln_s[:, :, :], ss[:, :, :], ACT.Ln)
                act.wait_ge(act_own, i + 2)
                act.activation(nl[:, :, :], ez[:, :, :], ACT.Ln, bias=1.0).then_inc(logged, 1)

            def copy_scalars(i):
                act.wait_ge(v_turned, i + 1)
                act.wait_ge(v_stored, i * 64)
                for k in range(2):
                    last = act.activation(v_t[:, k, :], p_v[k][:, :], ACT.Copy)
                last.then_inc(v_copied, 1)

            def group(i, before, after):
                act.wait_ge(x_turned, i + 1)
                act.wait_ge(z_done, i)
                act.wait_ge(xt_stored, i * 16)
                act.activation(x_t[:, :], p_x[:, :], ACT.Copy).then_inc(x_copied, 1)
                if before:
                    logarithms(i - 1)
                for t in range(Q):
                    p = t % 2
                    act.wait_ge(projected[p], i * (Q // 2) + t // 2 + 1)
                    act.wait_ge(summed[p], i * (Q // 2) + t // 2)
                    act.activation(sq[p][:, 0, :], p_q[p][:, :], ACT.Square)
                    act.activation(sq[p][:, 1, :], p_k[p][:, :], ACT.Square).then_inc(squared[p], 1)
                if before:
                    copy_scalars(i - 1)

            groups(act, group)
            logarithms(B - 1)
            copy_scalars(B - 1)
            for p in range(2):
                act.wait_ge(reduced[p], NCH // 2)
            with act.Fori(0, NCH) as j:
                row = tables[:, bass.ds(j, 1), :]
                act.activation(row, row, ACT.Sin).then_inc(sines, 1)

        @block.vector
        def _(ve):
            own = Tally(ve, vec_own)
            ve.wait_ge(loaded, 16 * 7)
            m3 = modes[:, :].rearrange("p (h m) -> p h m", h=H)
            own.did(ve.tensor_reduce(row_h[:, :], m3, AX.X, ALU.max))
            ve.wait_ge(vec_own, own.value())
            ve.tensor_tensor(m3, m3, row_h[:, :].unsqueeze(2).broadcast_to([P, H, M]), ALU.subtract).then_inc(mode_ready, 1)
            ve.wait_ge(mode_exp, 2)
            b3 = row_b[:, :].rearrange("p (h m) -> p h m", h=H)
            own.did(ve.tensor_reduce(row_h[:, :], b3, AX.X, ALU.add))
            ve.wait_ge(vec_own, own.value())
            own.did(ve.reciprocal(row_h[:, :], row_h[:, :]))
            ve.wait_ge(vec_own, own.value())
            own.did(ve.tensor_tensor(b3, b3, row_h[:, :].unsqueeze(2).broadcast_to([P, H, M]), ALU.mult))
            ve.wait_ge(vec_own, own.value())
            ve.tensor_scalar(row_a[:, :], row_b[:, :], DK ** -0.5, 1e-18, ALU.mult, ALU.max).then_inc(mode_ready, 1)
            ve.wait_ge(mode_exp, 3)
            setup = own.value()
            VALUES, REDUCE = 5, 4
            split = lambda x: x.rearrange("p t (h m) -> p t h m", h=H)
            per_mode = lambda x: x.unsqueeze(3).broadcast_to([P, Q, H, M])

            def values(i, base):
                own = Tally(ve, vec_own, base)
                ve.wait_ge(logged, i + 1)
                ve.wait_ge(v_turned, i)
                own.did(ve.tensor_tensor(v[:, :, 0, :], nl[:, :, 0:HM], ln_rho[:, :].unsqueeze(1).broadcast_to([P, Q, HM]), ALU.add))
                own.did(ve.tensor_scalar(split(v[:, :, 2, :]), per_mode(ln_s[:, :, H:2 * H]), -0.5, None, ALU.mult))
                own.did(ve.tensor_scalar(split(v[:, :, 3, :]), per_mode(ln_s[:, :, 0:H]), -0.5, None, ALU.mult))
                ve.wait_ge(vec_own, own.value())
                own.did(ve.tensor_scalar(v[:, :, 0, :], v[:, :, 0, :], -1.0, float(np.log(1e-6)), ALU.mult, ALU.max))
                own.did(ve.tensor_tensor(v[:, :, 1, :], v[:, :, 2, :], nl[:, :, HM:], ALU.subtract))
                ve.tensor_tensor(v[:, :, 3, :], v[:, :, 3, :], ln_w[:, :].unsqueeze(1).broadcast_to([P, Q, HM]), ALU.add).then_inc(valued, 1)
                assert own.n == VALUES

            def group(i, before, after):
                if before:
                    values(i - 1, setup + (i - 1) * VALUES)
                for t in range(Q):
                    p = t % 2
                    ve.wait_ge(squared[p], i * (Q // 2) + t // 2 + 1)
                    if t == 0:
                        ve.wait_ge(logged, i)
                    ve.tensor_reduce(ss[:, t, :], sq[p][:, :, :].rearrange("p x (h d) -> p (x h) d", d=DK),
                                     AX.X, ALU.add).then_inc(summed[p], 1)
                ve.wait_ge(z_done, i + 1)
                ve.tensor_scalar(zz[:, :, :].rearrange("p t z -> p (t z)"), p_z[:, :], -1.0, 40.0, ALU.mult, ALU.min).then_inc(z_taken, 1)
                for p in range(2):
                    ve.wait_ge(summed[p], i * (Q // 2) + Q // 2)
                ve.tensor_scalar(ss[:, :, :], ss[:, :, :], 1e-6, None, ALU.add).then_inc(sums_ready, 1)

            def reduce_angles(half, p):
                own = Tally(ve, tab_own, (half * 2 + p) * REDUCE)

                def step(instruction):
                    own.did(instruction)
                    ve.wait_ge(tab_own, own.value())

                ve.wait_ge(counted[p], half + 1)
                r3, n3 = (x[:, :].rearrange("p (c f) -> p c f", c=2) for x in (r, turns[p]))
                step(ve.scalar_tensor_tensor(r3, n3, -TWO_PI_A, ang[p][:, :].unsqueeze(1).broadcast_to([P, 2, NA]),
                                             ALU.mult, ALU.add))
                step(ve.scalar_tensor_tensor(r[:, :], turns[p][:, :], -TWO_PI_B, r[:, :], ALU.mult, ALU.add))
                step(ve.scalar_tensor_tensor(r[:, :], turns[p][:, :], -TWO_PI_C, r[:, :], ALU.mult, ALU.add))
                step(ve.tensor_scalar(r[:, 0:NA], r[:, 0:NA], float(np.pi / 2), None, ALU.add))
                ve.tensor_scalar(tables[:, bass.ds(half * 2 + p, 1), :].rearrange("p o x -> p (o x)"), r[:, :],
                                 PI_SAFE, -PI_SAFE, ALU.min, ALU.max).then_inc(reduced[p], 1)
                assert own.n == REDUCE, own.n

            group(0, False, True)
            reduce_angles(0, 0)
            with ve.Fori(0, B // 2 - 1) as half:
                for p in range(2):
                    group(half * 2 + p + 1, True, True)
                    reduce_angles(half + p, 1 - p)
            group(B - 1, True, False)
            reduce_angles(NCH // 2 - 1, 1)
            values(B - 1, setup + (B - 1) * VALUES)

        @block.gpsimd
        def _(po):
            po.wait_ge(omega_ready, 1)
            po.wait_ge(pos_loaded, 16 * 6)
            PER = 5
            with po.Fori(0, NCH // 2) as half:
                for p in range(2):
                    own = Tally(po, pool_own, (half * 2 + p) * PER)

                    def step(instruction):
                        own.did(instruction)
                        po.wait_ge(pool_own, own.value())
                        apart(po, po_passed)

                    step(po.tensor_tensor(at[:, :], om[:, :], pos[:, bass.ds(half * 2 + p, 1)].broadcast_to([P, HP]), ALU.mult))
                    po.wait_ge(reduced[p], half)
                    step(po.tensor_tensor(ang[p][:, :].rearrange("p (m f) -> p m f", f=HALF),
                                          at[:, :].unsqueeze(2).broadcast_to([P, HP, HALF]),
                                          freq[:, :].unsqueeze(1).broadcast_to([P, HP, HALF]), ALU.mult))
                    own.did(po.tensor_scalar(turns[p][:, 0:NA], ang[p][:, :], 1 / (2 * np.pi), 0.25, ALU.mult, ALU.add))
                    step(po.tensor_scalar(turns[p][:, NA:], ang[p][:, :], 1 / (2 * np.pi), None, ALU.mult))
                    step(po.tensor_scalar(turns[p][:, :], turns[p][:, :], MAGIC, None, ALU.add))
                    po.tensor_scalar(turns[p][:, :], turns[p][:, :], MAGIC, None, ALU.subtract).then_inc(counted[p], 1)
                    assert own.n == PER, own.n


def sooner(pair, p, r):
    return (pair[1], r) if p == 0 else (pair[0], r + 1)


def within_chunks(nc, a, s):
    with ExitStack() as ctx:
        def sb(name, shape):
            return ctx.enter_context(nc.sbuf_tensor("wc_" + name, shape, F32))

        def ps(name, shape):
            return ctx.enter_context(nc.psum_tensor("wc_" + name, shape, F32))

        def sem(name):
            return signal(nc, s, "wc_" + name)

        def two(name):
            return [sem(name + "0"), sem(name + "1")]

        ident, own_bh, pick = sb("ident", [P, P]), sb("own_bh", [P, P // HI]), sb("pick", [P, P])
        causal = sb("causal", [P, C, C])
        wq, wk = sb("wq", [P, H * DK]), sb("wk", [P, H * DK])
        tab = sb("tab", [P, 2, H, HI, HALF])
        x_r = [sb(f"x_r{p}", [P, LO, C]) for p in range(2)]
        q_s = sb("q_s", [P, H, 2, HALF])
        k_rot = [sb(f"k_rot{p}", [P, H, HI, 2, HALF]) for p in range(2)]
        q_rot = sb("q_rot", [P, H, HI, 2, HALF])
        k_tmp, q_tmp = sb("k_tmp", [P, 2, H, HI, HALF]), sb("q_tmp", [P, 2, H, HI, HALF])
        kq_t = [sb(f"kq_t{p}", [P, 2, H, LO, C]) for p in range(2)]
        kq = sb("kq", [P, P, 2 * C])
        solved = sb("solved", [P, P, 2, C])
        raw = sb("raw", [P, 2, C, LO, C])
        ea, ep = sb("ea", [P, C, LO, C]), sb("ep", [P, C, LO, C])
        scal = sb("scal", [P, 4, LO, C])
        cg, cs = sb("cg", [P, LO, C]), sb("cs", [P, LO, C])
        sx = sb("sx", [P, 5, LO, C])
        g_c = sb("g_c", [P, LO])
        g_own = sb("g_own", [P, P // HI, LO])
        ones = sb("ones", [P, C])
        g_out = sb("g_out", [P, GB, 3, HP])
        d_out = sb("d_out", [P, GB * H * LO])
        p_k, p_q = ps("p_k", [P, 512]), ps("p_q", [P, 512])
        p_t = [ps(f"p_t{i}", [P, 512]) for i in range(2)]
        p_c = [ps(f"p_c{i}", [P, 512]) for i in range(2)]
        p_kk = [ps(f"p_kk{i}", [P, 512]) for i in range(2)]

        loaded = sem("loaded")
        x_loaded, tab_loaded, scal_loaded = two("x_loaded"), sem("tab_loaded"), sem("scal_loaded")
        projected, q_copied, k_rotated, q_rotated = two("projected"), two("q_copied"), two("k_rotated"), two("q_rotated")
        kt_turned, qt_turned, kt_copied, qt_copied = (two(x) for x in ("kt_turned", "qt_turned", "kt_copied", "qt_copied"))
        products, products_copied = two("products"), two("products_copied")
        k_stored, kq_stored = two("k_stored"), two("kq_stored")
        chain_turned, chain_copied = sem("chain_turned"), sem("chain_copied")
        exponents, exps, small_exps = (sem(x) for x in ("exponents", "exps", "small_exps"))
        vec_rot, vec_own, pool_rot, pool_setup, vec_solved, pool_solved = (
            sem(x) for x in ("vec_rot", "vec_own", "pool_rot", "pool_setup", "vec_solved", "pool_solved"))
        a_ready, queries_ready, t_started, scaled_ready, gown_ready = (
            sem(x) for x in ("a_ready", "queries_ready", "t_started", "scaled_ready", "gown_ready"))
        t_negated = sem("t_negated")
        solved_stored, g_stored = sem("solved_stored"), sem("g_stored")
        pe_passed = sem("pe_passed")
        block = ctx.enter_context(nc.Block())

        GROUPS = NG * NCH
        PAIRS = GB // 2
        IN_BANKS = 2 * C // 4
        G_BANKS = 2
        FORM_BANKS = C // 4
        BANKS = IN_BANKS + G_BANKS + 2 * FORM_BANKS
        SPLIT = 3
        SLICE_BANKS = [range(0, 8), range(0), range(16, 20), range(20, 23), range(23, 26), range(26, 29),
                       range(29, 32), range(32, 34)]
        TAIL_BANKS = range(8, 16)
        BACK = [(0, 0), (1, 0), (0, 1), (0, 2), (1, 1), (0, 3), (0, 4), (1, 2), (0, 5), (0, 6), (1, 3),
                (0, 7), (1, 4), (1, 5), (1, 6), (1, 7)]
        SLICE_SCALED = [range(0), range(0), range(0, 1), range(1, 2), range(2, 3), range(3, 4), range(4, 6), range(6, 8)]
        SLICE_ROWS = [range(0), range(1, 5), range(5, 10), range(10, 14), range(14, 18), range(18, 23),
                      range(23, C - 1), range(0)]
        ROWS_SOLVED = C - 2
        solved_after = [sum(len(rows) for rows in SLICE_ROWS[:k + 1]) for k in range(GB)]

        def grouped(eng, turn, chain_slice, last=None, tail=None):
            for k in range(GB):
                turn(0, k, first=k == 0)
            with eng.Fori(1, GROUPS) as grp:
                for k in range(GB):
                    turn(grp, k, chain=lambda: chain_slice(grp - 1, k))
                    if tail and k == 0:
                        tail(grp - 1)
            if last:
                last()
            for k in range(GB):
                chain_slice(GROUPS - 1, k)
                if tail and k == 0:
                    tail(GROUPS - 1)

        @block.sync
        def _(sp):
            for dst, src in ((ident[:, :], a["ident"]), (own_bh[:, :], a["own"]), (pick[:, :], a["pick"]),
                             (causal[:, :, :], a["causal"].rearrange("p (t s) -> p t s", t=C)),
                             (wq[:, :], a["Wq"]), (wk[:, :], a["Wk"])):
                sp.dma_start(dst, src).then_inc(loaded, 16)
            scal_v = s["scal"].rearrange("v (g b) (c l) t -> v g (b c) l t", g=NG, l=LO)

            def store_solved(grp, rows):
                for row in rows:
                    at = row * HP * 2 * C
                    sp.dma_start(s["od"][grp][:, at:at + HP * 2 * C],
                                 solved[:, row * HP:row * HP + HP, :, :].rearrange("p c x t -> p (c x t)")).then_inc(solved_stored, 16)

            def group(g, j, behind):
                grp = g * NCH + j
                for k in range(GB):
                    r, p = grp * PAIRS + k // 2, k % 2
                    sp.wait_ge(projected[p], r)
                    cols = s["xT"][:, bass.ds((g * GB + k) * T + j * C, C)]
                    sp.dma_start(x_r[p][:, :, :], cols.unsqueeze(1).broadcast_to([P, LO, C])).then_inc(x_loaded[p], 16)
                    if k == 1:
                        sp.wait_ge(k_rotated[1], grp * PAIRS)
                        sp.wait_ge(q_rotated[1], grp * PAIRS)
                        sp.dma_start(tab[:, :, :, :, :].rearrange("p x h i f -> p (x h i f)"), s["tab"][j]).then_inc(tab_loaded, 16)
                    if behind and k in (1, 2, 3):
                        if k == 1:
                            sp.wait_ge(chain_copied, (grp - 1) * BANKS)
                        store_solved(grp - 2, (range(0, 2), range(2, 5), range(5, 8))[k - 1])
                    if k == 5:
                        sp.wait_ge(small_exps, grp)
                        for v in range(4):
                            sp.dma_start(scal[:, v, :, :], scal_v[v, g, :, :, bass.ds(j * C, C)]).then_inc(scal_loaded, 16)

            group(0, 0, False)
            group(0, 1, False)
            for g in range(NG):
                with sp.Fori(0 if g else 2, NCH) as j:
                    group(g, j, True)
            for grp in (GROUPS - 2, GROUPS - 1):
                sp.wait_ge(chain_copied, (grp + 1) * BANKS)
                store_solved(grp, range(GB))

        @block.tensor
        def _(pe):
            pe.wait_ge(loaded, 16 * 6)
            pe.wait_ge(pool_setup, 1)

            def multiply(r, p):
                pe.wait_ge(kt_copied[p], r + 1)
                pe.wait_ge(qt_copied[p], r + 1)
                pe.wait_ge(*sooner(products_copied, p, r))
                apart(pe, pe_passed)
                for h in range(H):
                    for lo in range(LO):
                        for hi in range(HI):
                            rows = slice(DK * hi, DK * hi + DK)
                            last = pe.matmul(p_kk[hi][C * lo:C * lo + C, 2 * C * h:2 * C * h + 2 * C],
                                             kq_t[p][rows, 0, h, lo, :], kq_t[p][rows, :, h, lo, :],
                                             start=True, stop=True, tile_position=(DK * hi, C * lo))
                last.then_inc(products[p], 1)

            def turn(grp, k, first=False, chain=None):
                r, p = grp * PAIRS + k // 2, k % 2
                pe.wait_ge(x_loaded[p], r * 16 + 16)
                if not first:
                    pe.wait_ge(*sooner(k_rotated, p, r))
                    pe.wait_ge(*sooner(q_copied, p, r))
                rep = x_r[p][:, :, :].rearrange("p l t -> p (l t)")
                pe.matmul(p_q[:, :], rep, wq[:, :], start=True, stop=True)
                pe.matmul(p_k[:, :], rep, wk[:, :], start=True, stop=True).then_inc(projected[p], 1)
                if not first:
                    multiply(*((r, 0) if p else (r - 1, 1)))
                pe.wait_ge(k_rotated[p], r + 1)
                if not first:
                    pe.wait_ge(*sooner(qt_copied, p, r))
                for h in range(H):
                    last = pe.transpose(p_t[h // 4][:, P * (h % 4):P * (h % 4) + P],
                                        k_rot[p][:, h, :, :, :].rearrange("p i x f -> p (i x f)"), ident[:, :])
                last.then_inc(kt_turned[p], 1)
                if chain:
                    chain()
                pe.wait_ge(q_rotated[p], r + 1)
                pe.wait_ge(kt_copied[p], r + 1)
                for h in range(H):
                    last = pe.transpose(p_t[h // 4][:, P * (h % 4):P * (h % 4) + P],
                                        q_rot[:, h, :, :, :].rearrange("p i x f -> p (i x f)"), ident[:, :])
                last.then_inc(qt_turned[p], 1)

            def chain_slice(grp, k):
                turn_banks(grp, SLICE_BANKS[k])

            def turn_banks(grp, banks):
                for m in banks:
                    bank = p_c[m % 2]
                    if m == 0:
                        pe.wait_ge(products_copied[1], grp * PAIRS + PAIRS)
                    pe.wait_ge(chain_copied, grp * BANKS + max(m - 1, 0))
                    if m < IN_BANKS:
                        for i in range(4):
                            last = pe.transpose(bank[:, P * i:P * i + P], kq[:, :, 4 * m + i], ident[:, :])
                    elif m == IN_BANKS:
                        pe.wait_ge(small_exps, grp + 1)
                        for i in range(3):
                            last = pe.transpose(bank[:, P * i:P * i + P], sx[:, 2 + i, :, :].rearrange("p l t -> p (l t)"), ident[:, :])
                    elif m == IN_BANKS + 1:
                        pe.wait_ge(gown_ready, grp + 1)
                        last = pe.matmul(bank[:, 0:2 * P], pick[:, :], g_own[:, :, :].rearrange("p c l -> p (c l)"),
                                         start=True, stop=True)
                    else:
                        form, four = BACK[m - IN_BANKS - G_BANKS]
                        if form:
                            pe.wait_ge(scaled_ready, grp * FORM_BANKS + four + 1)
                        elif four == 0:
                            pe.wait_ge(queries_ready, grp + 1)
                        for i in range(4):
                            last = pe.transpose(bank[:, P * i:P * i + P],
                                                raw[:, 1 - form, 4 * four + i, :, :].rearrange("p l s -> p (l s)"), ident[:, :])
                    last.then_inc(chain_turned, 1)

            grouped(pe, turn, chain_slice, last=lambda: multiply(GROUPS * PAIRS - 1, 1),
                    tail=lambda grp: turn_banks(grp, TAIL_BANKS))

        @block.scalar
        def _(act):
            act.wait_ge(loaded, 16 * 6)

            def copy_products(grp, k):
                r, p = grp * PAIRS + k // 2, k % 2
                act.wait_ge(products[p], r + 1)
                for hi in range(HI):
                    last = act.activation(kq[:, HP * k + hi:HP * k + HP:HI, :],
                                          p_kk[hi][:, :].rearrange("p (h x) -> p h x", h=H), ACT.Copy)
                last.then_inc(products_copied[p], 1)

            def turn(grp, k, first=False, chain=None):
                r, p = grp * PAIRS + k // 2, k % 2
                act.wait_ge(projected[p], r + 1)
                if not first:
                    act.wait_ge(*sooner(q_rotated, p, r))
                act.activation(q_s[:, :, :, :].rearrange("p h x f -> p (h x f)"), p_q[:, :], ACT.Copy).then_inc(q_copied[p], 1)
                if k:
                    copy_products(grp, k - 1)
                elif not first:
                    copy_products(grp - 1, GB - 1)
                act.wait_ge(kt_turned[p], r + 1)
                act.wait_ge(products[p], r)
                act.wait_ge(kq_stored[p], r * 16)
                for i in range(2):
                    last = act.activation(kq_t[p][:, 0, 4 * i:4 * i + 4, :, :].rearrange("p h l t -> p (h l t)"),
                                          p_t[i][:, :], ACT.Copy)
                last.then_inc(kt_copied[p], 1)
                act.dma_start(s["kd"][grp * GB + k], k_rot[p][:, :, :, :, :].rearrange("p h i x f -> p (h i x f)")).then_inc(k_stored[p], 16)
                if chain:
                    chain()
                act.wait_ge(qt_turned[p], r + 1)
                for i in range(2):
                    last = act.activation(kq_t[p][:, 1, 4 * i:4 * i + 4, :, :].rearrange("p h l t -> p (h l t)"),
                                          p_t[i][:, :], ACT.Copy)
                last.then_inc(qt_copied[p], 1)
                act.wait_ge(qt_copied[p], r + 1)
                act.wait_ge(kt_copied[p], r + 1)
                act.dma_start(s["qd"][grp * GB + k], kq_t[p][:, :, :, :, :].rearrange("p x h l t -> p (x h l t)")).then_inc(kq_stored[p], 16)

            def copy_banks(grp, banks):
                for m in banks:
                    bank = p_c[m % 2]
                    act.wait_ge(chain_turned, grp * BANKS + m + 1)
                    if m < IN_BANKS:
                        last = act.activation(raw[:, m // 8, 4 * (m % 8):4 * (m % 8) + 4, :, :].rearrange("p t l s -> p (t l s)"),
                                              bank[:, :], ACT.Copy)
                    elif m == IN_BANKS:
                        act.wait_ge(g_stored, grp * 32)
                        last = act.activation(g_out[:, :, :, :].rearrange("p b x c -> p x b c"),
                                              bank[:, 0:3 * P].rearrange("p (x b c) -> p x b c", x=3, b=GB), ACT.Copy)
                    elif m == IN_BANKS + 1:
                        last = act.activation(d_out[:, :], bank[:, 0:2 * P], ACT.Copy)
                    else:
                        form, four = BACK[m - IN_BANKS - G_BANKS]
                        if m == IN_BANKS + G_BANKS:
                            act.wait_ge(solved_stored, grp * 16 * GB)
                        last = act.activation(solved[:, :, form, 4 * four:4 * four + 4], bank[:, :].rearrange("p (t c) -> p c t", t=4), ACT.Copy)
                    last.then_inc(chain_copied, 1)

            def tail(grp):
                copy_banks(grp, TAIL_BANKS)
                act.wait_ge(exponents, grp * 2 + 1)
                act.activation(ea[:, :, :, :].rearrange("p t l s -> p (t l s)"),
                               ea[:, :, :, :].rearrange("p t l s -> p (t l s)"), ACT.Exp).then_inc(exps, 1)

            def chain_slice(grp, k):
                copy_banks(grp, SLICE_BANKS[k])
                if k == 1:
                    act.wait_ge(exponents, grp * 2 + 2)
                    act.activation(ep[:, :, :, :].rearrange("p t l s -> p (t l s)"),
                                   ep[:, :, :, :].rearrange("p t l s -> p (t l s)"), ACT.Exp).then_inc(exps, 1)
                    act.activation(sx[:, :, :, :].rearrange("p k l t -> p (k l t)"),
                                   sx[:, :, :, :].rearrange("p k l t -> p (k l t)"), ACT.Exp)
                    act.activation(g_c[:, :], cg[:, :, C - 1], ACT.Exp).then_inc(small_exps, 1)
                    act.wait_ge(a_ready, grp + 1)
                    act.activation(ea[:, :, :, :].rearrange("p t l s -> p (t l s)"),
                                   raw[:, 0, :, :, :].rearrange("p t l s -> p (t l s)"), ACT.Copy, scale=-1.0).then_inc(t_negated, 1)
                if k == 2:
                    act.wait_ge(chain_copied, grp * BANKS + IN_BANKS + G_BANKS)
                    act.dma_start(s["gd"][grp], g_out[:, :, :, :].rearrange("p b x c -> p (b x c)")).then_inc(g_stored, 16)
                    act.dma_start(s["sd"][grp], d_out[:, :]).then_inc(g_stored, 16)

            grouped(act, turn, chain_slice, last=lambda: copy_products(GROUPS - 1, GB - 1), tail=tail)
            for p in range(2):
                act.wait_ge(k_stored[p], 16 * GROUPS * PAIRS)
                act.wait_ge(kq_stored[p], 16 * GROUPS * PAIRS)
            act.wait_ge(solved_stored, 16 * GB * GROUPS)
            act.wait_ge(g_stored, 32 * GROUPS)

        def rotate(eng, own, src, dst, tmp, done):
            for x in range(2):
                own.did(eng.tensor_tensor(dst[:, :, :, x, :], src[:, :, x, :].unsqueeze(2).broadcast_to([P, H, HI, HALF]),
                                          tab[:, 0, :, :, :], ALU.mult))
                own.did(eng.tensor_tensor(tmp[:, x, :, :, :], src[:, :, 1 - x, :].unsqueeze(2).broadcast_to([P, H, HI, HALF]),
                                          tab[:, 1, :, :, :], ALU.mult))
            eng.wait_ge(own.sem, own.value())
            for x, op in ((0, ALU.add), (1, ALU.subtract)):
                last = eng.tensor_tensor(dst[:, :, :, x, :], dst[:, :, :, x, :], tmp[:, x, :, :, :], op)
            last.then_inc(done, 1)

        def solve(eng, sem, grp, rows, los, tmp):
            n = los.stop - los.start
            own = Tally(eng, sem, grp * 2 * ROWS_SOLVED + 2 * (rows.start - 1))
            for i in rows:
                below = C - 1 - i
                part = tmp[:, :, :, :, :].rearrange("p x h i f -> p (x h i f)")[:, 0:below * n * i]
                part = part.rearrange("p (t l s) -> p t l s", t=below, l=n)
                eng.wait_ge(sem, own.value())
                own.did(eng.tensor_tensor(part, raw[:, 0, i + 1:C, los, i:i + 1].broadcast_to([P, below, n, i]),
                                          ea[:, i:i + 1, los, 0:i].broadcast_to([P, below, n, i]), ALU.mult))
                eng.wait_ge(sem, own.value())
                rest = ea[:, i + 1:C, los, 0:i]
                own.did(eng.tensor_tensor(rest, rest, part, ALU.subtract))

        @block.gpsimd
        def _(po):
            po.memset(ones[:, :], 1.0).then_inc(pool_setup, 1)

            def turn(grp, k, first=False, chain=None):
                r, p = grp * PAIRS + k // 2, k % 2
                own = Tally(po, pool_rot, grp * (GB * 4) + k * 4)
                if k == 0:
                    po.wait_ge(tab_loaded, grp * 16 + 16)
                po.wait_ge(q_copied[p], r + 1)
                if not first:
                    po.wait_ge(*sooner(qt_turned, p, r))
                    po.wait_ge(*sooner(q_rotated, p, r))
                rotate(po, own, q_s, q_rot, q_tmp, q_rotated[p])
                if chain:
                    po.wait_ge(q_rotated[p], r + 1)
                    chain()
                    po.wait_ge(pool_solved, (grp - 1) * 2 * ROWS_SOLVED + 2 * solved_after[k])

            def chain_slice(grp, k):
                if k == 1:
                    po.wait_ge(a_ready, grp + 1)
                    po.wait_ge(t_started, grp * LO + LO)
                solve(po, pool_solved, grp, SLICE_ROWS[k], slice(SPLIT, LO), q_tmp)

            grouped(po, turn, chain_slice)

        @block.vector
        def _(ve):
            ve.wait_ge(loaded, 16 * 6)
            ve.wait_ge(pool_setup, 1)
            FIRST_STEPS = 11

            def turn(grp, k, first=False, chain=None):
                r, p = grp * PAIRS + k // 2, k % 2
                own = Tally(ve, vec_rot, grp * (GB * 4) + k * 4)
                if k == 0:
                    ve.wait_ge(tab_loaded, grp * 16 + 16)
                ve.wait_ge(projected[p], r + 1)
                ve.wait_ge(kt_turned[p], r)
                ve.wait_ge(k_stored[p], r * 16)
                if not first:
                    ve.wait_ge(*sooner(k_rotated, p, r))
                k4 = p_k[:, :].rearrange("p (h x f) -> p h x f", h=H, x=2)
                rotate(ve, own, k4, k_rot[p], k_tmp, k_rotated[p])
                if chain:
                    ve.wait_ge(k_rotated[p], r + 1)
                    chain()
                    ve.wait_ge(vec_solved, (grp - 1) * 2 * ROWS_SOLVED + 2 * solved_after[k])
                if k == GB - 1:
                    by_step(grp)

            def by_step(grp):
                own = Tally(ve, vec_own, grp * FIRST_STEPS)

                def settle():
                    ve.wait_ge(vec_own, own.value())

                ve.wait_ge(scal_loaded, grp * 64 + 64)
                ve.wait_ge(small_exps, grp)
                ve.wait_ge(scaled_ready, grp * FORM_BANKS)
                ve.wait_ge(queries_ready, grp)
                for lo in range(LO):
                    own.did(ve.tensor_tensor_scan(cg[:, lo, :], ones[:, :], scal[:, 0, lo, :], 0.0, ALU.mult, ALU.add))
                settle()
                own.did(ve.tensor_tensor(cs[:, :, :], cg[:, :, :], scal[:, 2, :, :], ALU.subtract))
                own.did(ve.tensor_tensor(sx[:, 0, :, :], scal[:, 1, :, :], scal[:, 2, :, :], ALU.subtract))
                own.did(ve.tensor_tensor(sx[:, 1, :, :], scal[:, 1, :, :], cg[:, :, :], ALU.add))
                own.did(ve.tensor_tensor(sx[:, 3, :, :], scal[:, 3, :, :], cg[:, :, :], ALU.add))
                own.did(ve.tensor_tensor(sx[:, 4, :, :], scal[:, 2, :, :], cg[:, :, :], ALU.add))
                settle()
                own.did(ve.tensor_tensor(sx[:, 2, :, :], cg[:, :, C - 1:C].broadcast_to([P, LO, C]), cs[:, :, :], ALU.subtract))
                own.did(ve.tensor_tensor(ep[:, :, :, :], causal[:, :, :].unsqueeze(2).broadcast_to([P, C, LO, C]),
                                         cs[:, :, :].unsqueeze(1).broadcast_to([P, C, LO, C]), ALU.subtract))
                settle()
                assert own.n == FIRST_STEPS, own.n

            def by_pair(grp):
                by_t = lambda x: x.rearrange("p l t -> p t l").unsqueeze(3).broadcast_to([P, C, LO, C])
                ve.tensor_tensor(ea[:, :, :, :], ep[:, :, :, :], by_t(sx[:, 1, :, :]), ALU.add).then_inc(exponents, 1)
                ve.wait_ge(exponents, grp * 2 + 1)
                ve.tensor_tensor(ep[:, :, :, :], ep[:, :, :, :], by_t(sx[:, 3, :, :]), ALU.add).then_inc(exponents, 1)
                ve.wait_ge(exponents, grp * 2 + 2)

            def start_triangle(grp):
                ve.wait_ge(chain_copied, grp * BANKS + IN_BANKS // 2)
                ve.wait_ge(exps, grp * 2 + 1)
                ve.tensor_tensor(raw[:, 0, :, :, :], raw[:, 0, :, :, :], ea[:, :, :, :], ALU.mult).then_inc(a_ready, 1)
                ve.wait_ge(chain_copied, grp * BANKS + IN_BANKS)
                ve.wait_ge(exps, grp * 2 + 2)
                ve.tensor_tensor(raw[:, 1, :, :, :], raw[:, 1, :, :, :], ep[:, :, :, :], ALU.mult).then_inc(queries_ready, 1)
                ve.wait_ge(small_exps, grp + 1)
                ve.tensor_tensor(g_own[:, :, :], own_bh[:, :].unsqueeze(2).broadcast_to([P, P // HI, LO]),
                                 g_c[:, :].unsqueeze(1).broadcast_to([P, P // HI, LO]), ALU.mult).then_inc(gown_ready, 1)
                ve.wait_ge(t_negated, grp + 1)
                flat = ea[:, :, :, :].rearrange("p t l s -> p (t l s)")
                for lo in range(LO):
                    ve.memset(flat[:, C * lo:C * lo + (LO * C + 1) * (C - 1) + 1:LO * C + 1], 1.0).then_inc(t_started, 1)
                ve.wait_ge(t_started, grp * LO + LO)

            def chain_slice(grp, k):
                if k == 0:
                    by_pair(grp)
                if k == 1:
                    start_triangle(grp)
                for four in SLICE_SCALED[k]:
                    if four == SLICE_SCALED[k].start:
                        done = grp * 2 * ROWS_SOLVED + 2 * solved_after[k - 1]
                        ve.wait_ge(vec_solved, done)
                        ve.wait_ge(pool_solved, done)
                    rows = slice(4 * four, 4 * four + 4)
                    ve.tensor_tensor(raw[:, 0, rows, :, :], ea[:, rows, :, :], sx[:, 0, :, :].unsqueeze(1).broadcast_to([P, 4, LO, C]),
                                     ALU.mult).then_inc(scaled_ready, 1)
                solve(ve, vec_solved, grp, SLICE_ROWS[k], slice(0, SPLIT), k_tmp)

            grouped(ve, turn, chain_slice)


class Turn:

    def __init__(self, seq, t, step=0):
        self.p = t % 2
        self.same = seq * (NCH // 2) + t // 2 + step
        self.all = seq * NCH + t + step * 2
        self.first, self.last = t == 0, t == NCH - 1
        self.stated = seq * (NCH - 1) + (0 if self.first else t - 1) + step * 2
        self.updating = seq * (NCH - 1) + t + step * 2
        self.both = seq * (NCH - 2) + (0 if self.first else t - 1) + step * 2
        self.both_same = seq * (NCH // 2 - 1) + (0 if self.first else (t - 1) // 2) + step


def across_chunks(nc, a, s):
    with ExitStack() as ctx:
        def sb(name, shape):
            return ctx.enter_context(nc.sbuf_tensor("ac_" + name, shape, F32))

        def ps(name, shape):
            return ctx.enter_context(nc.psum_tensor("ac_" + name, shape, F32))

        def sem(name):
            return signal(nc, s, "ac_" + name)

        def two(name):
            return [sem(name + "0"), sem(name + "1")]

        HH = H // 2
        wv, fold = sb("wv", [P, H * DK]), sb("fold", [P, C])
        x_r = [sb(f"x_r{p}", [P, LO, C]) for p in range(2)]
        k_in = [sb(f"k_in{p}", [P, HP, DK]) for p in range(2)]
        kq_in = [sb(f"kq_in{p}", [P, 2, H, LO, C]) for p in range(2)]
        forms = [sb(f"forms{p}", [P, HP, 2, C]) for p in range(2)]
        g_in = [sb(f"g_in{p}", [P, 3, HP]) for p in range(2)]
        decay = [sb(f"decay{p}", [P, H, LO]) for p in range(2)]
        v_s = sb("v_s", [P, H, DK])
        k_s = [sb(f"k_s{p}", [P, HP, DK]) for p in range(2)]
        state = sb("state", [P, H, LO, HI, DK])
        rest = [sb(f"rest{h}", [P, HI, HH, DK]) for h in range(2)]
        u = [sb(f"u{h}", [P, HI, HH, DK]) for h in range(2)]
        u_wide = [sb(f"u_wide{h}", [P, HI, HH, LO, DK]) for h in range(2)]
        qs = [sb(f"qs{h}", [P, HI, HH, DK]) for h in range(2)]
        o_out = [sb(f"o_out{p}", [P, 2 * DK]) for p in range(2)]
        p_m = [[ps(f"p_m{h}{i}", [P, 512]) for i in range(HH // 2)] for h in range(2)]
        p_h = [ps(f"p_h{i}", [P, 512]) for i in range(2)]
        p_u, p_o = ps("p_u", [P, 512]), ps("p_o", [P, 512])

        loaded = sem("loaded")
        x_loaded, in_loaded, scal_loaded = two("x_loaded"), two("in_loaded"), two("scal_loaded")
        v_done, v_copied, keys_scaled = (sem(x) for x in ("v_done", "v_copied", "keys_scaled"))
        products, rest_ready, qs_ready, vec_own = two("products"), two("rest_ready"), two("qs_ready"), sem("vec_own")
        u_done, u_copied, u_spread, cleared = two("u_done"), two("u_copied"), two("u_spread"), sem("cleared")
        out_low, out_high, o_copied, o_stored = sem("out_low"), two("out_high"), sem("o_copied"), two("o_stored")
        updated, applied, decayed_low, decayed_high = two("updated"), two("applied"), sem("decayed_low"), two("decayed_high")
        pe_passed, sp_passed = sem("pe_passed"), sem("sp_passed")
        block = ctx.enter_context(nc.Block())

        def sequences(eng, body):
            with eng.Fori(0, NG) as g:
                with eng.Fori(0, GB) as b:
                    seq = g * GB + b
                    body(Turn(seq, 0), g * NCH, b, None)
                    body(Turn(seq, 1), g * NCH + 1, b, Turn(seq, 0))
                    with eng.Fori(0, NCH // 2 - 2) as j:
                        for t in (2, 3):
                            body(Turn(seq, t, j), g * NCH + j * 2 + t, b, Turn(seq, t - 1, j))
                    for t in (NCH - 2, NCH - 1):
                        body(Turn(seq, t), g * NCH + t, b, Turn(seq, t - 1))

        @block.sync
        def _(sp):
            sp.dma_start(wv[:, :], a["Wv"]).then_inc(loaded, 16)
            sp.dma_start(fold[:, :], a["fold"]).then_inc(loaded, 16)

            def turn(n, grp, b, before):
                p = n.p
                sp.wait_ge(out_high[p], n.same)
                apart(sp, sp_passed)
                sp.wait_ge(decayed_high[p], n.both_same)
                apart(sp, sp_passed)
                cols = s["xT"][:, bass.ds(n.all * C, C)]
                sp.dma_start(x_r[p][:, :, :], cols.unsqueeze(1).broadcast_to([P, LO, C])).then_inc(x_loaded[p], 16)
                sp.dma_start(kq_in[p][:, :, :, :, :].rearrange("p x h l t -> p (x h l t)"), s["qd"][grp * GB + b]).then_inc(in_loaded[p], 16)
                sp.dma_start(g_in[p][:, :, :].rearrange("p x c -> p (x c)"),
                             s["gd"][grp][:, bass.ds(b * (3 * HP), 3 * HP)]).then_inc(scal_loaded[p], 16)
                sp.dma_start(decay[p][:, :, :].rearrange("p h l -> p (h l)"),
                             s["sd"][grp][:, bass.ds(b * (H * LO), H * LO)]).then_inc(scal_loaded[p], 16)
                sp.dma_start(k_in[p][:, :, :].rearrange("p c k -> p (c k)"), s["kd"][grp * GB + b]).then_inc(in_loaded[p], 16)
                sp.dma_start(forms[p][:, :, :, :].rearrange("p c x t -> p (c x t)"),
                             s["od"][grp][:, bass.ds(b * (HP * 2 * C), HP * 2 * C)]).then_inc(in_loaded[p], 16)

            sequences(sp, turn)

        @block.tensor
        def _(pe):
            pe.wait_ge(loaded, 32)
            pe.wait_ge(cleared, 3)

            def heads(half):
                return [(h, half * HH + h) for h in range(HH)]

            def read_state(n, half):
                pe.wait_ge(in_loaded[n.p], n.same * 48 + 48)
                if half == 0:
                    pe.wait_ge(qs_ready[1], n.stated)
                else:
                    pe.wait_ge(qs_ready[0], n.stated + 1)
                for h, head in heads(half):
                    if h % 2 == 0:
                        pe.wait_ge(applied[half], (n.updating - 1) * 2 + h // 2 + 1)
                    for x in range(2):
                        for lo in range(LO):
                            last = pe.matmul(p_h[x][C * lo:C * lo + C, HI * DK * h:HI * DK * h + HI * DK],
                                             kq_in[n.p][:, x, head, lo, :],
                                             state[:, head, lo, :, :].rearrange("p i v -> p (i v)"),
                                             start=True, stop=True, tile_position=(0, C * lo))
                last.then_inc(products[half], 1)

            def values(n):
                pe.wait_ge(x_loaded[n.p], n.same * 16 + 16)
                pe.wait_ge(u_copied[1], n.all)
                pe.matmul(p_u[:, :], x_r[n.p][:, :, :].rearrange("p l t -> p (l t)"), wv[:, :],
                          start=True, stop=True).then_inc(v_done, 1)

            def solve(n, half):
                pe.wait_ge(v_copied, n.all + 1)
                if half:
                    pe.wait_ge(u_copied[0], n.all + 1)
                if n.first:
                    pe.wait_ge(in_loaded[n.p], n.same * 48 + 48)
                else:
                    pe.wait_ge(rest_ready[half], n.stated + 1)
                apart(pe, pe_passed)
                for h, head in heads(half):
                    for hi in range(HI):
                        for lo in range(LO):
                            rows = slice(C * lo, C * lo + C)
                            src = v_s[rows, head, :] if n.first else rest[half][rows, hi, h, :]
                            at = DK * (hi * HH + h)
                            last = pe.matmul(p_u[rows, at:at + DK], forms[n.p][rows, head * HI + hi, 1, :], src,
                                             start=True, stop=True, tile_position=(C * lo, C * lo))
                last.then_inc(u_done[half], 1)

            def output(n, half):
                pe.wait_ge(u_copied[half], n.all + 1)
                if half == 0:
                    pe.wait_ge(o_copied, n.all)
                if not n.first:
                    pe.wait_ge(qs_ready[half], n.stated + 1)
                    for hi in range(HI):
                        for q in range(2):
                            quarter = C * (2 * half + q)
                            pe.matmul(p_o[quarter:quarter + C, 0:2 * DK], fold[:, :],
                                      qs[half][:, hi, 2 * q:2 * q + 2, :].rearrange("p h v -> p (h v)"),
                                      start=hi == 0, stop=False, tile_position=(0, quarter), skip_group_check=True)
                for h2 in range(2):
                    for hi in range(HI):
                        for q in range(2):
                            h = 2 * q + h2
                            quarter = C * (2 * half + q)
                            last = pe.matmul(p_o[quarter:quarter + C, DK * h2:DK * h2 + DK],
                                             forms[n.p][:, (half * HH + h) * HI + hi, 0, :], u[half][:, hi, h, :],
                                             start=n.first and hi == 0 and h2 == 0, stop=hi == HI - 1,
                                             tile_position=(0, quarter), skip_group_check=True)
                last.then_inc(out_high[n.p] if half else out_low, 1)

            def update(n, half):
                if half == 0:
                    pe.wait_ge(keys_scaled, n.updating + 1)
                pe.wait_ge(u_spread[half], n.updating + 1)
                pe.wait_ge(applied[half], n.updating * 2)
                for h, head in heads(half):
                    for hi in range(HI):
                        at = LO * DK * (h % 2)
                        last = pe.matmul(p_m[half][h // 2][DK * hi:DK * hi + DK, at:at + LO * DK],
                                         k_s[n.p][:, head * HI + hi, :],
                                         u_wide[half][:, hi, h, :, :].rearrange("p l v -> p (l v)"),
                                         start=True, stop=True, tile_position=(0, DK * hi))
                    if h % 2:
                        last.then_inc(updated[half], 1)

            def turn(n, grp, b, before):
                if not n.first:
                    read_state(n, 0)
                values(n)
                if before:
                    output(before, 1)
                    update(before, 1)
                solve(n, 0)
                if not n.first:
                    read_state(n, 1)
                output(n, 0)
                if not n.last:
                    update(n, 0)
                solve(n, 1)
                if n.last:
                    output(n, 1)

            sequences(pe, turn)

        @block.scalar
        def _(act):
            act.wait_ge(cleared, 3)

            def copy_o(n):
                act.wait_ge(out_high[n.p], n.same + 1)
                act.wait_ge(o_stored[n.p], n.same * 64)
                act.activation(o_out[n.p][:, :], p_o[:, 0:2 * DK], ACT.Copy).then_inc(o_copied, 1)
                act.wait_ge(o_copied, n.all + 1)
                for q in range(4):
                    act.dma_start(s["oo"][bass.ds(n.all * C, C), 2 * DK * q:2 * DK * q + 2 * DK],
                                  o_out[n.p][C * q:C * q + C, :]).then_inc(o_stored[n.p], 16)

            def copy_u(n, half):
                act.wait_ge(u_done[half], n.all + 1)
                act.wait_ge(out_high[1 - n.p] if half else out_low, (n.same + n.p) if half else n.all)
                act.activation(u[half][:, :, :, :].rearrange("p i h v -> p (i h v)"), p_u[:, :], ACT.Copy).then_inc(u_copied[half], 1)
                if n.last:
                    return
                act.wait_ge(u_copied[half], n.all + 1)
                act.wait_ge(updated[half], n.updating * 2)
                for lo in range(LO):
                    rows = slice(C * lo, C * lo + C)
                    last = act.activation(u_wide[half][rows, :, :, lo, :].rearrange("p i h v -> p (i h) v"),
                                          u[half][rows, :, :, :].rearrange("p i h v -> p (i h) v"), ACT.Copy)
                last.then_inc(u_spread[half], 1)

            def turn(n, grp, b, before):
                act.wait_ge(v_done, n.all + 1)
                act.wait_ge(u_done[1], n.all)
                if not n.first:
                    act.wait_ge(rest_ready[1], n.stated)
                act.activation(v_s[:, :, :].rearrange("p h v -> p (h v)"), p_u[:, :], ACT.Copy).then_inc(v_copied, 1)
                if before:
                    copy_o(before)
                copy_u(n, 0)
                copy_u(n, 1)
                if n.last:
                    copy_o(n)

            sequences(act, turn)
            for p in range(2):
                act.wait_ge(o_stored[p], 64 * B * NCH // 2)

        @block.gpsimd
        def _(po):
            for x in (state, u_wide[0], u_wide[1]):
                po.memset(x[:, :, :, :, :], 0.0).then_inc(cleared, 1)
            po.wait_ge(cleared, 3)

            def turn(n, grp, b, before):
                p = n.p
                po.wait_ge(scal_loaded[p], n.same * 32 + 32)
                if not n.last:
                    po.wait_ge(in_loaded[p], n.same * 48 + 48)
                    if n.first:
                        po.wait_ge(updated[1], n.updating * 2)
                    po.tensor_tensor(k_s[p][:, :, :], k_in[p][:, :, :],
                                     g_in[p][:, 0, :].unsqueeze(2).broadcast_to([P, HP, DK]), ALU.mult).then_inc(keys_scaled, 1)
                if n.first or n.last:
                    return
                for half in range(2):
                    po.wait_ge(products[half], n.stated + 1)
                    part = state[:, half * HH:half * HH + HH, :, :, :].rearrange("p h l i v -> p (h l) (i v)")
                    po.tensor_tensor(part, part, decay[p][:, half * HH:half * HH + HH, :].rearrange("p h l -> p (h l)").unsqueeze(2)
                                     .broadcast_to([P, HH * LO, HI * DK]), ALU.mult).then_inc(decayed_high[p] if half else decayed_low, 1)

            sequences(po, turn)

        @block.vector
        def _(ve):
            ve.wait_ge(cleared, 3)

            def read(n, half):
                p = n.p
                ve.wait_ge(products[half], n.stated + 1)
                ve.wait_ge(u_done[half], n.all)
                ve.wait_ge(out_high[1 - p] if half else out_low, (n.same + p) if half else n.all)
                ve.wait_ge(scal_loaded[p], n.same * 32 + 32)
                own = Tally(ve, vec_own, n.stated * 2 + half)
                scalar = [g_in[p][:, x, :].rearrange("p (h i) -> p h i", i=HI)[:, half * HH:half * HH + HH, :] for x in range(3)]
                by_hi = lambda x: x.rearrange("p (h i v) -> p i h v", h=HH, i=HI)
                per_row = lambda x: x.rearrange("p h i -> p i h").unsqueeze(3).broadcast_to([P, HI, HH, DK])
                own.did(ve.tensor_tensor(rest[half][:, :, :, :], by_hi(p_h[0][:, :]), per_row(scalar[2]), ALU.mult))
                ve.tensor_tensor(qs[half][:, :, :, :], by_hi(p_h[1][:, :]), per_row(scalar[1]), ALU.mult).then_inc(qs_ready[half], 1)
                ve.wait_ge(vec_own, own.value())
                ve.wait_ge(v_copied, n.all + 1)
                last = ve.tensor_tensor(rest[half][:, :, :, :],
                                        v_s[:, half * HH:half * HH + HH, :].unsqueeze(1).broadcast_to([P, HI, HH, DK]),
                                        rest[half][:, :, :, :], ALU.subtract)
                last.then_inc(rest_ready[half], 1)

            def apply(n, half):
                if n.first:
                    ve.wait_ge(products[half], n.stated)
                else:
                    ve.wait_ge(decayed_high[n.p] if half else decayed_low, (n.both_same if half else n.both) + 1)
                for i in range(HH // 2):
                    ve.wait_ge(updated[half], n.updating * 2 + i + 1)
                    for hi in range(HI):
                        rows, first_head = slice(DK * hi, DK * hi + DK), half * HH + 2 * i
                        part = state[rows, first_head:first_head + 2, :, hi, :].rearrange("p h l v -> p (h l) v")
                        fresh = p_m[half][i][rows, :].rearrange("p (x v) -> p x v", v=DK)
                        last = ve.tensor_copy(part, fresh) if n.first else ve.tensor_tensor(part, part, fresh, ALU.add)
                    last.then_inc(applied[half], 1)

            def turn(n, grp, b, before):
                if not n.first:
                    read(n, 0)
                if before:
                    apply(before, 1)
                if not n.first:
                    read(n, 1)
                if not n.last:
                    apply(n, 0)

            sequences(ve, turn)


def after_attention(nc, a, s, w):
    with ExitStack() as ctx:
        def sb(name, shape):
            return ctx.enter_context(nc.sbuf_tensor("aa_" + name, shape, F32))

        def ps(name, shape):
            return ctx.enter_context(nc.psum_tensor("aa_" + name, shape, F32))

        def sem(name):
            return signal(nc, s, "aa_" + name)

        def two(name):
            return [sem(name + "0"), sem(name + "1")]

        KO = H * DK // P
        ident, wg, wo = sb("ident", [P, P]), sb("wg", [P, H * DK]), sb("wo", [P, KO, D])
        x_t = [sb(f"x_t{p}", [P, P]) for p in range(2)]
        x_in = [sb(f"x_in{p}", [P, D]) for p in range(2)]
        o_in = [sb(f"o_in{p}", [P, H * DK]) for p in range(2)]
        z = [sb(f"z{p}", [P, H * DK]) for p in range(2)]
        og = [sb(f"og{p}", [P, H * DK]) for p in range(2)]
        og_t = [sb(f"og_t{p}", [P, KO, P]) for p in range(2)]
        p_g, p_t, p_a = ([ps(f"{n}{p}", [P, 512]) for p in range(2)] for n in ("p_g", "p_t", "p_a"))
        loaded = sem("loaded")
        t_loaded, o_loaded, x_loaded = two("t_loaded"), two("o_loaded"), two("x_loaded")
        gate_done, gate_ready, gated, turned, copied, out_done, added = (
            two(x) for x in ("gate_done", "gate_ready", "gated", "turned", "copied", "out_done", "added"))
        block = ctx.enter_context(nc.Block())
        HALF_TILES = TILES // 2

        def stages(eng, first, second=None, third=None):
            first and first(0, 0)
            first and first(0, 1)
            second and second(0, 0)
            with eng.Fori(1, HALF_TILES) as r:
                for p in range(2):
                    first and first(r, p)
                    second and second(*((r, 0) if p else (r - 1, 1)))
                    third and third(r - 1, p)
            second and second(HALF_TILES - 1, 1)
            for p in range(2):
                third and third(HALF_TILES - 1, p)

        @block.sync
        def _(sp):
            sp.dma_start(wg[:, :], a["Wg"]).then_inc(loaded, 16)
            x_v = a["x"].rearrange("b (q p) d -> (b q) p d", p=P)

            def load(r, p):
                i = r * 2 + p
                sp.wait_ge(gate_done[p], r)
                sp.dma_start(x_t[p][:, :], s["xT"][:, bass.ds(i * P, P)]).then_inc(t_loaded[p], 16)
                sp.wait_ge(gated[p], r)
                sp.dma_start(o_in[p][:, :], s["oo"][bass.ds(i * P, P), :]).then_inc(o_loaded[p], 16)

            def load_x(r, p):
                sp.wait_ge(added[p], r)
                sp.dma_start(x_in[p][:, :], x_v[r * 2 + p]).then_inc(x_loaded[p], 16)

            for p in range(2):
                load(0, p)
            sp.dma_start(ident[:, :], a["ident"]).then_inc(loaded, 16)
            sp.dma_start(wo[:, :, :], a["Wo"].rearrange("(k p) d -> p k d", p=P)).then_inc(loaded, 16)
            load_x(0, 0)
            with sp.Fori(1, HALF_TILES) as r:
                for p in range(2):
                    load(r, p)
                    load_x(*((r, 0) if p else (r - 1, 1)))
            load_x(HALF_TILES - 1, 1)

        @block.tensor
        def _(pe):
            pe.wait_ge(loaded, 48)

            def gate(r, p):
                pe.wait_ge(t_loaded[p], r * 16 + 16)
                pe.wait_ge(gate_ready[p], r)
                pe.matmul(p_g[p][:, :], x_t[p][:, :], wg[:, :], start=True, stop=True).then_inc(gate_done[p], 1)

            def turn(r, p):
                pe.wait_ge(gated[p], r + 1)
                pe.wait_ge(copied[p], r)
                for k in range(KO):
                    last = pe.transpose(p_t[p][:, P * k:P * k + P], og[p][:, P * k:P * k + P], ident[:, :])
                last.then_inc(turned[p], 1)

            def project(r, p):
                pe.wait_ge(copied[p], r + 1)
                pe.wait_ge(added[p], r)
                for k in range(KO):
                    last = pe.matmul(p_a[p][:, 0:D], og_t[p][:, k, :], wo[:, k, :], start=k == 0, stop=k == KO - 1)
                last.then_inc(out_done[p], 1)

            stages(pe, gate, turn, project)

        @block.scalar
        def _(act):
            def sigmoid(r, p):
                act.wait_ge(gate_done[p], r + 1)
                act.wait_ge(gated[p], r)
                act.activation(z[p][:, :], p_g[p][:, :], ACT.Sigmoid).then_inc(gate_ready[p], 1)

            def copy(r, p):
                act.wait_ge(turned[p], r + 1)
                act.wait_ge(out_done[p], r)
                act.activation(og_t[p][:, :, :].rearrange("p k t -> p (k t)"), p_t[p][:, :], ACT.Copy).then_inc(copied[p], 1)

            stages(act, sigmoid, copy)

        @block.vector
        def _(ve):
            def apply_gate(r, p):
                ve.wait_ge(gate_ready[p], r + 1)
                ve.wait_ge(o_loaded[p], r * 16 + 16)
                ve.wait_ge(turned[p], r)
                ve.tensor_tensor(og[p][:, :], o_in[p][:, :], z[p][:, :], ALU.mult).then_inc(gated[p], 1)

            def add(r, p):
                ve.wait_ge(out_done[p], r + 1)
                ve.wait_ge(x_loaded[p], r * 16 + 16)
                ve.tensor_tensor(w["rest"][:, bass.ds(r * 2 + p, 1), :].rearrange("p o d -> p (o d)"),
                                 x_in[p][:, :], p_a[p][:, 0:D], ALU.add).then_inc(added[p], 1)

            stages(ve, apply_gate, None, add)


def layer_norm(ve, own, act_done, requested, normed, dst, src, stats, turn):
    n = src.shape[1]
    raw, mean, var, inv = stats

    def step(instruction):
        own.did(instruction)
        ve.wait_ge(own.sem, own.value())

    for t in range(n):
        own.did(ve.bn_stats(raw[:, t, :], src[:, t, :]))
    ve.wait_ge(own.sem, own.value())
    own.did(ve.tensor_tensor(mean, raw[:, :, 1], raw[:, :, 4], ALU.add))
    own.did(ve.tensor_tensor(inv, raw[:, :, 1], raw[:, :, 4], ALU.subtract))
    step(ve.tensor_tensor(var, raw[:, :, 2], raw[:, :, 5], ALU.add))
    own.did(ve.tensor_scalar(mean, mean, 0.5, None, ALU.mult))
    own.did(ve.tensor_scalar(var, var, 1.0 / D, LN_EPS, ALU.mult, ALU.add))
    step(ve.scalar_tensor_tensor(inv, inv, 0.25, inv, ALU.mult, ALU.mult))
    ve.tensor_tensor(inv, inv, var, ALU.add).then_inc(requested, 1)
    ve.wait_ge(act_done, turn + 1)
    norm_share(ve, own, normed, dst, src, stats, slice(0, VE_TILES))


VE_TILES = 46


def norm_share(eng, own, normed, dst, src, stats, tiles):
    raw, mean, var, inv = stats
    spread = lambda x: x[:, tiles].unsqueeze(2).broadcast_to([P, tiles.stop - tiles.start, D])
    own.did(eng.tensor_tensor(dst[:, tiles, :], src[:, tiles, :], spread(mean), ALU.subtract))
    eng.wait_ge(own.sem, own.value())
    eng.tensor_tensor(dst[:, tiles, :], dst[:, tiles, :], spread(inv), ALU.mult).then_inc(normed, 1)


def inverse_roots(act, own, requested, done, inv, turns):
    for k in range(turns):
        act.wait_ge(requested, k + 1)
        act.activation(inv, inv, ACT.Ln).then_inc(own, 1)
        act.wait_ge(own, k + 1)
        act.activation(inv, inv, ACT.Exp, scale=-0.5).then_inc(done, 1)


def norms(nc, a, s, w):
    with ExitStack() as ctx:
        def sb(name, shape):
            return ctx.enter_context(nc.sbuf_tensor("no_" + name, shape, F32))

        def sem(name):
            return signal(nc, s, "no_" + name)

        gain, bias = sb("gain", [P, D]), sb("bias", [P, D])
        raw, mean, var, inv = sb("raw", [P, TILES, 6]), sb("mean", [P, TILES]), sb("var", [P, TILES]), sb("inv", [P, TILES])
        loaded, vec_own, pool_own, act_own, requested, rooted, normed, zero_ready, zeroed = (
            sem(x) for x in ("loaded", "vec_own", "pool_own", "act_own", "requested", "rooted", "normed", "zero_ready", "zeroed"))
        block = ctx.enter_context(nc.Block())
        x1, h = w["rest"][:, :, :], w["h"][:, :, :]
        stats = (raw[:, :, :], mean[:, :], var[:, :], inv[:, :])

        def scale_and_shift(eng, own, tiles):
            part = h[:, tiles, :]
            spread = lambda x: x[:, :].unsqueeze(1).broadcast_to([P, tiles.stop - tiles.start, D])
            own.did(eng.tensor_tensor(part, part, spread(gain), ALU.mult))
            eng.wait_ge(own.sem, own.value())
            own.did(eng.tensor_tensor(part, part, spread(bias), ALU.add))

        @block.sync
        def _(sp):
            sp.dma_start(gain[:, :], a["ln_g"].partition_broadcast(P)).then_inc(loaded, 16)
            sp.dma_start(bias[:, :], a["ln_b"].partition_broadcast(P)).then_inc(loaded, 16)
            sp.wait_ge(zero_ready, 1)
            sp.dma_start(s["xe"].rearrange("(t p) d -> p t d", p=P), w["zeros"][:, :, :]).then_inc(zeroed, 16)
            sp.wait_ge(zeroed, 16)

        @block.gpsimd
        def _(po):
            own = Tally(po, pool_own)
            po.memset(w["zeros"][:, :, :], 0.0).then_inc(zero_ready, 1)
            tiles = slice(VE_TILES, TILES)
            po.wait_ge(rooted, 1)
            norm_share(po, own, normed, x1, x1, stats, tiles)
            po.wait_ge(rooted, 2)
            norm_share(po, own, normed, h, x1, stats, tiles)
            po.wait_ge(normed, 4)
            po.wait_ge(loaded, 32)
            scale_and_shift(po, own, tiles)

        @block.scalar
        def _(act):
            inverse_roots(act, act_own, requested, rooted, inv[:, :], 2)

        @block.vector
        def _(ve):
            own = Tally(ve, vec_own)
            layer_norm(ve, own, rooted, requested, normed, x1, x1, stats, 0)
            ve.wait_ge(normed, 2)
            layer_norm(ve, own, rooted, requested, normed, h, x1, stats, 1)
            ve.wait_ge(normed, 4)
            ve.wait_ge(loaded, 32)
            scale_and_shift(ve, own, slice(0, VE_TILES))


def routing(nc, a, s, w):
    with ExitStack() as ctx:
        def sb(name, shape, dt=F32):
            return ctx.enter_context(nc.sbuf_tensor("ro_" + name, shape, dt))

        def ps(name, shape):
            return ctx.enter_context(nc.psum_tensor("ro_" + name, shape, F32))

        def sem(name):
            return signal(nc, s, "ro_" + name)

        def two(name):
            return [sem(name + "0"), sem(name + "1")]

        E8 = 8
        ident, before, lane = sb("ident", [P, P]), sb("before", [P, P]), sb("lane", [P, E8])
        ones = sb("ones", [P, P])
        wr = sb("wr", [P, E_R])
        h_s = [sb(f"h_s{p}", [P, D]) for p in range(2)]
        h_t = [sb(f"h_t{p}", [P, P]) for p in range(2)]
        logits = sb("logits", [P, TILES, E8])
        cand = sb("cand", [P, TILES, E8])
        picked = [sb(f"picked{c}", [P, TILES, E8]) for c in range(2)]
        total = [sb(f"total{c}", [P, TILES, E8]) for c in range(2)]
        running = [sb(f"running{c}", [P, E8, TILES]) for c in range(2)]
        place = sb("place", [P, TILES, E8])
        best = [sb(f"best{c}", [P, TILES]) for c in range(2)]
        expert = [sb(f"expert{c}", [P, TILES]) for c in range(2)]
        spot, keep, den, odds = sb("spot", [P, TILES]), sb("keep", [P, TILES]), sb("den", [P, TILES]), sb("odds", [P, TILES])
        p_t = [ps(f"p_t{p}", [P, 512]) for p in range(2)]
        p_l = [ps(f"p_l{p}", [P, 512]) for p in range(2)]
        p_c = [ps(f"p_c{c}", [P, 512]) for c in range(4)]
        loaded, setup = sem("loaded"), sem("setup")
        staged, turned, copied, scored, kept = (two(x) for x in ("staged", "turned", "copied", "scored", "kept"))
        vec_own, odds_asked, odds_ready, picked_ready, counted = (
            sem(x) for x in ("vec_own", "odds_asked", "odds_ready", "picked_ready", "counted"))
        block = ctx.enter_context(nc.Block())

        @block.sync
        def _(sp):
            for dst, src in ((ident, "ident"), (before, "before"), (lane, "lane"), (wr, "Wr")):
                sp.dma_start(dst[:, :], a[src]).then_inc(loaded, 16)

        @block.gpsimd
        def _(po):
            po.memset(ones[:, :], 1.0).then_inc(setup, 1)
            with po.Fori(0, TILES // 2) as r:
                for p in range(2):
                    po.wait_ge(turned[p], r)
                    po.tensor_copy(h_s[p][:, :], w["h"][:, bass.ds(r * 2 + p, 1), :].rearrange("p o d -> p (o d)")).then_inc(staged[p], 1)

        @block.tensor
        def _(pe):
            pe.wait_ge(loaded, 64)
            with pe.Fori(0, TILES // 2) as r:
                for p in range(2):
                    pe.wait_ge(staged[p], r + 1)
                    pe.wait_ge(copied[p], r)
                    pe.transpose(p_t[p][:, 0:P], h_s[p][:, :], ident[:, :]).then_inc(turned[p], 1)
                for p in range(2):
                    pe.wait_ge(copied[p], r + 1)
                    pe.wait_ge(kept[p], r)
                    pe.matmul(p_l[p][:, 0:E_R], h_t[p][:, :], wr[:, :], start=True, stop=True).then_inc(scored[p], 1)
            pe.wait_ge(setup, 1)
            for c in range(2):
                pe.wait_ge(picked_ready, c + 1)
                flat = picked[c][:, :, :].rearrange("p t e -> p (t e)")
                pe.matmul(p_c[2 * c][:, :], before[:, :], flat, start=True, stop=True)
                pe.matmul(p_c[2 * c + 1][:, :], ones[:, :], flat, start=True, stop=True).then_inc(counted, 1)

        @block.scalar
        def _(act):
            with act.Fori(0, TILES // 2) as r:
                for p in range(2):
                    act.wait_ge(turned[p], r + 1)
                    act.wait_ge(scored[p], r)
                    act.activation(w["hT"][:, bass.ds((r * 2 + p) * P, P)], p_t[p][:, 0:P], ACT.Copy)
                    act.activation(h_t[p][:, :], p_t[p][:, 0:P], ACT.Copy).then_inc(copied[p], 1)
            act.wait_ge(odds_asked, 1)
            act.activation(odds[:, :], odds[:, :], ACT.Exp).then_inc(odds_ready, 1)

        @block.vector
        def _(ve):
            own = Tally(ve, vec_own)

            def step(instruction):
                own.did(instruction)
                ve.wait_ge(vec_own, own.value())

            ve.wait_ge(loaded, 64)
            ve.wait_ge(setup, 1)
            step(ve.memset(logits[:, :, E_R:E8], -1e30))
            with ve.Fori(0, TILES // 2) as r:
                for p in range(2):
                    ve.wait_ge(scored[p], r + 1)
                    ve.tensor_copy(logits[:, bass.ds(r * 2 + p, 1), 0:E_R].rearrange("p o e -> p (o e)"), p_l[p][:, 0:E_R]).then_inc(kept[p], 1)
            for p in range(2):
                ve.wait_ge(kept[p], TILES // 2)
            per_tile = lambda x: x[:, :].unsqueeze(2).broadcast_to([P, TILES, E8])
            lanes = lane[:, :].unsqueeze(1).broadcast_to([P, TILES, E8])
            for c in range(2):
                step(ve.tensor_reduce(best[c][:, :], logits[:, :, :], AX.X, ALU.max))
                step(ve.tensor_tensor(cand[:, :, :], logits[:, :, :], per_tile(best[c]), ALU.is_lt))
                step(ve.scalar_tensor_tensor(cand[:, :, :], cand[:, :, :], float(E8), lanes, ALU.mult, ALU.add))
                step(ve.tensor_reduce(expert[c][:, :], cand[:, :, :], AX.X, ALU.min))
                ve.tensor_tensor(picked[c][:, :, :], lanes, per_tile(expert[c]), ALU.is_equal).then_inc(picked_ready, 1)
                ve.wait_ge(picked_ready, c + 1)
                if c == 0:
                    step(ve.scalar_tensor_tensor(logits[:, :, :], picked[0][:, :, :], -1e30, logits[:, :, :], ALU.mult, ALU.add))
            ve.tensor_tensor(odds[:, :], best[1][:, :], best[0][:, :], ALU.subtract).then_inc(odds_asked, 1)
            ve.wait_ge(odds_ready, 1)
            step(ve.tensor_scalar(den[:, :], odds[:, :], 1.0, None, ALU.add))
            step(ve.reciprocal(w["gate"][:, 0, :], den[:, :]))
            step(ve.tensor_tensor(w["gate"][:, 1, :], odds[:, :], w["gate"][:, 0, :], ALU.mult))
            for c in range(2):
                ve.wait_ge(counted, c + 1)
                step(ve.tensor_copy(total[c][:, :, :].rearrange("p t e -> p (t e)"), p_c[2 * c + 1][:, :]))
                for e in range(E8):
                    own.did(ve.tensor_tensor_scan(running[c][:, e, :], ones[:, 0:TILES], total[c][:, :, e], 0.0, ALU.mult, ALU.add))
                ve.wait_ge(vec_own, own.value())
                turned_back = running[c][:, :, :].rearrange("p e t -> p t e")
                step(ve.tensor_tensor(place[:, :, :], turned_back, total[c][:, :, :], ALU.subtract))
                step(ve.tensor_tensor(place[:, :, :], place[:, :, :], p_c[2 * c][:, :].rearrange("p (t e) -> p t e", e=E8), ALU.add))
                if c == 1:
                    step(ve.tensor_tensor(place[:, :, :], place[:, :, :],
                                          running[0][:, :, TILES - 1].unsqueeze(1).broadcast_to([P, TILES, E8]), ALU.add))
                step(ve.tensor_tensor(place[:, :, :], place[:, :, :], picked[c][:, :, :], ALU.mult))
                step(ve.tensor_reduce(spot[:, :], place[:, :, :], AX.X, ALU.add))
                step(ve.tensor_scalar(keep[:, :], spot[:, :], float(CAP), None, ALU.is_lt))
                step(ve.tensor_tensor(w["gate"][:, c, :], w["gate"][:, c, :], keep[:, :], ALU.mult))
                step(ve.scalar_tensor_tensor(spot[:, :], expert[c][:, :], float(CAPP), spot[:, :], ALU.mult, ALU.add))
                step(ve.tensor_scalar(keep[:, :], keep[:, :], -float(2 * ROWS), float(2 * ROWS), ALU.mult, ALU.add))
                step(ve.tensor_tensor(spot[:, :], spot[:, :], keep[:, :], ALU.add))
                step(ve.tensor_copy(w["slot"][:, :, c], spot[:, :]))


def dispatch_and_shared(nc, a, s, w):
    with ExitStack() as ctx:
        def sb(name, shape, dt=F32):
            return ctx.enter_context(nc.sbuf_tensor("di_" + name, shape, dt))

        def ps(name, shape):
            return ctx.enter_context(nc.psum_tensor("di_" + name, shape, F32))

        def sem(name):
            return signal(nc, s, "di_" + name)

        KF, Q4 = FF // P, 4
        GROUPS = TILES // Q4
        w1, w3, w2 = sb("w1", [P, FF]), sb("w3", [P, FF]), sb("w2", [P, KF, D])
        act_a, g_t = sb("act_a", [P, KF, Q4 * P]), sb("g_t", [P, KF, Q4 * P])
        h_s = [sb(f"h_s{q}", [P, D]) for q in range(Q4)]
        ix = [sb(f"ix{q}", [P, 2], U32) for q in range(Q4)]
        p_y = ps("p_y", [P, 512])
        p_a = [ps(f"p_a{i}", [P, 512]) for i in range(2)]
        p_b = [ps(f"p_b{i}", [P, 512]) for i in range(2)]
        loaded, a_done, b_done, silu_done, g_done, y_done, added, po_passed = (
            sem(x) for x in ("loaded", "a_done", "b_done", "silu_done", "g_done", "y_done", "added", "po_passed"))
        staged, sent = ([sem(f"{n}{q}") for q in range(Q4)] for n in ("staged", "sent"))
        block = ctx.enter_context(nc.Block())

        @block.sync
        def _(sp):
            sp.dma_start(w1[:, :], a["W1s"]).then_inc(loaded, 16)
            sp.dma_start(w3[:, :], a["W3s"]).then_inc(loaded, 16)
            sp.dma_start(w2[:, :, :], a["W2s"].rearrange("(k p) d -> p k d", p=P)).then_inc(loaded, 16)

        @block.gpsimd
        def _(po):
            with po.Fori(0, GROUPS) as i:
                for q in range(Q4):
                    po.wait_ge(staged[q], i * 2 + 2)
                    apart(po, po_passed)
                    for c in range(2):
                        po.indirect_dma_start(s["xe"][:, :], bass.IndirectOffsetOnAxis(ap=ix[q][:, c:c + 1], axis=0),
                                              h_s[q][:, :], None, bounds_check=ROWS - 1, oob_is_err=False).then_inc(sent[q], 16)
            for q in range(Q4):
                po.wait_ge(sent[q], 32 * GROUPS)

        @block.tensor
        def _(pe):
            pe.wait_ge(loaded, 48)
            with pe.Fori(0, GROUPS) as i:
                h_t = w["hT"][:, bass.ds(i * (Q4 * P), Q4 * P)]
                for k in range(KF):
                    pe.wait_ge(g_done, i * KF if k < 2 else i * KF + k - 1)
                    pe.matmul(p_a[k % 2][:, :], w1[:, P * k:P * k + P], h_t, start=True, stop=True).then_inc(a_done, 1)
                    pe.matmul(p_b[k % 2][:, :], w3[:, P * k:P * k + P], h_t, start=True, stop=True).then_inc(b_done, 1)
                pe.wait_ge(g_done, i * KF + KF)
                pe.wait_ge(added, i)
                for t in range(Q4):
                    for k in range(KF):
                        last = pe.matmul(p_y[:, P * t:P * t + P], g_t[:, k, P * t:P * t + P], w2[:, k, :],
                                         start=k == 0, stop=k == KF - 1)
                last.then_inc(y_done, 1)

        @block.scalar
        def _(act):
            with act.Fori(0, GROUPS) as i:
                for k in range(KF):
                    act.wait_ge(a_done, i * KF + k + 1)
                    act.wait_ge(g_done, i * KF)
                    act.activation(act_a[:, k, :], p_a[k % 2][:, :], ACT.Silu).then_inc(silu_done, 1)

        @block.vector
        def _(ve):
            with ve.Fori(0, GROUPS) as i:
                for k in range(KF):
                    tile = i * Q4 + k
                    ve.wait_ge(sent[k], i * 32)
                    ve.tensor_copy(h_s[k][:, :], w["h"][:, bass.ds(tile, 1), :].rearrange("p o d -> p (o d)")).then_inc(staged[k], 1)
                    ve.tensor_copy(ix[k][:, :], w["slot"][:, bass.ds(tile, 1), :].rearrange("p o c -> p (o c)")).then_inc(staged[k], 1)
                    ve.wait_ge(silu_done, i * KF + k + 1)
                    ve.wait_ge(b_done, i * KF + k + 1)
                    ve.wait_ge(y_done, i)
                    ve.tensor_tensor(g_t[:, k, :], act_a[:, k, :], p_b[k % 2][:, :], ALU.mult).then_inc(g_done, 1)
                ve.wait_ge(y_done, i + 1)
                part = w["rest"][:, bass.ds(i * Q4, Q4), :]
                ve.tensor_tensor(part, part, p_y[:, :].rearrange("p (t d) -> p t d", t=Q4), ALU.add).then_inc(added, 1)


def experts(nc, a, s, w):
    with ExitStack() as ctx:
        def sb(name, shape):
            return ctx.enter_context(nc.sbuf_tensor("ex_" + name, shape, F32))

        def ps(name, shape):
            return ctx.enter_context(nc.psum_tensor("ex_" + name, shape, F32))

        def sem(name):
            return signal(nc, s, "ex_" + name)

        KF, RT = FF // P, CAPP // P
        ident = sb("ident", [P, P])
        w1, w3, x_e = ([sb(f"{n}{p}", shape) for p in range(2)]
                       for n, shape in (("w1", [P, FF]), ("w3", [P, FF]), ("x_e", [P, RT, D])))
        w2, x_t = ([sb(f"{n}{p}", shape) for p in range(2)] for n, shape in (("w2", [P, KF, D]), ("x_t", [P, CAPP])))
        y_e = sb("y_e", [P, RT, D])
        act_a, g_t = sb("act_a", [P, KF, CAPP]), sb("g_t", [P, KF, CAPP])
        p_t, p_y = ps("p_t", [P, 512]), ps("p_y", [P, 512])
        p_a = [ps(f"p_a{i}", [P, 512]) for i in range(2)]
        p_b = [ps(f"p_b{i}", [P, 512]) for i in range(2)]
        const_loaded, turned, copied, a_done, b_done, silu_done, g_done, y_done, y_copied, stored = (
            sem(x) for x in ("const_loaded", "turned", "copied", "a_done", "b_done", "silu_done", "g_done",
                             "y_done", "y_copied", "stored"))
        loaded = [sem(f"loaded{p}") for p in range(2)]
        block = ctx.enter_context(nc.Block())
        LAST = E_R - 1
        assert LAST % 2 == 0

        @block.sync
        def _(sp):
            sp.dma_start(ident[:, :], a["ident"]).then_inc(const_loaded, 16)
            x_v = s["xe"].rearrange("(e t p) d -> e p t d", p=P, t=RT)
            y_v = s["ye"].rearrange("(e t p) d -> e p t d", p=P, t=RT)

            def load(e, p):
                sp.dma_start(x_e[p][:, :, :], x_v[e]).then_inc(loaded[p], 16)
                sp.dma_start(w1[p][:, :], a["W1"][e]).then_inc(loaded[p], 16)
                sp.dma_start(w3[p][:, :], a["W3"][e]).then_inc(loaded[p], 16)
                sp.dma_start(w2[p][:, :, :], a["W2"].rearrange("e (k p) d -> e p k d", p=P)[e]).then_inc(loaded[p], 16)

            def expert(e, p, more):
                if more:
                    sp.wait_ge(y_done, e + 1)
                    load(e + 2, p)
                sp.wait_ge(y_copied, e + 1)
                sp.dma_start(y_v[e], y_e[:, :, :]).then_inc(stored, 16)

            load(0, 0)
            load(1, 1)
            with sp.Fori(0, LAST // 2 - 1) as r:
                for p in range(2):
                    expert(r * 2 + p, p, True)
            expert(LAST - 2, 0, True)
            expert(LAST - 1, 1, False)
            expert(LAST, 0, False)
            sp.wait_ge(stored, 16 * E_R)

        def all_experts(eng, body):
            with eng.Fori(0, LAST // 2) as r:
                for p in range(2):
                    body(r, p, True)
            body(LAST // 2, 0, False)

        @block.tensor
        def _(pe):
            pe.wait_ge(const_loaded, 16)

            def turn(r, p):
                pe.wait_ge(loaded[p], r * 64 + 64)
                pe.wait_ge(copied, r * 2 + p)
                for t in range(RT):
                    last = pe.transpose(p_t[:, P * t:P * t + P], x_e[p][:, t, :], ident[:, :])
                last.then_inc(turned, 1)

            def expert(r, p, more):
                e = r * 2 + p
                pe.wait_ge(copied, e + 1)
                for k in range(KF):
                    pe.wait_ge(g_done, e * KF if k < 2 else e * KF + k - 1)
                    pe.matmul(p_a[k % 2][:, 0:CAPP], w1[p][:, P * k:P * k + P], x_t[p][:, :], start=True, stop=True).then_inc(a_done, 1)
                    pe.matmul(p_b[k % 2][:, 0:CAPP], w3[p][:, P * k:P * k + P], x_t[p][:, :], start=True, stop=True).then_inc(b_done, 1)
                if more:
                    turn(*((r + 1, 0) if p else (r, 1)))
                pe.wait_ge(g_done, e * KF + KF)
                pe.wait_ge(y_copied, e)
                for t in range(RT):
                    for k in range(KF):
                        last = pe.matmul(p_y[:, P * t:P * t + P], g_t[:, k, P * t:P * t + P], w2[p][:, k, :],
                                         start=k == 0, stop=k == KF - 1)
                last.then_inc(y_done, 1)

            turn(0, 0)
            all_experts(pe, expert)

        @block.scalar
        def _(act):
            def copy_x(e, p):
                act.wait_ge(turned, e + 1)
                act.activation(x_t[p][:, :], p_t[:, 0:CAPP], ACT.Copy).then_inc(copied, 1)

            def expert(r, p, more):
                e = r * 2 + p
                for k in range(KF):
                    act.wait_ge(a_done, e * KF + k + 1)
                    act.wait_ge(g_done, e * KF)
                    act.activation(act_a[:, k, :], p_a[k % 2][:, 0:CAPP], ACT.Silu).then_inc(silu_done, 1)
                if more:
                    act.wait_ge(b_done, e * KF)
                    copy_x(e + 1, 1 - p)
                act.wait_ge(y_done, e + 1)
                act.wait_ge(stored, e * 16)
                act.activation(y_e[:, :, :].rearrange("p t d -> p (t d)"), p_y[:, 0:CAPP], ACT.Copy).then_inc(y_copied, 1)

            copy_x(0, 0)
            all_experts(act, expert)

        @block.vector
        def _(ve):
            with ve.Fori(0, E_R) as e:
                for k in range(KF):
                    ve.wait_ge(silu_done, e * KF + k + 1)
                    ve.wait_ge(b_done, e * KF + k + 1)
                    ve.wait_ge(y_done, e)
                    ve.tensor_tensor(g_t[:, k, :], act_a[:, k, :], p_b[k % 2][:, 0:CAPP], ALU.mult).then_inc(g_done, 1)


def gather(nc, a, s, w):
    with ExitStack() as ctx:
        def sb(name, shape, dt=F32):
            return ctx.enter_context(nc.sbuf_tensor("ga_" + name, shape, dt))

        def sem(name):
            return signal(nc, s, "ga_" + name)

        Q4 = 4
        GROUPS = TILES // Q4
        ix = [[sb(f"ix{q}{c}", [P, 1], U32) for c in range(2)] for q in range(Q4)]
        rows = [[sb(f"rows{q}{c}", [P, D]) for c in range(2)] for q in range(Q4)]
        cleared, po_passed, vec_own = (sem(x) for x in ("cleared", "po_passed", "vec_own"))
        staged, gathered, summed = ([sem(f"{n}{q}") for q in range(Q4)] for n in ("staged", "gathered", "summed"))
        block = ctx.enter_context(nc.Block())

        @block.gpsimd
        def _(po):
            po.wait_ge(cleared, 2 * Q4)
            with po.Fori(0, GROUPS) as i:
                for q in range(Q4):
                    po.wait_ge(summed[q], i)
                    po.wait_ge(staged[q], i * 2 + 2)
                    apart(po, po_passed)
                    for c in range(2):
                        po.indirect_dma_start(rows[q][c][:, :], None, s["ye"][:, :],
                                              bass.IndirectOffsetOnAxis(ap=ix[q][c][:, :], axis=0),
                                              bounds_check=ROWS - 1, oob_is_err=False).then_inc(gathered[q], 16)

        @block.vector
        def _(ve):
            for q in range(Q4):
                for c in range(2):
                    ve.memset(rows[q][c][:, :], 0.0).then_inc(cleared, 1)

            def stage(q, tile):
                for c in range(2):
                    ve.tensor_copy(ix[q][c][:, :], w["slot"][:, bass.ds(tile, 1), c]).then_inc(staged[q], 1)

            def add(i, q):
                one = w["rest"][:, bass.ds(i * Q4 + q, 1), :].rearrange("p o d -> p (o d)")
                gate = [w["gate"][:, c, bass.ds(i * Q4 + q, 1)] for c in range(2)]
                ve.wait_ge(gathered[q], i * 32 + 32)
                ve.scalar_tensor_tensor(one, rows[q][0][:, :], gate[0], one, ALU.mult, ALU.add).then_inc(vec_own, 1)
                ve.wait_ge(vec_own, i * Q4 + q + 1)
                ve.scalar_tensor_tensor(one, rows[q][1][:, :], gate[1], one, ALU.mult, ALU.add).then_inc(summed[q], 1)

            for q in range(Q4):
                stage(q, q)
            with ve.Fori(0, GROUPS - 1) as i:
                for q in range(Q4):
                    add(i, q)
                    stage(q, i * Q4 + Q4 + q)
            for q in range(Q4):
                add(GROUPS - 1, q)


def last_norm(nc, a, s, w, out):
    with ExitStack() as ctx:
        def sb(name, shape):
            return ctx.enter_context(nc.sbuf_tensor("ln_" + name, shape, F32))

        def sem(name):
            return signal(nc, s, "ln_" + name)

        raw, mean, var, inv = sb("raw", [P, TILES, 6]), sb("mean", [P, TILES]), sb("var", [P, TILES]), sb("inv", [P, TILES])
        vec_own, pool_own, act_own, requested, rooted, normed, stored = (
            sem(x) for x in ("vec_own", "pool_own", "act_own", "requested", "rooted", "normed", "stored"))
        block = ctx.enter_context(nc.Block())
        rest = w["rest"][:, :, :]
        stats = (raw[:, :, :], mean[:, :], var[:, :], inv[:, :])

        @block.scalar
        def _(act):
            inverse_roots(act, act_own, requested, rooted, inv[:, :], 1)

        @block.vector
        def _(ve):
            layer_norm(ve, Tally(ve, vec_own), rooted, requested, normed, rest, rest, stats, 0)

        @block.gpsimd
        def _(po):
            po.wait_ge(rooted, 1)
            norm_share(po, Tally(po, pool_own), normed, rest, rest, stats, slice(VE_TILES, TILES))

        @block.sync
        def _(sp):
            sp.wait_ge(normed, 2)
            sp.dma_start(out.rearrange("b (q p) d -> p (b q) d", p=P), rest).then_inc(stored, 16)
            sp.wait_ge(stored, 16)


def apart(eng, passed):
    eng.sem_inc(passed, 1)


def signal(nc, s, name):
    s["signals"].append(nc.alloc_semaphore(name=name))
    return s["signals"][-1]


def phase(nc, a, s, body, *more):
    s["signals"] = []
    body(nc, a, s, *more)
    nc.clear_and_free_semaphores(s["signals"])
    nc.all_engine_barrier()


def build(nc, a, s, out):
    for body in (token_scalars, within_chunks, across_chunks):
        phase(nc, a, s, body)
    with ExitStack() as ctx:
        def sb(name, shape, dt=F32):
            return ctx.enter_context(nc.sbuf_tensor(name, shape, dt))

        w = {"rest": sb("rest", [P, TILES, D]), "h": sb("h", [P, TILES, D]),
             "gate": sb("gate", [P, 2, TILES]), "slot": sb("slot", [P, TILES, 2], U32)}
        with nc.sbuf_tensor("zeros", [P, ROWS // P, D], F32) as zeros:
            w["zeros"] = zeros
            phase(nc, a, s, after_attention, w)
            phase(nc, a, s, norms, w)
        w["hT"] = sb("hT", [P, N_TOK])
        for body in (routing, dispatch_and_shared, experts, gather):
            phase(nc, a, s, body, w)
        phase(nc, a, s, last_norm, w, out)


_INS = ["L0_attn_" + n for n in ("hidden_states", "Wq", "Wk", "Wv", "Wbeta", "Wtg", "mode_logits", "log_decay",
                                 "omega_log_scale", "Wg", "Wo")] + \
       ["L0_ffn_" + n for n in ("ln_g", "ln_b", "Wr", "W1", "W3", "W2", "W1s", "W3s", "W2s")]


def kernel(**inputs):
    import numpy as _np
    import concourse.bacc as _bacc
    from concourse import mybir as _mybir
    from concourse.bass_utils import run_bass_kernel_spmd as _run

    nc = _bacc.Bacc("TRN2", target_bir_lowering=False, num_devices=1)
    arrays, args = {}, {}
    named = {n.split("_", 2)[2]: _np.ascontiguousarray(inputs[n]) for n in _INS}
    named["x"] = named.pop("hidden_states")
    named.update(constants())
    for name, value in named.items():
        arrays[f"in_{name}_dram"] = value
        args[name] = nc.dram_tensor(f"in_{name}_dram", value.shape, _mybir.dt.from_np(value.dtype), kind="ExternalInput").ap()
    out = nc.dram_tensor("out_0_dram", (B, T, D), F32, kind="ExternalOutput").ap()
    build(nc, args, scratch(nc), out)
    r = _run(nc, [arrays], core_ids=[0])
    return r.results[0]["out_0_dram"]
```
